# Optimizing a Trainium2 kernel written in Bass

```python
import numpy as np
import jax
import jax.numpy as jnp

def _softmax(x, axis=-1):
    return jax.nn.softmax(x, axis=axis)

def _gelu(x):
    return jax.nn.gelu(x, approximate=True)

def _silu(x):
    return jax.nn.silu(x)

def _sigmoid(x):
    return jax.nn.sigmoid(x)

def _layernorm(x, axis=-1, eps=1e-05):
    m = jnp.mean(x, axis=axis, keepdims=True)
    v = jnp.var(x, axis=axis, keepdims=True)
    return (x - m) / jnp.sqrt(v + eps)

def _scatter_add(tgt, idx, src, axis=0):
    return tgt.at[idx].add(src)

def _segment_sum(src, seg, n):
    return jax.ops.segment_sum(src, seg, n)
kernel_name = 'mk_sandwich_d1_jaxref_r8_69c598'

def setup_inputs(seed: int=0):
    np.random.seed(seed)
    _w = jnp.asarray

    def _L0_attn_setup():
        import jax, jax.numpy as jnp
        import numpy as np
        import math
        N_EMBED = 256
        N_HEAD = 16
        D_KV = 128
        D_C = 64
        D_R = 64
        D_H = N_EMBED // N_HEAD
        B = 2
        S = 256

        def _rope_tables(seq_len, d_r):
            half = d_r // 2
            freqs = jnp.exp(jnp.arange(half, dtype=jnp.float32) * (-math.log(10000.0) / half))
            angles = jnp.arange(seq_len, dtype=jnp.float32)[:, None] * freqs[None, :]
            return (jnp.cos(angles), jnp.sin(angles))

        def _apply_rope(t, cos, sin):
            shp = t.shape
            pairs = t.reshape(shp[:-1] + (shp[-1] // 2, 2))
            x0, x1 = (pairs[..., 0], pairs[..., 1])
            r0 = x0 * cos - x1 * sin
            r1 = x0 * sin + x1 * cos
            return jnp.stack([r0, r1], axis=-1).reshape(shp)
        key = jax.random.key(seed)
        ks = jax.random.split(key, 10)
        sc = 0.02
        return {'x': jax.random.normal(ks[0], (B, S, N_EMBED), dtype=jnp.float32), 'W_dkv': jax.random.normal(ks[1], (N_EMBED, D_KV), dtype=jnp.float32) * sc, 'W_dq': jax.random.normal(ks[2], (N_EMBED, D_KV), dtype=jnp.float32) * sc, 'W_kr': jax.random.normal(ks[3], (N_EMBED, D_R), dtype=jnp.float32) * sc, 'W_qc': jax.random.normal(ks[4], (N_HEAD, D_KV, D_C), dtype=jnp.float32) * sc, 'W_qr': jax.random.normal(ks[5], (N_HEAD, D_KV, D_R), dtype=jnp.float32) * sc, 'W_uk': jax.random.normal(ks[6], (N_HEAD, D_KV, D_C), dtype=jnp.float32) * sc, 'W_uv': jax.random.normal(ks[7], (N_HEAD, D_KV, D_H), dtype=jnp.float32) * sc, 'W_o': jax.random.normal(ks[8], (N_HEAD * D_H, N_EMBED), dtype=jnp.float32) * sc}
    _L0_attn_in = _L0_attn_setup()

    def _L0_ffn_setup():
        import jax, jax.numpy as jnp
        import numpy as np
        BLOCK_SIZE = 32
        HIDDEN_SIZE = 256
        MLP_DIM = 2048
        NVFP4_LUT = jnp.array([0.0, 0.5, 1.0, 1.5, 2.0, 3.0, 4.0, 6.0, 0.0, -0.5, -1.0, -1.5, -2.0, -3.0, -4.0, -6.0], dtype=jnp.float32)

        def dequant_nvfp4(W_packed, scales, block=BLOCK_SIZE):
            N = W_packed.shape[0]
            low = W_packed & 15
            high = W_packed >> 4 & 15
            idx = jnp.stack([low, high], axis=-1).reshape(N, -1)
            vals = NVFP4_LUT[idx]
            K = vals.shape[1]
            vals = vals.reshape(N, K // block, block) * scales[:, :, None]
            return vals.reshape(N, K)
        key = jax.random.key(seed)
        ks = jax.random.split(key, 7)
        x = jax.random.normal(ks[0], (4, 32, HIDDEN_SIZE), dtype=jnp.float32)
        gate_W_packed = jax.random.randint(ks[1], (MLP_DIM, HIDDEN_SIZE // 2), 0, 32, dtype=jnp.int32)
        gate_scales = jax.random.uniform(ks[2], (MLP_DIM, HIDDEN_SIZE // BLOCK_SIZE), dtype=jnp.float32) * 0.1 + 0.001
        up_W_packed = jax.random.randint(ks[3], (MLP_DIM, HIDDEN_SIZE // 2), 0, 32, dtype=jnp.int32)
        up_scales = jax.random.uniform(ks[4], (MLP_DIM, HIDDEN_SIZE // BLOCK_SIZE), dtype=jnp.float32) * 0.1 + 0.001
        down_W_packed = jax.random.randint(ks[5], (HIDDEN_SIZE, MLP_DIM // 2), 0, 32, dtype=jnp.int32)
        down_scales = jax.random.uniform(ks[6], (HIDDEN_SIZE, MLP_DIM // BLOCK_SIZE), dtype=jnp.float32) * 0.1 + 0.001
        return {'x': x, 'gate_W_packed': gate_W_packed, 'gate_scales': gate_scales, 'up_W_packed': up_W_packed, 'up_scales': up_scales, 'down_W_packed': down_W_packed, 'down_scales': down_scales}
    _L0_ffn_in = _L0_ffn_setup()
    _d = {'L0_attn_x': _L0_attn_in['x'], 'L0_attn_W_dkv': _L0_attn_in['W_dkv'], 'L0_attn_W_dq': _L0_attn_in['W_dq'], 'L0_attn_W_kr': _L0_attn_in['W_kr'], 'L0_attn_W_qc': _L0_attn_in['W_qc'], 'L0_attn_W_qr': _L0_attn_in['W_qr'], 'L0_attn_W_uk': _L0_attn_in['W_uk'], 'L0_attn_W_uv': _L0_attn_in['W_uv'], 'L0_attn_W_o': _L0_attn_in['W_o'], 'L0_ffn_gate_W_packed': _L0_ffn_in['gate_W_packed'], 'L0_ffn_gate_scales': _L0_ffn_in['gate_scales'], 'L0_ffn_up_W_packed': _L0_ffn_in['up_W_packed'], 'L0_ffn_up_scales': _L0_ffn_in['up_scales'], 'L0_ffn_down_W_packed': _L0_ffn_in['down_W_packed'], 'L0_ffn_down_scales': _L0_ffn_in['down_scales']}
    _x0 = _d['L0_attn_x']
    _d['L0_attn_x'] = jax.random.normal(jax.random.fold_in(jax.random.key(seed), 1), (1, 1024, 256), dtype=_x0.dtype)
    del _x0
    return _d

def reference(L0_attn_x, L0_attn_W_dkv, L0_attn_W_dq, L0_attn_W_kr, L0_attn_W_qc, L0_attn_W_qr, L0_attn_W_uk, L0_attn_W_uv, L0_attn_W_o, L0_ffn_gate_W_packed, L0_ffn_gate_scales, L0_ffn_up_W_packed, L0_ffn_up_scales, L0_ffn_down_W_packed, L0_ffn_down_scales):

    def _L0_attn_ref(x, W_dkv, W_dq, W_kr, W_qc, W_qr, W_uk, W_uv, W_o):
        import jax, jax.numpy as jnp
        import numpy as np
        import math
        N_EMBED = 256
        N_HEAD = 16
        D_KV = 128
        D_C = 64
        D_R = 64
        D_H = N_EMBED // N_HEAD
        B = 2
        S = 256

        def _rope_tables(seq_len, d_r):
            half = d_r // 2
            freqs = jnp.exp(jnp.arange(half, dtype=jnp.float32) * (-math.log(10000.0) / half))
            angles = jnp.arange(seq_len, dtype=jnp.float32)[:, None] * freqs[None, :]
            return (jnp.cos(angles), jnp.sin(angles))

        def _apply_rope(t, cos, sin):
            shp = t.shape
            pairs = t.reshape(shp[:-1] + (shp[-1] // 2, 2))
            x0, x1 = (pairs[..., 0], pairs[..., 1])
            r0 = x0 * cos - x1 * sin
            r1 = x0 * sin + x1 * cos
            return jnp.stack([r0, r1], axis=-1).reshape(shp)
        Bx, Sx, E = x.shape
        H, _, d_c = W_qc.shape
        d_r = W_kr.shape[1]
        d_h = W_uv.shape[2]
        cos, sin = _rope_tables(Sx, d_r)
        c_kv = x @ W_dkv
        x_dq = x @ W_dq
        k_rope = _apply_rope(x @ W_kr, cos, sin)
        q_nope = jnp.einsum('bsk,hkc->bhsc', x_dq, W_qc)
        q_rope = _apply_rope(jnp.einsum('bsk,hkr->bhsr', x_dq, W_qr), cos, sin)
        k_nope = jnp.einsum('bsk,hkc->bhsc', c_kv, W_uk)
        v = jnp.einsum('bsk,hkd->bhsd', c_kv, W_uv)
        score = jnp.einsum('bhsc,bhtc->bhst', q_nope, k_nope) + jnp.einsum('bhsr,btr->bhst', q_rope, k_rope)
        causal = jnp.tril(jnp.ones((Sx, Sx), dtype=bool))
        score = jnp.where(causal, score, -jnp.inf)
        attn = jax.nn.softmax(score / math.sqrt(d_h), axis=-1)
        out = jnp.einsum('bhst,bhtd->bhsd', attn, v)
        out = out.transpose(0, 2, 1, 3).reshape(Bx, Sx, H * d_h)
        return out @ W_o

    def _L0_ffn_ref(x, gate_W_packed, gate_scales, up_W_packed, up_scales, down_W_packed, down_scales):
        import jax, jax.numpy as jnp
        import numpy as np
        BLOCK_SIZE = 32
        HIDDEN_SIZE = 256
        MLP_DIM = 2048
        NVFP4_LUT = jnp.array([0.0, 0.5, 1.0, 1.5, 2.0, 3.0, 4.0, 6.0, 0.0, -0.5, -1.0, -1.5, -2.0, -3.0, -4.0, -6.0], dtype=jnp.float32)

        def dequant_nvfp4(W_packed, scales, block=BLOCK_SIZE):
            N = W_packed.shape[0]
            low = W_packed & 15
            high = W_packed >> 4 & 15
            idx = jnp.stack([low, high], axis=-1).reshape(N, -1)
            vals = NVFP4_LUT[idx]
            K = vals.shape[1]
            vals = vals.reshape(N, K // block, block) * scales[:, :, None]
            return vals.reshape(N, K)
        B, S, H = x.shape
        xt = x.reshape(B * S, H)
        Wg = dequant_nvfp4(gate_W_packed, gate_scales)
        Wu = dequant_nvfp4(up_W_packed, up_scales)
        Wd = dequant_nvfp4(down_W_packed, down_scales)
        gate = jnp.einsum('th,nh->tn', xt, Wg)
        up = jnp.einsum('th,nh->tn', xt, Wu)
        gelu = jnp.tanh(0.7978845608028654 * (gate + 0.044715 * gate ** 3)) * gate * 0.5 + gate * 0.5
        inter = gelu * up
        out = jnp.einsum('tn,hn->th', inter, Wd)
        return out.reshape(B, S, H)
    x = L0_attn_x
    x = x + _layernorm(_L0_attn_ref(_layernorm(x, axis=-1), L0_attn_W_dkv, L0_attn_W_dq, L0_attn_W_kr, L0_attn_W_qc, L0_attn_W_qr, L0_attn_W_uk, L0_attn_W_uv, L0_attn_W_o), axis=-1)
    x = x + _layernorm(_L0_ffn_ref(_layernorm(x, axis=-1), L0_ffn_gate_W_packed, L0_ffn_gate_scales, L0_ffn_up_W_packed, L0_ffn_up_scales, L0_ffn_down_W_packed, L0_ffn_down_scales), axis=-1)
    return x

_drawn_inputs = setup_inputs


def setup_inputs(seed=0):
    import zlib

    import numpy as np

    out = dict(_drawn_inputs(seed))
    spreads = {}
    factors = {'L0_attn_W_qc': 5.376, 'L0_attn_W_uk': 5.459}
    for name, (base, spread) in spreads.items():
        noise = np.random.default_rng([zlib.crc32(name.encode()), seed]).standard_normal(out[name].shape)
        drawn = base * np.exp(spread * noise) if base else spread * noise
        out[name] = jnp.asarray(drawn.astype(out[name].dtype))
    for name, factor in factors.items():
        out[name] = (out[name] * factor).astype(out[name].dtype)
    return out
```

```python
import math
from contextlib import ExitStack

import numpy as np

import concourse.bass as bass
from concourse import mybir

F32 = mybir.dt.float32
F16 = mybir.dt.float16
BF16 = mybir.dt.bfloat16
I32 = mybir.dt.int32
ALU = mybir.AluOpType
ACT = mybir.ActivationFunctionType
AX = mybir.AxisListType
RMAX = bass.bass_isa.ReduceOp.max

T, E = 1024, 256
H, DKV, DC, DR, DH = 16, 128, 64, 64, 16
F = 2048
QB = 32
NB = T // 128
NT = F // 128
HG = 4
G = H // HG
U = NB * HG
EPS = 1e-5
GC = 0.7978845608028654
G3 = 0.044715
XS = 2.0 ** 11
WS = 2.0 ** 14
FS = 2.0 ** 11
CODE = 2.0 ** 14
IS = 2.0 ** -6
MASK = -1e38


def layer_kernel(nc, x, w_dkv, w_dq, w_kr, w_qc, w_qr, w_uk, w_uv, w_o, gate_w, gate_s, up_w, up_s,
                 down_w, down_s, rope_cos, rope_sin, out):
    with ExitStack() as ctx:
        def sb(name, shape, dt=F32):
            return ctx.enter_context(nc.sbuf_tensor(name, shape, dt))

        def sem(name):
            return ctx.enter_context(nc.semaphore(name))

        X = sb("X", [128, NB, E])
        XD = sb("XD", [128, 2, T], F16)
        CK = sb("CK", [128, 2, T], F16)
        WP = sb("WP", [128, 8192], F16)
        CA = sb("CA", [128, T])
        CB = sb("CB", [128, T])
        SS = sb("SS", [128, T])
        V = sb("V", [128, NB, H, DH + 1])
        QH = sb("QH", [128, 2, HG, T], F16)
        QL = sb("QL", [128, 2, HG, T], F16)
        KH = sb("KH", [128, 2, HG, T], F16)
        KL = sb("KL", [128, 2, HG, T], F16)
        PR = sb("PR", [128, 4, 512])
        PT = sb("PT", [128, 2, HG, NB, 128])
        OT = sb("OT", [128, G, T])
        STG = sb("STG", [128, 2, 3, 512])
        WO = sb("WO", [128, 2, E])
        RAW = sb("RAW", [128, 2, 512], I32)
        BITS = sb("BITS", [128, 512], I32)
        DQ = sb("DQ", [128, 2, 1024])
        ident = sb("ident", [128, 128])
        identb = sb("identb", [128, 128], BF16)
        maskb = sb("maskb", [128, 128], BF16)
        ones = sb("ones", [128, 128])
        st6 = sb("st6", [128, NB, 6])
        mv = sb("mv", [128, NB, 2])
        rs = sb("rs", [128, NB])
        powc = sb("powc", [128, 2, 8])
        nrm = sb("nrm", [128, 32])
        mx = sb("mx", [128, 8])
        nb = sb("nb", [128, 8])
        SG = sb("SG", [128, 3, NT * 8])
        SM = sb("SM", [128, 8, NT])
        gx = sb("gx", [128, 16])
        rc = sb("rc", [128, 2, H])
        PS = ctx.enter_context(nc.psum_tensor("PS", [128, 8, 512], F32))

        pt = PT[:, :, :, :, :].rearrange("p a h b c -> p (a h b c)")
        xT = pt[:, 0:2048].rearrange("p (k t) -> p k t", k=2)
        CKV = pt[:, 2048:3072]
        r_qc = pt[:, 3072:4096].rearrange("p (h c) -> p h c", h=H)
        r_qr = pt[:, 4096:5120].rearrange("p (h c) -> p h c", h=H)
        r_uk = pt[:, 5120:6144].rearrange("p (h c) -> p h c", h=H)
        CF = pt[:, 6144:7168]
        w_dq_s = pt[:, 7168:7424].rearrange("p (k m) -> p k m", k=2)
        w_dkv_s = pt[:, 7424:7680].rearrange("p (k m) -> p k m", k=2)
        r_kr = pt[:, 7680:7808].rearrange("p (k m) -> p k m", k=2)
        ot = OT[:, :, :].rearrange("p g t -> p (g t)")
        WQ32 = ot[:, 0:2048].rearrange("p (h c) -> p h c", h=H)
        WUK32 = ot[:, 2048:3072].rearrange("p (q c) -> p q c", q=H // 2)
        w_uv_s = ot[:, 3072:3328].rearrange("p (h c) -> p h c", h=H)
        KR2 = ot[:, 3328:3584].rearrange("p (k m) -> p k m", k=2)
        KR2S = ot[:, 3584:3840].rearrange("p (k m) -> p k m", k=2)
        XN = PR[:, :, :].rearrange("p a (b c) -> p (a b) c", c=E)
        pr = PR[:, :, :].rearrange("p a c -> p (a c)")
        junk = STG[:, :, :, :].rearrange("p a b c -> p (a b c)")
        WQ = WP[:, 0:4096].rearrange("p (s h c) -> p s h c", s=2, h=H)
        WSW = WP[:, 4096:6144].rearrange("p (s q c) -> p s q c", s=2, q=H // 2)
        WUK = WP[:, 6144:8192].rearrange("p (s q c) -> p s q c", s=2, q=H // 2)
        WG = [q[:, 0, :, :].rearrange("p h t -> p (h t)").rearrange("p (k n) -> p k n", k=2)
              for q in (QH, QL)]
        WU = [q[:, 0, :, :].rearrange("p h t -> p (h t)").rearrange("p (k n) -> p k n", k=2)
              for q in (KH, KL)]
        WD = [WP[:, 4096 * s:4096 * (s + 1)].rearrange("p (n h) -> p n h", n=NT) for s in range(2)]
        X2 = pt[:, 0:2048].bitcast(F16).rearrange("p (s k t) -> p s k t", s=2, k=2)
        sq = pt[:, 2048:3072].rearrange("p (a t) -> p a t", a=2)
        inn = pt[:, 3072:4096].rearrange("p (a t) -> p a t", a=2)
        hg = pt[:, 4096:5120].rearrange("p (a t) -> p a t", a=2)
        itr = pt[:, 5120:6144].rearrange("p (a t) -> p a t", a=2)
        IH = pt[:, 6144:7680].bitcast(F16).rearrange("p (a s t) -> p a s t", a=3, s=2)
        AN = pr[:, 0:1024].rearrange("p (a c) -> p a c", a=4)
        YB = pr[:, 1024:2048].rearrange("p (a c) -> p a c", a=4)
        AT = STG[:, 0, :, :].rearrange("p a c -> p (a c)")[:, 0:1024].rearrange(
            "p (a k t) -> p a k t", a=4, k=2)
        XN2 = STG[:, 1, :, :].rearrange("p a c -> p (a c)")[:, 0:1024].rearrange(
            "p (a c) -> p a c", a=4)
        NF, NR = nrm[:, 0:6], nrm[:, 8:14]
        DEN, rD, ESC, NESC, CEPS = (nrm[:, i:i + 1] for i in (16, 17, 18, 19, 20))
        f_dq, f_dkv, f_kr, f_q, f_uk, f_uv = (nrm[:, i:i + 1] for i in range(21, 27))
        tmp1, tmp2, tmp3 = (nrm[:, i:i + 1] for i in (27, 28, 29))
        GM, UM, GI, UI, K3, KT, KI = (SM[:, i, :] for i in range(7))

        ld_x, ld_w, ld_h, ld_rope, ld_wo, ld_s = (sem(s) for s in (
            "ld_x", "ld_w", "ld_h", "ld_rope", "ld_wo", "ld_s"))
        ld_raw = [sem("ld_raw0"), sem("ld_raw1")]
        s_const = sem("s_const")
        s_sq = sem("s_sq")
        s_nsum = sem("s_nsum")
        s_v = sem("s_v")
        s_pow = sem("s_pow")
        s_st = sem("s_st")
        s_xn = sem("s_xn")
        s_xtp = sem("s_xtp")
        s_xt = sem("s_xt")
        s_wf = sem("s_wf")
        s_whi = sem("s_whi")
        s_wlo = sem("s_wlo")
        s_wsw = sem("s_wsw")
        s_pj = sem("s_pj")
        s_phi = sem("s_phi")
        s_plo = sem("s_plo")
        s_vp = sem("s_vp")
        s_vs = sem("s_vs")
        s_sc = sem("s_sc")
        s_nb = sem("s_nb")
        s_mx = sem("s_mx")
        s_ex = sem("s_ex")
        s_tp = sem("s_tp")
        s_te = sem("s_te")
        s_pv = sem("s_pv")
        s_ov = sem("s_ov")
        s_aux = sem("s_aux")
        s_afr = sem("s_afr")
        s_ahi = sem("s_ahi")
        s_rot = sem("s_rot")
        s_qhi = sem("s_qhi")
        s_qlo = sem("s_qlo")
        s_bits = sem("s_bits")
        s_deq = sem("s_deq")
        s_sm = sem("s_sm")
        s_gm = sem("s_gm")
        s_sf = sem("s_sf")
        t_a, t_b, t_c, t_d = (sem(s) for s in ("t_a", "t_b", "t_c", "t_d"))
        t_n = sem("t_n")
        t_e = sem("t_e")
        t_st = sem("t_st")
        t_pw = sem("t_pw")
        t_y = sem("t_y")
        t_x = sem("t_x")
        t_xn = sem("t_xn")
        t_hi = sem("t_hi")
        t_lo = sem("t_lo")
        m_g, m_u, m_d = sem("m_g"), sem("m_u"), sem("m_d")
        m_sq, m_in, m_th, m_h, m_it, m_hi, m_lo = (sem(s) for s in (
            "m_sq", "m_in", "m_th", "m_h", "m_it", "m_hi", "m_lo"))
        s_out = sem("s_out")

        ps = PS[:, :, :].rearrange("p b c -> p (b c)")

        def bank(b, w=512):
            return PS[:, b, 0:w]

        def width(sb_):
            return (sb_ + 1) * 128

        def nbanks(i):
            return i // HG // 4 + 1

        def banks_before(n):
            g, i = divmod(n, U)
            return g * sum(nbanks(k) for k in range(U)) + sum(nbanks(k) for k in range(i))

        SMALL = U // 2

        def after(i):
            if i < HG:
                return -2 + i // 2
            if i < SMALL:
                return i - HG
            return {SMALL: SMALL - 3, SMALL + 1: SMALL - 1}.get(i, i - 2)

        def slot(base, n):
            i = n % U
            w, a = width(i // HG), (i % HG if i < SMALL else 2 * (i % 2))
            return base[:, 512 * a:512 * a + w]

        LEAD = {i: [m for m in range(U + HG) if (after(m % U) + (m // U) * U) == i]
                for i in range(-2, U)}
        SOON = {i: [m for m in range(U + HG)
                    if max(after(m % U) + (m // U) * U, m - 2) == i] for i in range(-2, U)}

        QJOBS = [(pr, hf, kind) for pr in range(HG // 2) for hf in range(2) for kind in "SABK"]
        CHUNKS = [(m, c) for m in range(2) for c in range(4)] + [(2, c) for c in range(4)]
        WJOBS = [(m, c, k) for m, c in CHUNKS for k in range(2)]
        job_at = [j * 3 // 2 for j in range(16)]
        wjob_at = [4 + j for j in range(24)]

        def aux_index(g, j):
            return 16 * g + j

        block = ctx.enter_context(nc.Block())

        @block.sync
        def _(sp):
            sp.dma_start(X[:, :, :], x.rearrange("o (b p) e -> p (o b) e", p=128)).then_inc(ld_x, 16)
            sp.dma_start(w_dq_s, w_dq.rearrange("(k p) m -> p k m", p=128)).then_inc(ld_w, 16)
            sp.dma_start(w_dkv_s, w_dkv.rearrange("(k p) m -> p k m", p=128)).then_inc(ld_w, 16)
            sp.dma_start(r_kr, w_kr.rearrange("(k p) m -> p k m", p=128)).then_inc(ld_w, 16)
            sp.dma_start(r_qc, w_qc.rearrange("h p c -> p h c")).then_inc(ld_w, 16)
            sp.dma_start(r_qr, w_qr.rearrange("h p c -> p h c")).then_inc(ld_w, 16)
            sp.dma_start(r_uk, w_uk.rearrange("h p c -> p h c")).then_inc(ld_w, 16)
            sp.dma_start(w_uv_s, w_uv.rearrange("h p c -> p h c")).then_inc(ld_w, 16)
            sp.dma_start(CF, rope_cos[:, :]).then_inc(ld_rope, 16)
            sp.dma_start(SS[:, :], rope_sin[:, :]).then_inc(ld_rope, 16)
            sp.dma_start(CA[0:64, :], rope_cos[0:64, :]).then_inc(ld_rope, 16)
            sp.dma_start(CB[64:128, :], rope_cos[64:128, :]).then_inc(ld_rope, 16)
            sp.dma_start(WO[:, :, :], w_o.rearrange("(k p) e -> p k e", p=128)).then_inc(ld_wo, 16)
            for i, s in enumerate((gate_s, up_s)):
                sp.dma_start(SG[:, i, :].rearrange("p (n b) -> p n b", b=8),
                             s.rearrange("(n p) b -> p n b", p=128)).then_inc(ld_s, 16)
            sp.dma_start(SG[:, 2, :].rearrange("p (h b) -> p h b", h=2),
                         down_s.rearrange("(h p) b -> p h b", p=128)).then_inc(ld_s, 16)
            gw = gate_w.rearrange("(n p) w -> p n w", p=128)
            uw = up_w.rearrange("(n p) w -> p n w", p=128)
            dw = down_w.rearrange("(h p) w -> p h w", p=128)
            for q, (m, c) in enumerate(CHUNKS):
                if q >= 2:
                    sp.wait_ge(s_bits, q - 1)
                if m < 2:
                    sp.dma_start(RAW[:, q % 2, :].rearrange("p (n w) -> p n w", n=4),
                                 (gw, uw)[m][:, 4 * c:4 * c + 4, :]).then_inc(ld_raw[q % 2], 16)
                else:
                    sp.dma_start(RAW[:, q % 2, :], dw[:, c // 2, 512 * (c % 2):512 * (c % 2 + 1)]
                                 ).then_inc(ld_raw[q % 2], 16)
            for b in range(NB):
                sp.wait_ge(t_x, NB + b + 1)
                sp.dma_start(out.rearrange("o (b p) e -> p (o b) e", p=128)[:, b, :],
                             X[:, b, :]).then_inc(s_out, 16)
            sp.wait_ge(s_out, 16 * NB)

        @block.gpsimd
        def _(pool):
            nc.gpsimd.memset(ones[:, :], 1.0).then_inc(s_const, 1)
            nc.gpsimd.memset(powc[:, 0, :], -0.5).then_inc(s_const, 1)
            nc.gpsimd.memset(powc[:, 1, :], 0.5).then_inc(s_const, 1)
            nc.gpsimd.memset(ident[:, :], 0.0).then_inc(s_const, 1)
            nc.gpsimd.memset(identb[:, :], 0.0).then_inc(s_const, 1)
            nc.gpsimd.memset(maskb[:, :], 0.0).then_inc(s_const, 1)
            pool.wait_ge(s_const, 6)
            nc.gpsimd.affine_select(out=ident[:, :], in_=ident[:, :], compare_op=ALU.not_equal,
                                    fill=1.0, base=0, pattern=[[-1, 128]],
                                    channel_multiplier=1).then_inc(s_const, 1)
            nc.gpsimd.affine_select(out=identb[:, :], in_=identb[:, :], compare_op=ALU.not_equal,
                                    fill=1.0, base=0, pattern=[[-1, 128]],
                                    channel_multiplier=1).then_inc(s_const, 1)
            nc.gpsimd.affine_select(out=maskb[:, :], in_=maskb[:, :], compare_op=ALU.is_ge,
                                    fill=MASK, base=0, pattern=[[-1, 128]],
                                    channel_multiplier=1).then_inc(s_const, 1)
            pool.wait_ge(s_st, 1)
            nc.gpsimd.tensor_tensor(rs[:, :], rs[:, :], powc[:, 0, :], ALU.pow).then_inc(s_pow, 1)
            pool.wait_ge(s_st, 2)
            nc.gpsimd.tensor_tensor(NR, NF, powc[:, 1, 0:6], ALU.pow).then_inc(s_pow, 1)
            pool.wait_ge(s_pow, 2)
            nc.gpsimd.memset(CA[64:128, :], 1.0 / WS).then_inc(s_const, 1)
            pool.wait_ge(s_const, 10)
            nc.gpsimd.memset(CB[0:64, :], 1.0 / WS).then_inc(s_const, 1)
            pool.wait_ge(s_const, 11)
            nc.gpsimd.memset(V[:, :, :, DH:DH + 1], 1.0).then_inc(s_const, 1)
            for s in range(2):
                if s == 0:
                    pool.wait_ge(s_whi, 1)
                else:
                    pool.wait_ge(s_wlo, 1)
                wq = WQ[:, s, :, :].rearrange("p (q e) c -> p q e c", e=2)
                for e in range(2):
                    o = 64 * e
                    for a in range(2):
                        nc.gpsimd.tensor_copy(
                            WSW[:, s, :, o + 32 * a:o + 32 * a + 32],
                            wq[:, :, e, o + 32 * (1 - a):o + 32 * (1 - a) + 32]).then_inc(s_wsw, 1)

            def rotate(g, m):
                n = 4 * g + m
                pr, hf = m // 2, m % 2
                pool.wait_ge(s_afr, 4 * n + 3)
                w, a, b = (STG[:, n % 2, k, :] for k in range(3))
                if n == 0:
                    pool.wait_ge(s_wsw, 8)
                else:
                    pool.wait_ge(s_qlo, 2 * n)
                nc.gpsimd.tensor_tensor(a[0:64, :], a[0:64, :], w[0:64, :], ALU.add)\
                    .then_inc(s_rot, 1)
                pool.wait_ge(s_rot, 2 * n + 1)
                nc.gpsimd.tensor_tensor(b[64:128, :], b[64:128, :], w[64:128, :], ALU.add)\
                    .then_inc(s_rot, 1)
                pool.wait_ge(s_qhi, 2 * (n + 1))
                for e in range(2):
                    dst = QL[:, g % 2, 2 * pr + e, 512 * hf:512 * hf + 512]
                    if e == 0 and g >= 2 and m == 0:
                        pool.wait_ge(s_sc, U * (g - 1))
                    nc.gpsimd.tensor_tensor(dst, STG[:, n % 2, 1 + e, :],
                                            QH[:, g % 2, 2 * pr + e, 512 * hf:512 * hf + 512],
                                            ALU.subtract).then_inc(s_qlo, 1)

            def dequant(q):
                m, c = CHUNKS[q]
                pool.wait_ge(s_bits, q + 1)
                if q == 0:
                    pool.wait_ge(s_sf, 1)
                if q >= 2:
                    pool.wait_ge(s_aux, 16 * G + 2 * (q - 1))
                codes = BITS[:, :].bitcast(F16).rearrange("p (b k) -> p b k", k=QB)
                if m < 2:
                    sc = SG[:, m, 32 * c:32 * c + 32]
                else:
                    sc = SG[:, 2, 64 * (c // 2) + 32 * (c % 2):64 * (c // 2) + 32 * (c % 2) + 32]
                nc.gpsimd.tensor_tensor(DQ[:, q % 2, :].rearrange("p (b k) -> p b k", k=QB), codes,
                                        sc.unsqueeze(2).broadcast_to([128, 32, QB]),
                                        ALU.mult).then_inc(s_deq, 1)

            for m in range(4):
                rotate(0, m)
            pool.wait_ge(s_sm, 1)
            nc.gpsimd.partition_all_reduce(gx[:, 4:7], gx[:, 0:3], 128, RMAX).then_inc(s_gm, 1)
            for g in range(1, G):
                for m in range(4):
                    rotate(g, m)
            for q in range(12):
                dequant(q)
            for s in range(NB + 3):
                if 0 <= s - 2 < NB:
                    b = s - 2
                    pool.wait_ge(t_st, 2 * b + 1)
                    nc.gpsimd.tensor_tensor(rs[:, b:b + 1], rs[:, b:b + 1], powc[:, 0, 0:1],
                                            ALU.pow).then_inc(t_pw, 1)
                    pool.wait_ge(t_y, b + 1)
                    nc.gpsimd.tensor_tensor(X[:, b, :], X[:, b, :], YB[:, b % 4, :], ALU.add)\
                        .then_inc(t_x, 1)
                    pool.wait_ge(t_st, 2 * b + 2)
                    nc.gpsimd.tensor_tensor(rs[:, b:b + 1], rs[:, b:b + 1], powc[:, 0, 0:1],
                                            ALU.pow).then_inc(t_pw, 1)
            for k in range(2 * NT):
                pool.wait_ge(m_hi, k + 1)
                if k >= 3:
                    pool.wait_ge(m_d, k - 2)
                nc.gpsimd.tensor_tensor(IH[:, k % 3, 1, :], itr[:, k % 2, :], IH[:, k % 3, 0, :],
                                        ALU.subtract).then_inc(m_lo, 1)
            for b in range(NB):
                pool.wait_ge(t_st, 2 * NB + b + 1)
                nc.gpsimd.tensor_tensor(rs[:, b:b + 1], rs[:, b:b + 1], powc[:, 0, 0:1], ALU.pow)\
                    .then_inc(t_pw, 1)
                pool.wait_ge(t_y, NB + b + 1)
                nc.gpsimd.tensor_tensor(X[:, b, :], X[:, b, :], YB[:, b % 4, :], ALU.add)\
                    .then_inc(t_x, 1)

        @block.scalar
        def _(act):
            act.wait_ge(ld_w, 112)
            for i, w in enumerate((w_dq_s, w_dkv_s, r_kr, r_qc, r_qr, r_uk)):
                n = w.shape[1] * w.shape[2]
                nc.scalar.activation(junk[:, 0:n].rearrange("p (a b) -> p a b", a=w.shape[1]), w,
                                     ACT.Square, accum_out=nrm[:, i:i + 1]).then_inc(s_sq, 1)
                act.wait_ge(s_sq, i + 1)
            for b in range(4):
                act.wait_ge(s_xtp, b + 1)
                hf, k = divmod(b, 2)
                nc.scalar.activation(xT[:, k, 512 * hf:512 * hf + 512], bank(b), ACT.Copy)\
                    .then_inc(s_xt, 1)
            act.wait_ge(s_wf, 2)
            nc.scalar.activation(WQ[:, 0, :, :], WQ32, ACT.Copy).then_inc(s_whi, 1)
            act.wait_ge(s_wf, 3)
            nc.scalar.activation(WUK[:, 0, :, :], WUK32, ACT.Copy).then_inc(s_whi, 1)
            for j in range(4):
                act.wait_ge(s_pj, j + 1)
                hf = j % 2
                dst = (XD, CK)[j // 2][:, 0, 512 * hf:512 * hf + 512]
                if j < 2:
                    nc.scalar.activation(dst, bank(4 + j), ACT.Copy).then_inc(s_phi, 1)
                else:
                    nc.scalar.activation(CKV[:, 512 * hf:512 * hf + 512], bank(4 + j), ACT.Copy)\
                        .then_inc(s_phi, 1)
                    nc.scalar.activation(dst, bank(4 + j), ACT.Copy).then_inc(s_phi, 1)

            def khi(g, j):
                pr, hf, _ = QJOBS[j]
                act.wait_ge(s_aux, aux_index(g, j) + 1)
                if g >= 2 and j == 3:
                    act.wait_ge(s_sc, U * (g - 1))
                for e, r in ((1, 0), (0, 64)):
                    nc.scalar.activation(KH[r:r + 64, g % 2, 2 * pr + e, 512 * hf:512 * hf + 512],
                                         PS[r:r + 64, 7, :], ACT.Copy, scale=1.0 / WS)\
                        .then_inc(s_ahi, 1)

            def whi(j):
                m, c, k = WJOBS[j]
                act.wait_ge(s_aux, 16 * G + j + 1)
                if j == 0:
                    act.wait_ge(s_sc, U * (G - 1))
                if m < 2:
                    nc.scalar.activation((WG, WU)[m][0][:, k, 512 * c:512 * c + 512], bank(7),
                                         ACT.Copy).then_inc(s_ahi, 1)
                else:
                    h, n0 = c // 2, 8 * (c % 2) + 4 * k
                    nc.scalar.activation(WD[0][:, n0:n0 + 4, 128 * h:128 * h + 128],
                                         bank(7).rearrange("p (n c) -> p n c", n=4), ACT.Copy)\
                        .then_inc(s_ahi, 1)

            def exps(n):
                i = n % U
                w = width(i // HG)
                act.wait_ge(s_nb, n + 1)
                last = n - i + after(i)
                if last >= 0:
                    act.wait_ge(s_tp, banks_before(last + 1))
                nc.scalar.activation(slot(pr, n), slot(ps, n), ACT.Exp,
                                     bias=nb[:, n % 8:n % 8 + 1], scale=ESC).then_inc(s_ex, 1)

            def evac(n):
                g, i = divmod(n, U)
                sb_, h = divmod(i, HG)
                u = g * NB + sb_
                if h == 0 and u >= 2:
                    act.wait_ge(s_pv, u - 1)
                for q in range(nbanks(i)):
                    act.wait_ge(s_tp, banks_before(n) + q + 1)
                    k = min(4, sb_ + 1 - 4 * q)
                    nc.scalar.activation(PT[:, u % 2, h, 4 * q:4 * q + k, :],
                                         bank(4 + (banks_before(n) + q) % 2, 128 * k)
                                         .rearrange("p (b c) -> p b c", c=128), ACT.Copy)\
                        .then_inc(s_te, 1)

            for j in (3, 7, 11, 15):
                khi(0, j)
            for m in SOON[-2] + SOON[-1]:
                exps(m)
            for g in range(G):
                for i in range(U):
                    n = g * U + i
                    evac(n)
                    if g < G - 1 and i in job_at and QJOBS[job_at.index(i)][2] == "K":
                        khi(g + 1, job_at.index(i))
                    if g == G - 1 and i in wjob_at:
                        whi(wjob_at.index(i))
                    for m in SOON[i]:
                        if g * U + m < G * U:
                            exps(g * U + m)
            for s in range(NB + 5):
                if 0 <= s - 1 < NB:
                    b = s - 1
                    act.wait_ge(t_b, b + 1)
                    nc.scalar.activation(AT[:, b % 4, :, :],
                                         bank(2 + b % 2, 256).rearrange("p (k t) -> p k t", k=2),
                                         ACT.Copy).then_inc(t_e, 1)
                if 0 <= s - 4 < NB:
                    b = s - 4
                    act.wait_ge(t_d, b + 1)
                    nc.scalar.activation(X2[:, 0, :, 128 * b:128 * b + 128],
                                         bank(6 + b % 2, 256).rearrange("p (k t) -> p k t", k=2),
                                         ACT.Copy).then_inc(t_hi, 1)
            def square(k):
                n = k % NT
                act.wait_ge(m_g, k + 1)
                if k >= 2:
                    act.wait_ge(m_in, k - 1)
                nc.scalar.activation(sq[:, k % 2, :], bank(k % 2), ACT.Square,
                                     scale=K3[:, n:n + 1]).then_inc(m_sq, 1)

            square(0)
            for k in range(2 * NT):
                n = k % NT
                act.wait_ge(m_in, k + 1)
                nc.scalar.activation(inn[:, k % 2, :], inn[:, k % 2, :], ACT.Tanh,
                                     scale=KT[:, n:n + 1]).then_inc(m_th, 1)
                if k + 1 < 2 * NT:
                    square(k + 1)
                act.wait_ge(m_it, k + 1)
                if k >= 3:
                    act.wait_ge(m_d, k - 2)
                nc.scalar.activation(IH[:, k % 3, 0, :], itr[:, k % 2, :], ACT.Copy)\
                    .then_inc(m_hi, 1)

        @block.tensor
        def _(pe):
            def split_mm(out_, lhs, rhs, start=True, stop=True, check=True):
                nc.tensor.matmul(out_, lhs[0], rhs[0], start=start, stop=False,
                                 skip_group_check=not check)
                nc.tensor.matmul(out_, lhs[0], rhs[1], start=False, stop=False,
                                 skip_group_check=not check)
                return nc.tensor.matmul(out_, lhs[1], rhs[0], start=False, stop=stop,
                                        skip_group_check=not check)

            pe.wait_ge(s_const, 9)
            for hf in range(2):
                pe.wait_ge(s_xn, 4 * hf + 4)
                for k in range(2):
                    for b in range(4):
                        mm = nc.tensor.transpose(PS[:, 2 * hf + k, 128 * b:128 * b + 128],
                                                 XN[:, 4 * hf + b, 128 * k:128 * k + 128],
                                                 ident[:, :])
                    mm.then_inc(s_xtp, 1)
            pe.wait_ge(s_sq, 6)
            nc.tensor.matmul(bank(7, 6), ones[:, :], NF, start=True, stop=True).then_inc(s_nsum, 1)
            pe.wait_ge(s_xt, 4)
            pe.wait_ge(s_wf, 1)
            setups = [(w_dq_s, 0), (w_dq_s, 1), (w_dkv_s, 0), (w_dkv_s, 1),
                      (KR2, 0), (KR2S, 0), (KR2, 1), (KR2S, 1)]
            for j, (w, hf) in enumerate(setups):
                for k in range(2):
                    mm = nc.tensor.matmul(bank((4 + j) % 8), w[:, k, :],
                                          xT[:, k, 512 * hf:512 * hf + 512],
                                          start=(k == 0), stop=(k == 1))
                mm.then_inc(s_pj, 1)
            pe.wait_ge(s_phi, 6)
            for v in range(4):
                if v < 2:
                    pe.wait_ge(s_plo, v + 1)
                else:
                    pe.wait_ge(s_plo, 4)
                for a in range(2):
                    b = 2 * v + a
                    mm = nc.tensor.matmul(PS[:, 4 + v, 256 * a:256 * a + 256],
                                          CKV[:, 128 * b:128 * b + 128],
                                          w_uv_s.rearrange("p h c -> p (h c)"),
                                          start=True, stop=True)
                mm.then_inc(s_vp, 1)

            def qjob(g, j):
                pr, hf, kind = QJOBS[j]
                n = aux_index(g, j)
                if n >= 1:
                    pe.wait_ge(s_afr, n)
                q, cols = 2 * g + pr, slice(512 * hf, 512 * hf + 512)
                xd = (XD[:, 0, cols], XD[:, 1, cols])
                if kind == "S":
                    mm = split_mm(bank(7), (WSW[:, 0, q, :], WSW[:, 1, q, :]), xd)
                elif kind == "K":
                    mm = split_mm(bank(7), (WUK[:, 0, q, :], WUK[:, 1, q, :]),
                                  (CK[:, 0, cols], CK[:, 1, cols]))
                else:
                    h = 2 * q + (kind == "B")
                    mm = split_mm(bank(7), (WQ[:, 0, h, :], WQ[:, 1, h, :]), xd)
                mm.then_inc(s_aux, 1)

            def wjob(j):
                m, c, k = WJOBS[j]
                q = j // 2
                pe.wait_ge(s_afr, 16 * G + j)
                pe.wait_ge(s_deq, q + 1)
                for a in range(4):
                    if m < 2:
                        src = DQ[:, q % 2, 256 * a + 128 * k:256 * a + 128 * k + 128]
                    else:
                        src = DQ[:, q % 2, 128 * (4 * k + a):128 * (4 * k + a) + 128]
                    mm = nc.tensor.transpose(PS[:, 7, 128 * a:128 * a + 128], src, ident[:, :])
                mm.then_inc(s_aux, 1)

            def scores(n):
                g, i = divmod(n, U)
                sb_, h = divmod(i, HG)
                w = width(sb_)
                last = n - i + after(i)
                if last >= 0:
                    pe.wait_ge(s_ex, last + 1)
                if i == 0:
                    pe.wait_ge(s_qhi, 8 * (g + 1))
                    pe.wait_ge(s_qlo, 8 * (g + 1))
                    pe.wait_ge(s_afr, 16 * (g + 1))
                qs = [q[:, g % 2, h, 128 * sb_:128 * sb_ + 128] for q in (QH, QL)]
                for c in range((w + 511) // 512):
                    last = 512 * (c + 1) >= w
                    ks = [k[:, g % 2, h, 512 * c:min(w, 512 * c + 512)] for k in (KH, KL)]
                    o = slot(ps, n)[:, 512 * c:min(w, 512 * c + 512)]
                    mm = split_mm(o, qs, ks, stop=not last)
                    if last:
                        mm = nc.tensor.matmul(o[:, o.shape[1] - 128:o.shape[1]], identb[:, :],
                                              maskb[:, :], start=False, stop=True)
                mm.then_inc(s_sc, 1)

            def transp(n):
                g, i = divmod(n, U)
                sb_ = i // HG
                pe.wait_ge(s_ex, n + 1)
                for q in range(nbanks(i)):
                    k = banks_before(n) + q
                    if k >= 2:
                        pe.wait_ge(s_te, k - 1)
                    for a in range(min(4, sb_ + 1 - 4 * q)):
                        b = 4 * q + a
                        mm = nc.tensor.transpose(PS[:, 4 + k % 2, 128 * a:128 * a + 128],
                                                 slot(pr, n)[:, 128 * b:128 * b + 128],
                                                 ident[:, :])
                    mm.then_inc(s_tp, 1)

            def pv(g, sb_):
                u = g * NB + sb_
                pe.wait_ge(s_te, banks_before(g * U + HG * sb_ + HG))
                pe.wait_ge(s_ov, u + 1)
                for b in range(sb_ + 1):
                    for h in range(HG):
                        mm = nc.tensor.matmul(PS[32 * h:32 * h + DH + 1, 6, 0:128],
                                              V[:, b, HG * g + h, :], PT[:, u % 2, h, b, :],
                                              start=(b == 0), stop=(b == sb_),
                                              tile_position=(0, 32 * h))
                mm.then_inc(s_pv, 1)

            pe.wait_ge(s_vs, 4)
            pe.wait_ge(s_plo, 6)
            pe.wait_ge(s_wlo, 2)
            pe.wait_ge(s_whi, 2)
            pe.wait_ge(s_wsw, 8)
            for j in range(16):
                qjob(0, j)
            for m in LEAD[-2] + LEAD[-1]:
                scores(m)
            for g in range(G):
                for i in range(U):
                    n = g * U + i
                    if g < G - 1 and i in job_at:
                        qjob(g + 1, job_at.index(i))
                    if g == G - 1 and i in wjob_at:
                        wjob(wjob_at.index(i))
                    transp(n)
                    for m in LEAD[i]:
                        if g * U + m < G * U:
                            scores(g * U + m)
                    if i % HG == 0 and i > 0:
                        pv(g, i // HG - 1)
                pv(g, NB - 1)

            pe.wait_ge(ld_wo, 16)
            pe.wait_ge(s_ex, G * U)
            pe.wait_ge(s_te, banks_before(G * U))
            pe.wait_ge(s_afr, 16 * G + 24)
            pe.wait_ge(s_ov, G * NB + 1)
            for s in range(NB + 5):
                if s < NB:
                    b = s
                    if b >= 2:
                        pe.wait_ge(t_n, b - 1)
                    for g in range(G):
                        mm = nc.tensor.transpose(PS[:, b % 2, 128 * g:128 * g + 128],
                                                 OT[:, g, 128 * b:128 * b + 128], ident[:, :])
                    mm.then_inc(t_a, 1)
                if 0 <= s - 1 < NB:
                    b = s - 1
                    pe.wait_ge(t_n, b + 1)
                    if b >= 2:
                        pe.wait_ge(t_e, b - 1)
                    for k in range(2):
                        mm = nc.tensor.transpose(PS[:, 2 + b % 2, 128 * k:128 * k + 128],
                                                 AN[:, b % 4, 128 * k:128 * k + 128], ident[:, :])
                    mm.then_inc(t_b, 1)
                if 0 <= s - 2 < NB:
                    b = s - 2
                    pe.wait_ge(t_e, b + 1)
                    if b >= 2:
                        pe.wait_ge(t_y, b - 1)
                    for k in range(2):
                        mm = nc.tensor.matmul(bank(4 + b % 2, 256), AT[:, b % 4, k, :], WO[:, k, :],
                                              start=(k == 0), stop=(k == 1))
                    mm.then_inc(t_c, 1)
                if 0 <= s - 4 < NB:
                    b = s - 4
                    pe.wait_ge(t_xn, b + 1)
                    if b >= 2:
                        pe.wait_ge(t_lo, b - 1)
                    for k in range(2):
                        mm = nc.tensor.transpose(PS[:, 6 + b % 2, 128 * k:128 * k + 128],
                                                 XN2[:, b % 4, 128 * k:128 * k + 128], ident[:, :])
                    mm.then_inc(t_d, 1)

            def down(k):
                c, n = divmod(k, NT)
                pe.wait_ge(m_hi, k + 1)
                pe.wait_ge(m_lo, k + 1)
                for a in range(4):
                    o = PS[:, 4 + 2 * c + a // 2, 256 * (a % 2):256 * (a % 2) + 256]
                    lh = [IH[:, k % 3, s, 128 * a:128 * a + 128] for s in range(2)]
                    mm = split_mm(o, lh, [WD[s][:, n, :] for s in range(2)],
                                  start=(n == 0 and a % 2 == 0), stop=(n == NT - 1), check=False)
                mm.then_inc(m_d, 1)

            pe.wait_ge(t_lo, NB)
            pe.wait_ge(t_y, NB)
            for k in range(2 * NT + 2):
                if k < 2 * NT:
                    c, n = divmod(k, NT)
                    xs = [[X2[:, s, kc, 512 * c:512 * c + 512] for s in range(2)]
                          for kc in range(2)]
                    for w, b0, done in ((WG, 0, m_g), (WU, 2, m_u)):
                        if k >= 2:
                            pe.wait_ge(m_h if b0 == 0 else m_it, k - 1)
                        for kc in range(2):
                            mm = split_mm(bank(b0 + k % 2),
                                          [w[s][:, kc, 128 * n:128 * n + 128] for s in range(2)],
                                          xs[kc], start=(kc == 0), stop=(kc == 1))
                        mm.then_inc(done, 1)
                if k >= 2:
                    down(k - 2)

        @block.vector
        def _(dve):
            chain = [0]

            def link(ins):
                chain[0] += 1
                ins.then_inc(s_v, 1)
                dve.wait_ge(s_v, chain[0])

            V_ = nc.vector
            dve.wait_ge(ld_x, 16)
            for b in range(NB):
                i = V_.bn_stats(st6[:, b, :], X[:, b, :])
            link(i)
            for b in range(NB):
                i = V_.bn_aggr(mv[:, b, :], st6[:, b, :])
            link(i)
            V_.tensor_scalar(rs[:, :], mv[:, :, 1], EPS, None, ALU.add).then_inc(s_st, 1)
            dve.wait_ge(s_pow, 1)
            for b in range(NB):
                V_.tensor_scalar(XN[:, b, :], X[:, b, :], mv[:, b, 0:1], rs[:, b:b + 1],
                                 ALU.subtract, ALU.mult).then_inc(s_xn, 1)
            dve.wait_ge(s_nsum, 1)
            link(V_.tensor_scalar(NF, bank(7, 6), 1e-20, None, ALU.max))
            link(V_.tensor_tensor(nrm[:, 3:4], nrm[:, 3:4], nrm[:, 4:5], ALU.add))
            V_.tensor_copy(nrm[:, 6:7], nrm[:, 3:4]).then_inc(s_st, 1)
            dve.wait_ge(s_pow, 2)
            n_dq, n_dkv, n_kr, n_q, n_uk = (nrm[:, 8 + i:9 + i] for i in (0, 1, 2, 3, 5))
            link(V_.tensor_scalar(tmp1, n_dkv, n_uk, None, ALU.mult))
            link(V_.tensor_tensor(DEN, tmp1, n_kr, ALU.add))
            link(V_.reciprocal(rD, DEN))
            link(V_.reciprocal(nrm[:, 24:25], n_q))
            link(V_.reciprocal(nrm[:, 21:22], n_dq))
            link(V_.reciprocal(nrm[:, 22:23], n_dkv))
            link(V_.tensor_scalar(f_q, f_q, WS, None, ALU.mult))
            link(V_.tensor_scalar(f_dq, f_dq, XS, None, ALU.mult))
            link(V_.tensor_scalar(f_dkv, f_dkv, XS, None, ALU.mult))
            link(V_.tensor_scalar(f_kr, rD, XS * WS, None, ALU.mult))
            link(V_.tensor_scalar(f_uk, rD, n_dkv, WS, ALU.mult, ALU.mult))
            link(V_.tensor_scalar(f_uv, n_dkv, 1.0 / XS, None, ALU.mult))
            link(V_.tensor_scalar(tmp2, n_dq, n_q, None, ALU.mult))
            link(V_.tensor_scalar(ESC, tmp2, DEN, DH ** -0.5 / XS ** 2, ALU.mult, ALU.mult))
            link(V_.tensor_scalar(NESC, ESC, -1.0, None, ALU.mult))
            V_.tensor_scalar(w_dq_s, w_dq_s, f_dq, None, ALU.mult)
            V_.tensor_scalar(w_dkv_s, w_dkv_s, f_dkv, None, ALU.mult)
            krp = r_kr.rearrange("p k (i a) -> p k a i", a=2)
            for e in range(2):
                for a in range(2):
                    o = 64 * e + 32 * a
                    V_.tensor_scalar(KR2[:, :, o:o + 32], krp[:, :, a, :], f_kr, None, ALU.mult)
                    i = V_.tensor_scalar(KR2S[:, :, o:o + 32], krp[:, :, 1 - a, :], f_kr, None,
                                         ALU.mult)
            i.then_inc(s_wf, 1)
            for e in range(2):
                dst = WQ32.rearrange("p (q e) c -> p q e c", e=2)[:, :, e, :]
                qc = r_qc.rearrange("p (q e) c -> p q e c", e=2)[:, :, e, :]
                qr = r_qr.rearrange("p (q e) (i a) -> p q e a i", e=2, a=2)[:, :, e, :, :]
                for a in range(2):
                    o = 64 * e + 32 * a
                    V_.tensor_scalar(dst[:, :, o:o + 32], qr[:, :, a, :], f_q, None, ALU.mult)
                o = 64 * (1 - e)
                i = V_.tensor_scalar(dst[:, :, o:o + 64], qc, f_q, None, ALU.mult)
            i.then_inc(s_wf, 1)
            for e in range(2):
                i = V_.tensor_scalar(WUK32[:, :, 64 * (1 - e):64 * (1 - e) + 64],
                                     r_uk.rearrange("p (q e) c -> p q e c", e=2)[:, :, e, :],
                                     f_uk, None, ALU.mult)
            i.then_inc(s_wf, 1)
            link(V_.tensor_scalar(w_uv_s, w_uv_s, f_uv, None, ALU.mult))
            dve.wait_ge(s_wf, 3)
            dve.wait_ge(s_whi, 1)
            V_.tensor_tensor(WQ[:, 1, :, :], WQ32, WQ[:, 0, :, :], ALU.subtract).then_inc(s_wlo, 1)
            dve.wait_ge(s_whi, 2)
            V_.tensor_tensor(WUK[:, 1, :, :], WUK32, WUK[:, 0, :, :], ALU.subtract)\
                .then_inc(s_wlo, 1)
            for j in range(4):
                hf = j % 2
                cols = slice(512 * hf, 512 * hf + 512)
                dve.wait_ge(s_phi, j + 1 if j < 2 else 2 + 2 * (j - 1))
                t = (XD, CK)[j // 2]
                V_.tensor_tensor(t[:, 1, cols], bank(4 + j), t[:, 0, cols], ALU.subtract)\
                    .then_inc(s_plo, 1)
            dve.wait_ge(ld_rope, 64)
            for hf in range(2):
                cols = slice(512 * hf, 512 * hf + 512)
                dve.wait_ge(s_pj, 6 + 2 * hf)
                a, b = STG[:, 0, 0, :], STG[:, 0, 1, :]
                link(V_.tensor_tensor(a, bank(2 * hf), CF[:, cols], ALU.mult))
                link(V_.tensor_tensor(b, bank(2 * hf + 1), SS[:, cols], ALU.mult))
                link(V_.tensor_tensor(a, a, b, ALU.add))
                hi = STG[:, 0, 2, 0:256].bitcast(F16)
                link(V_.tensor_copy(hi, a))
                lo = STG[:, 1, 2, 0:256].bitcast(F16)
                link(V_.tensor_tensor(lo, a, hi, ALU.subtract))
                for e in range(2):
                    r = slice(64 * e, 64 * e + 64)
                    for k, src in ((KH, hi), (KL, lo)):
                        for bf in range(2):
                            for pr in range(2):
                                i = V_.tensor_copy(k[r, bf, 2 * pr + e, cols], src[r, :])
                i.then_inc(s_plo, 1)
                dve.wait_ge(s_plo, 5 + hf)
            for v in range(4):
                dve.wait_ge(s_vp, v + 1)
                V_.tensor_copy(V[:, 2 * v:2 * v + 2, :, 0:DH],
                               bank(4 + v).rearrange("p (b h c) -> p b h c", b=2, h=H))\
                    .then_inc(s_vs, 1)
            dve.wait_ge(s_vs, 4)
            V_.memset(bank(6), 0.0).then_inc(s_ov, 1)

            def qwork(g, j):
                pr, hf, kind = QJOBS[j]
                n, m = aux_index(g, j), 4 * g + j // 4
                cols = slice(512 * hf, 512 * hf + 512)
                dve.wait_ge(s_aux, n + 1)
                if kind == "K":
                    dve.wait_ge(s_ahi, 2 * (m + 1))
                    for e, r in ((1, 0), (0, 64)):
                        i = V_.scalar_tensor_tensor(
                            out=KL[r:r + 64, g % 2, 2 * pr + e, cols], in0=PS[r:r + 64, 7, :],
                            scalar=1.0 / WS, in1=KH[r:r + 64, g % 2, 2 * pr + e, cols],
                            op0=ALU.mult, op1=ALU.subtract)
                    i.then_inc(s_afr, 1)
                    return
                k = "SAB".index(kind)
                if k == 0 and m >= 2:
                    dve.wait_ge(s_qlo, 2 * (m - 1))
                tab = (SS, CA, CB)[k]
                V_.tensor_tensor(STG[:, m % 2, k, :], bank(7), tab[:, cols], ALU.mult)\
                    .then_inc(s_afr, 1)

            def qhi(g, m):
                n = 4 * g + m
                pr, hf = m // 2, m % 2
                if g >= 2 and m == 0:
                    dve.wait_ge(s_sc, U * (g - 1))
                dve.wait_ge(s_rot, 2 * (n + 1))
                for e in range(2):
                    V_.tensor_copy(QH[:, g % 2, 2 * pr + e, 512 * hf:512 * hf + 512],
                                   STG[:, n % 2, 1 + e, :]).then_inc(s_qhi, 1)

            def maxima(n):
                i = n % U
                w = width(i // HG)
                dve.wait_ge(s_sc, n + 1)
                if n >= 8:
                    dve.wait_ge(s_ex, n - 7)
                V_.tensor_reduce(mx[:, n % 4:n % 4 + 1], slot(ps, n), AX.X, ALU.max)\
                    .then_inc(s_mx, 1)
                dve.wait_ge(s_mx, n + 1)
                V_.tensor_scalar(nb[:, n % 8:n % 8 + 1], mx[:, n % 4:n % 4 + 1], NESC, None,
                                 ALU.mult).then_inc(s_nb, 1)

            def take_out(u):
                g, sb_ = divmod(u, NB)
                dve.wait_ge(s_pv, u + 1)
                V_.tensor_copy(OT[:, g, 128 * sb_:128 * sb_ + 128], PS[:, 6, 0:128])\
                    .then_inc(s_ov, 1)

            def scale_factors():
                dve.wait_ge(ld_s, 48)
                for m, dst in ((0, GM), (1, UM), (2, gx[:, 2:3])):
                    src = SG[:, m, :]
                    if m < 2:
                        src = src.rearrange("p (n b) -> p n b", b=8)
                    low = SM[:, 7, 0:dst.shape[1]]
                    link(V_.tensor_reduce(dst, src, AX.X, ALU.max))
                    link(V_.tensor_reduce(low, src, AX.X, ALU.min))
                    link(V_.scalar_tensor_tensor(out=dst, in0=low, scalar=-1.0, in1=dst,
                                                 op0=ALU.mult, op1=ALU.max))
                link(V_.tensor_scalar(SM[:, 0:2, :], SM[:, 0:2, :], 1e-6, None, ALU.max))
                link(V_.tensor_reduce(gx[:, 0:2], SM[:, 0:2, :], AX.X, ALU.max))
                V_.tensor_scalar(gx[:, 2:3], gx[:, 2:3], 1e-6, None, ALU.max).then_inc(s_sm, 1)
                link(V_.reciprocal(SM[:, 2:4, :], SM[:, 0:2, :]))
                dve.wait_ge(s_gm, 1)
                link(V_.reciprocal(gx[:, 8:11], gx[:, 4:7]))
                for m in range(2):
                    sv = SG[:, m, :].rearrange("p (n b) -> p n b", b=8)
                    link(V_.scalar_tensor_tensor(
                        out=sv, in0=sv, scalar=FS * CODE,
                        in1=SM[:, 2 + m, :].unsqueeze(2).broadcast_to([128, NT, 8]),
                        op0=ALU.mult, op1=ALU.mult))
                link(V_.tensor_scalar(SG[:, 2, :], SG[:, 2, :], gx[:, 10:11], FS * CODE, ALU.mult,
                                      ALU.mult))
                link(V_.tensor_scalar(K3, GM, math.sqrt(G3) / (XS * FS), None, ALU.mult))
                link(V_.tensor_scalar(KT, GM, GC / (XS * FS), None, ALU.mult))
                link(V_.tensor_tensor(KI, GM, UM, ALU.mult))
                link(V_.tensor_scalar(tmp1, gx[:, 8:9], gx[:, 9:10], None, ALU.mult))
                link(V_.tensor_scalar(KI, KI, tmp1, 0.5 * IS / (XS * FS) ** 2, ALU.mult, ALU.mult))
                link(V_.tensor_scalar(tmp2, tmp1, gx[:, 10:11], IS * FS, ALU.mult, ALU.mult))
                V_.tensor_scalar(CEPS, tmp2, tmp2, EPS, ALU.mult, ALU.mult).then_inc(s_sf, 1)

            def spread(q):
                raw = RAW[:, q % 2, :]
                y, t = (STG[:, 0, k, :].bitcast(I32) for k in range(2))
                if q == 0:
                    dve.wait_ge(s_qlo, 8 * G)
                dve.wait_ge(ld_raw[q % 2], 16 * (q // 2 + 1))
                link(V_.scalar_tensor_tensor(out=y, in0=raw, scalar=12, in1=raw,
                                             op0=ALU.logical_shift_left, op1=ALU.bitwise_or))
                link(V_.tensor_scalar(t, y, 0x00070007, 9, ALU.bitwise_and,
                                      ALU.logical_shift_left))
                link(V_.tensor_scalar(y, y, 0x00080008, 12, ALU.bitwise_and,
                                      ALU.logical_shift_left))
                if q >= 1:
                    dve.wait_ge(s_deq, q)
                V_.tensor_tensor(BITS[:, :], t, y, ALU.bitwise_or).then_inc(s_bits, 1)

            def wlo(j):
                m, c, k = WJOBS[j]
                dve.wait_ge(s_ahi, 8 * G + j + 1)
                if m < 2:
                    cols = slice(512 * c, 512 * c + 512)
                    w = (WG, WU)[m]
                    V_.tensor_tensor(w[1][:, k, cols], bank(7), w[0][:, k, cols], ALU.subtract)\
                        .then_inc(s_afr, 1)
                else:
                    h, n0 = c // 2, 8 * (c % 2) + 4 * k
                    V_.tensor_tensor(WD[1][:, n0:n0 + 4, 128 * h:128 * h + 128],
                                     bank(7).rearrange("p (n c) -> p n c", n=4),
                                     WD[0][:, n0:n0 + 4, 128 * h:128 * h + 128],
                                     ALU.subtract).then_inc(s_afr, 1)

            for m in range(4):
                for j in range(4 * m, 4 * m + 4):
                    qwork(0, j)
                qhi(0, m)
            for m in SOON[-2] + SOON[-1]:
                maxima(m)
            scale_factors()
            for g in range(G):
                if g == G - 1:
                    spread(0)
                for i in range(U):
                    n = g * U + i
                    if g < G - 1:
                        if i in job_at:
                            j = job_at.index(i)
                            qwork(g + 1, j)
                            if j % 4 == 1 and j > 4:
                                qhi(g + 1, j // 4 - 1)
                        if i == 26:
                            qhi(g + 1, 3)
                    elif i in wjob_at:
                        j = wjob_at.index(i)
                        wlo(j)
                    for m in SOON[i]:
                        if g * U + m < G * U:
                            maxima(g * U + m)
                    if g == G - 1 and i % 2 == 1 and i // 2 + 1 < 12:
                        spread(i // 2 + 1)
                    if i % HG == 0 and i > 0:
                        take_out(g * NB + i // HG - 1)
                take_out(g * NB + NB - 1)

            def norm_stats(src, b, eps, done):
                link(V_.bn_stats(st6[:, b, :], src))
                link(V_.bn_aggr(mv[:, b, :], st6[:, b, :]))
                V_.tensor_scalar(rs[:, b:b + 1], mv[:, b, 1:2], eps, None, ALU.add)\
                    .then_inc(done, 1)

            for s in range(NB + 5):
                if s < NB:
                    b = s
                    dve.wait_ge(t_a, b + 1)
                    t = bank(b % 2).rearrange("p (h c) -> p h c", c=32)
                    link(V_.reciprocal(rc[:, b % 2, :], t[:, :, DH]))
                    if b >= 4:
                        dve.wait_ge(t_b, b - 3)
                    V_.tensor_tensor(AN[:, b % 4, :].rearrange("p (h c) -> p h c", c=DH),
                                     t[:, :, 0:DH],
                                     rc[:, b % 2, :].unsqueeze(2).broadcast_to([128, H, DH]),
                                     ALU.mult).then_inc(t_n, 1)
                if 0 <= s - 2 < NB:
                    b = s - 2
                    dve.wait_ge(t_c, b + 1)
                    norm_stats(bank(4 + b % 2, 256), b, EPS, t_st)
                    dve.wait_ge(t_pw, 2 * b + 1)
                    V_.tensor_scalar(YB[:, b % 4, :], bank(4 + b % 2, 256), mv[:, b, 0:1],
                                     rs[:, b:b + 1], ALU.subtract, ALU.mult).then_inc(t_y, 1)
                    dve.wait_ge(t_x, b + 1)
                    norm_stats(X[:, b, :], b, EPS, t_st)
                    dve.wait_ge(t_pw, 2 * b + 2)
                    link(V_.tensor_scalar(XN2[:, b % 4, :], X[:, b, :], mv[:, b, 0:1],
                                          rs[:, b:b + 1], ALU.subtract, ALU.mult))
                    if b >= 4:
                        dve.wait_ge(t_d, b - 3)
                    V_.tensor_scalar(XN2[:, b % 4, :], XN2[:, b % 4, :], XS, None, ALU.mult)\
                        .then_inc(t_xn, 1)
                if 0 <= s - 4 < NB:
                    b = s - 4
                    dve.wait_ge(t_hi, b + 1)
                    cols = slice(128 * b, 128 * b + 128)
                    V_.tensor_tensor(X2[:, 1, :, cols],
                                     bank(6 + b % 2, 256).rearrange("p (k t) -> p k t", k=2),
                                     X2[:, 0, :, cols], ALU.subtract).then_inc(t_lo, 1)
            for k in range(2 * NT):
                n = k % NT
                dve.wait_ge(m_sq, k + 1)
                V_.scalar_tensor_tensor(out=inn[:, k % 2, :], in0=sq[:, k % 2, :], scalar=1.0,
                                        in1=bank(k % 2), op0=ALU.add, op1=ALU.mult)\
                    .then_inc(m_in, 1)
                dve.wait_ge(m_th, k + 1)
                V_.scalar_tensor_tensor(out=hg[:, k % 2, :], in0=inn[:, k % 2, :], scalar=1.0,
                                        in1=bank(k % 2), op0=ALU.add, op1=ALU.mult)\
                    .then_inc(m_h, 1)
                dve.wait_ge(m_h, k + 1)
                dve.wait_ge(m_u, k + 1)
                if k >= 2:
                    dve.wait_ge(m_lo, k - 1)
                V_.scalar_tensor_tensor(out=itr[:, k % 2, :], in0=hg[:, k % 2, :],
                                        scalar=KI[:, n:n + 1], in1=bank(2 + k % 2), op0=ALU.mult,
                                        op1=ALU.mult).then_inc(m_it, 1)
            for b in range(NB):
                o = PS[:, 4 + b // 2, 256 * (b % 2):256 * (b % 2) + 256]
                dve.wait_ge(m_d, NT * (b // 4 + 1))
                norm_stats(o, b, CEPS, t_st)
                dve.wait_ge(t_pw, 2 * NB + b + 1)
                if b >= 4:
                    dve.wait_ge(t_x, NB + b - 3)
                V_.tensor_scalar(YB[:, b % 4, :], o, mv[:, b, 0:1], rs[:, b:b + 1], ALU.subtract,
                                 ALU.mult).then_inc(t_y, 1)


_INS = ["L0_attn_x", "L0_attn_W_dkv", "L0_attn_W_dq", "L0_attn_W_kr", "L0_attn_W_qc", "L0_attn_W_qr",
        "L0_attn_W_uk", "L0_attn_W_uv", "L0_attn_W_o", "L0_ffn_gate_W_packed", "L0_ffn_gate_scales",
        "L0_ffn_up_W_packed", "L0_ffn_up_scales", "L0_ffn_down_W_packed", "L0_ffn_down_scales"]


def _rope_constants():
    half = DR // 2
    freqs = np.exp(np.arange(half, dtype=np.float32) * np.float32(-math.log(10000.0) / half))
    ang = (np.arange(T, dtype=np.float32)[None, :] * freqs[:, None].astype(np.float32))
    cos = (np.cos(ang.astype(np.float64)) / WS).astype(np.float32)
    sin = (np.sin(ang.astype(np.float64)) / WS).astype(np.float32)
    return np.concatenate([cos] * 4), np.concatenate([-sin, sin] * 2)


def kernel(**inputs):
    import numpy as _np
    import concourse.bacc as _bacc
    from concourse import mybir as _mybir
    from concourse.bass_utils import run_bass_kernel_spmd as _run

    nc = _bacc.Bacc("TRN2", target_bir_lowering=False, num_devices=1)
    arrays, args = {}, []
    cos, sin = _rope_constants()
    for name, a in [(n, inputs[n]) for n in _INS] + [("rope_cos", cos), ("rope_sin", sin)]:
        a = _np.ascontiguousarray(a)
        arrays[f"in_{name}_dram"] = a
        args.append(nc.dram_tensor(f"in_{name}_dram", a.shape, _mybir.dt.from_np(a.dtype),
                                   kind="ExternalInput").ap())
    out = nc.dram_tensor("out_0_dram", (1, T, E), F32, kind="ExternalOutput").ap()
    layer_kernel(nc, *args, out)
    r = _run(nc, [arrays], core_ids=[0])
    return r.results[0]["out_0_dram"]
```

```python
import math
from contextlib import ExitStack

import numpy as np

import concourse.bass as bass
from concourse import mybir

F32 = mybir.dt.float32
F16 = mybir.dt.float16
BF16 = mybir.dt.bfloat16
I32 = mybir.dt.int32
ALU = mybir.AluOpType
ACT = mybir.ActivationFunctionType
AX = mybir.AxisListType
RMAX = bass.bass_isa.ReduceOp.max

T, E = 1024, 256
H, DKV, DC, DR, DH = 16, 128, 64, 64, 16
F = 2048
QB = 32
NB = T // 128
NT = F // 128
HG = 4
G = H // HG
U = NB * HG
EPS = 1e-5
GC = 0.7978845608028654
G3 = 0.044715
XS = 2.0 ** 11
WS = 2.0 ** 14
FS = 2.0 ** 11
CODE = 2.0 ** 14
IS = 2.0 ** -6
MASK = -1e38


def layer_kernel(nc, x, w_dkv, w_dq, w_kr, w_qc, w_qr, w_uk, w_uv, w_o, gate_w, gate_s, up_w, up_s,
                 down_w, down_s, rope_cos, rope_sin, out):
    with ExitStack() as ctx:
        def sb(name, shape, dt=F32):
            return ctx.enter_context(nc.sbuf_tensor(name, shape, dt))

        def sem(name):
            return ctx.enter_context(nc.semaphore(name))

        X = sb("X", [128, NB, E])
        XD = sb("XD", [128, 2, T], F16)
        CK = sb("CK", [128, 2, T], F16)
        WP = sb("WP", [128, 8192], F16)
        CA = sb("CA", [128, T])
        CB = sb("CB", [128, T])
        SS = sb("SS", [128, T])
        V = sb("V", [128, NB, H, DH + 1])
        QH = sb("QH", [128, 2, HG, T], F16)
        QL = sb("QL", [128, 2, HG, T], F16)
        KH = sb("KH", [128, 2, HG, T], F16)
        KL = sb("KL", [128, 2, HG, T], F16)
        PR = sb("PR", [128, 4, 512])
        PT = sb("PT", [128, 2, HG, NB, 128])
        OT = sb("OT", [128, G, T])
        STG = sb("STG", [128, 2, 3, 512])
        WO = sb("WO", [128, 2, E])
        RAW = sb("RAW", [128, 2, 512], I32)
        BITS = sb("BITS", [128, 512], I32)
        DQ = sb("DQ", [128, 2, 1024])
        ident = sb("ident", [128, 128])
        identb = sb("identb", [128, 128], BF16)
        maskb = sb("maskb", [128, 128], BF16)
        ones = sb("ones", [128, 128])
        st6 = sb("st6", [128, NB, 6])
        mv = sb("mv", [128, NB, 2])
        rs = sb("rs", [128, NB])
        powc = sb("powc", [128, 2, 8])
        nrm = sb("nrm", [128, 32])
        mx = sb("mx", [128, 8])
        nb = sb("nb", [128, 8])
        SG = sb("SG", [128, 3, NT * 8])
        SM = sb("SM", [128, 8, NT])
        gx = sb("gx", [128, 16])
        rc = sb("rc", [128, 2, H])
        PS = ctx.enter_context(nc.psum_tensor("PS", [128, 8, 512], F32))

        pt = PT[:, :, :, :, :].rearrange("p a h b c -> p (a h b c)")
        xT = pt[:, 0:2048].rearrange("p (k t) -> p k t", k=2)
        CKV = pt[:, 2048:3072]
        r_qc = pt[:, 3072:4096].rearrange("p (h c) -> p h c", h=H)
        r_qr = pt[:, 4096:5120].rearrange("p (h c) -> p h c", h=H)
        r_uk = pt[:, 5120:6144].rearrange("p (h c) -> p h c", h=H)
        CF = pt[:, 6144:7168]
        r_dq = pt[:, 7168:7424].rearrange("p (k m) -> p k m", k=2)
        r_dkv = pt[:, 7424:7680].rearrange("p (k m) -> p k m", k=2)
        r_kr = pt[:, 7680:7808].rearrange("p (k m) -> p k m", k=2)
        ot = OT[:, :, :].rearrange("p g t -> p (g t)")
        r_uv = ot[:, 3072:3328].rearrange("p (h c) -> p h c", h=H)
        KR2 = ot[:, 3328:3584].rearrange("p (k m) -> p k m", k=2)
        KR2S = ot[:, 3584:3840].rearrange("p (k m) -> p k m", k=2)
        XN = PR[:, :, :].rearrange("p a (b c) -> p (a b) c", c=E)
        pr = PR[:, :, :].rearrange("p a c -> p (a c)")
        junk = STG[:, :, :, :].rearrange("p a b c -> p (a b c)")
        KRS = DQ[:, 1, :].bitcast(F16).rearrange("p (s t) -> p s t", s=2)
        WQ = WP[:, 0:4096].rearrange("p (s h c) -> p s h c", s=2, h=H)
        WSW = WP[:, 4096:6144].rearrange("p (s q c) -> p s q c", s=2, q=H // 2)
        WUK = WP[:, 6144:8192].rearrange("p (s q c) -> p s q c", s=2, q=H // 2)
        WG = [q[:, 0, :, :].rearrange("p h t -> p (h t)").rearrange("p (k n) -> p k n", k=2)
              for q in (QH, QL)]
        WU = [q[:, 0, :, :].rearrange("p h t -> p (h t)").rearrange("p (k n) -> p k n", k=2)
              for q in (KH, KL)]
        WD = [WP[:, 4096 * s:4096 * (s + 1)].rearrange("p (n h) -> p n h", n=NT) for s in range(2)]
        X2 = pt[:, 0:2048].bitcast(F16).rearrange("p (s k t) -> p s k t", s=2, k=2)
        sq = pt[:, 2048:3072].rearrange("p (a t) -> p a t", a=2)
        inn = pt[:, 3072:4096].rearrange("p (a t) -> p a t", a=2)
        hg = pt[:, 4096:5120].rearrange("p (a t) -> p a t", a=2)
        itr = pt[:, 5120:6144].rearrange("p (a t) -> p a t", a=2)
        IH = pt[:, 6144:7680].bitcast(F16).rearrange("p (a s t) -> p a s t", a=3, s=2)
        AN = pr[:, 0:1024].rearrange("p (a c) -> p a c", a=4)
        YB = pr[:, 1024:2048].rearrange("p (a c) -> p a c", a=4)
        AT = STG[:, 0, :, :].rearrange("p a c -> p (a c)")[:, 0:1024].rearrange(
            "p (a k t) -> p a k t", a=4, k=2)
        XN2 = STG[:, 1, :, :].rearrange("p a c -> p (a c)")[:, 0:1024].rearrange(
            "p (a c) -> p a c", a=4)
        NF, NR = nrm[:, 0:6], nrm[:, 8:14]
        DEN, rD, ESC, NESC, CEPS = (nrm[:, i:i + 1] for i in (16, 17, 18, 19, 20))
        f_dq, f_dkv, f_kr, f_q, f_uk = (nrm[:, i:i + 1] for i in range(21, 26))
        tmp1, tmp2, tmp3 = (nrm[:, i:i + 1] for i in (27, 28, 29))
        GM, UM, GI, UI, K3, KT, KI = (SM[:, i, :] for i in range(7))

        ld_x = [sem("ld_x0"), sem("ld_x1")]
        ld_w, ld_h, ld_rope, ld_wo, ld_s = (sem(s) for s in (
            "ld_w", "ld_h", "ld_rope", "ld_wo", "ld_s"))
        ld_raw = [sem("ld_raw0"), sem("ld_raw1")]
        s_const = sem("s_const")
        s_sq = sem("s_sq")
        s_nsum = sem("s_nsum")
        s_v = sem("s_v")
        s_pow = sem("s_pow")
        s_st = sem("s_st")
        s_xn = sem("s_xn")
        s_xtp = sem("s_xtp")
        s_xt = sem("s_xt")
        s_wf = sem("s_wf")
        s_whi = sem("s_whi")
        s_wlo = sem("s_wlo")
        s_uhi = sem("s_uhi")
        s_ulo = sem("s_ulo")
        s_krc = sem("s_krc")
        s_kr2 = sem("s_kr2")
        s_wsw = sem("s_wsw")
        s_pj = sem("s_pj")
        s_phi = sem("s_phi")
        s_plo = sem("s_plo")
        s_vp = sem("s_vp")
        s_vs = sem("s_vs")
        s_sc = sem("s_sc")
        s_nb = sem("s_nb")
        s_mx = sem("s_mx")
        s_ex = sem("s_ex")
        s_tp = sem("s_tp")
        s_te = sem("s_te")
        s_pv = sem("s_pv")
        s_ov = sem("s_ov")
        s_aux = sem("s_aux")
        s_afr = sem("s_afr")
        s_ahi = sem("s_ahi")
        s_rot = sem("s_rot")
        s_qhi = sem("s_qhi")
        s_qlo = sem("s_qlo")
        s_bits = sem("s_bits")
        s_deq = sem("s_deq")
        s_sm = sem("s_sm")
        s_gm = sem("s_gm")
        s_sf = sem("s_sf")
        t_a, t_b, t_c, t_d = (sem(s) for s in ("t_a", "t_b", "t_c", "t_d"))
        t_n = sem("t_n")
        t_e = sem("t_e")
        t_st = sem("t_st")
        t_pw = sem("t_pw")
        t_y = sem("t_y")
        t_x = sem("t_x")
        t_xn = sem("t_xn")
        t_hi = sem("t_hi")
        t_lo = sem("t_lo")
        m_g, m_u, m_d = sem("m_g"), sem("m_u"), sem("m_d")
        m_sq, m_in, m_th, m_h, m_it, m_hi, m_lo = (sem(s) for s in (
            "m_sq", "m_in", "m_th", "m_h", "m_it", "m_hi", "m_lo"))
        s_out = sem("s_out")

        ps = PS[:, :, :].rearrange("p b c -> p (b c)")

        def bank(b, w=512):
            return PS[:, b, 0:w]

        def width(sb_):
            return (sb_ + 1) * 128

        def nbanks(i):
            return i // HG // 4 + 1

        def banks_before(n):
            g, i = divmod(n, U)
            return g * sum(nbanks(k) for k in range(U)) + sum(nbanks(k) for k in range(i))

        SMALL = U // 2

        def after(i):
            if i < HG:
                return -2 + i // 2
            if i < SMALL:
                return i - HG
            return {SMALL: SMALL - 3, SMALL + 1: SMALL - 1}.get(i, i - 2)

        def slot(base, n):
            i = n % U
            w, a = width(i // HG), (i % HG if i < SMALL else 2 * (i % 2))
            return base[:, 512 * a:512 * a + w]

        LEAD = {i: [m for m in range(U + HG) if (after(m % U) + (m // U) * U) == i]
                for i in range(-2, U)}
        SOON = {i: [m for m in range(U + HG)
                    if max(after(m % U) + (m // U) * U, m - 2) == i] for i in range(-2, U)}

        QJOBS = [(pr, hf, kind) for hf in range(2) for pr in range(HG // 2) for kind in "KABS"]
        CHUNKS = [(m, c) for m in range(2) for c in range(4)] + [(2, c) for c in range(4)]
        WJOBS = [(m, c, k) for m, c in CHUNKS for k in range(2)]
        JOBS = [{j: (g, 8 + j) for j in range(8)} | {12 + 2 * j: (g + 1, j) for j in range(8)}
                for g in range(G)]
        JOBS[0] = {1 + j: (0, 8 + j) for j in range(8)} | {12 + 2 * j: (1, j) for j in range(8)}
        JOBS[G - 2] = {j: (G - 2, 8 + j) for j in range(8)} |\
            {9 + 2 * j: (G - 1, j) for j in range(12)}
        JOBS[G - 1] = {j: (G - 1, 12 + j) for j in range(4)}
        HIS = [{6: (g, 2), 10: (g, 3), 22: (g + 1, 0), 28: (g + 1, 1)} for g in range(G)]
        HIS[G - 2] = {6: (G - 2, 2), 10: (G - 2, 3), 18: (G - 1, 0), 26: (G - 1, 1)}
        HIS[G - 1] = {2: (G - 1, 2), 6: (G - 1, 3)}
        wjob_at = [5, 6] + list(range(9, 31))
        spread_at = [1, 4] + [2 * q + 5 for q in range(2, 12)]

        def aux_index(g, j):
            return 16 * g + j

        def jobbank(g, j):
            return FIRST_BANKS[j] if (g, j) < (0, 8) else 7

        TAIL = NB + 9
        HALF_DONE = NB // 2 + 8
        SETUP_BANKS = [4, 5, 3, 0, 1, 2, 6, 7]
        VALUE_BANKS = [4, 5, 3, 0]
        FIRST_BANKS = [1, 0, 4, 5, 3, 2, 4, 5]

        def Q_PARTS(s):
            wq = WQ[:, s, :, :].rearrange("p (q e) c -> p q e c", e=2)
            return [wq[:, :, e, o:o + n] for e in range(2)
                    for o, n in ((64 * e, 32), (64 * e + 32, 32), (64 - 64 * e, 64))]

        qr_v = r_qr.rearrange("p (q e) (i a) -> p q e a i", e=2, a=2)
        qc_v = r_qc.rearrange("p (q e) c -> p q e c", e=2)
        Q_SRC = [v for e in range(2) for v in (qr_v[:, :, e, 0, :], qr_v[:, :, e, 1, :],
                                               qc_v[:, :, e, :])]

        def UK_PARTS(s):
            return [WUK[:, s, :, 64 - 64 * e:128 - 64 * e] for e in range(2)]

        uk_v = r_uk.rearrange("p (q e) c -> p q e c", e=2)
        UK_SRC = [uk_v[:, :, e, :] for e in range(2)]
        KCOPIES = [(buf, hf, e, q, s) for buf in range(2) for hf in range(2) for q in range(2)
                   for e in range(2) for s in range(2)]
        STATS = [(which, s - lag) for s in range(TAIL) for which, lag in (("pow1", 3), ("pow2", 5))
                 if 0 <= s - lag < NB]

        def t_count(which, b):
            return STATS.index((which, b)) + 1

        block = ctx.enter_context(nc.Block())

        @block.sync
        def _(sp):
            xv = x.rearrange("o (b p) e -> p (o b) e", p=128)
            for k in range(2):
                sp.dma_start(X[:, 4 * k:4 * k + 4, :], xv[:, 4 * k:4 * k + 4, :])\
                    .then_inc(ld_x[k], 16)
            sp.dma_start(r_kr, w_kr.rearrange("(k p) m -> p k m", p=128)).then_inc(ld_w, 16)
            sp.dma_start(r_uk, w_uk.rearrange("h p c -> p h c")).then_inc(ld_h, 16)
            sp.dma_start(r_uv, w_uv.rearrange("h p c -> p h c")).then_inc(ld_h, 16)
            sp.dma_start(CF, rope_cos[:, :]).then_inc(ld_rope, 16)
            sp.dma_start(SS[:, :], rope_sin[:, :]).then_inc(ld_rope, 16)
            sp.dma_start(CA[0:64, :], rope_cos[0:64, :]).then_inc(ld_rope, 16)
            sp.dma_start(CB[64:128, :], rope_cos[64:128, :]).then_inc(ld_rope, 16)
            sp.dma_start(WO[:, :, :], w_o.rearrange("(k p) e -> p k e", p=128)).then_inc(ld_wo, 16)
            for i, s in enumerate((gate_s, up_s)):
                sp.dma_start(SG[:, i, :].rearrange("p (n b) -> p n b", b=8),
                             s.rearrange("(n p) b -> p n b", p=128)).then_inc(ld_s, 16)
            sp.dma_start(SG[:, 2, :].rearrange("p (h b) -> p h b", h=2),
                         down_s.rearrange("(h p) b -> p h b", p=128)).then_inc(ld_s, 16)
            gw = gate_w.rearrange("(n p) w -> p n w", p=128)
            uw = up_w.rearrange("(n p) w -> p n w", p=128)
            dw = down_w.rearrange("(h p) w -> p h w", p=128)
            for q, (m, c) in enumerate(CHUNKS):
                if q >= 2:
                    sp.wait_ge(s_bits, q - 1)
                if m < 2:
                    sp.dma_start(RAW[:, q % 2, :].rearrange("p (n w) -> p n w", n=4),
                                 (gw, uw)[m][:, 4 * c:4 * c + 4, :]).then_inc(ld_raw[q % 2], 16)
                else:
                    sp.dma_start(RAW[:, q % 2, :], dw[:, c // 2, 512 * (c % 2):512 * (c % 2 + 1)]
                                 ).then_inc(ld_raw[q % 2], 16)
            for b in range(NB):
                sp.wait_ge(t_x, NB + b + 1)
                sp.dma_start(out.rearrange("o (b p) e -> p (o b) e", p=128)[:, b, :],
                             X[:, b, :]).then_inc(s_out, 16)
            sp.wait_ge(s_out, 16 * NB)

        @block.gpsimd
        def _(pool):
            nc.gpsimd.memset(ones[:, :], 1.0).then_inc(s_const, 1)
            nc.gpsimd.memset(powc[:, 0, :], -0.5).then_inc(s_const, 1)
            nc.gpsimd.memset(powc[:, 1, :], 0.5).then_inc(s_const, 1)
            nc.gpsimd.memset(ident[:, :], 0.0).then_inc(s_const, 1)
            nc.gpsimd.memset(identb[:, :], 0.0).then_inc(s_const, 1)
            nc.gpsimd.memset(maskb[:, :], 0.0).then_inc(s_const, 1)
            pool.wait_ge(s_const, 6)
            nc.gpsimd.affine_select(out=ident[:, :], in_=ident[:, :], compare_op=ALU.not_equal,
                                    fill=1.0, base=0, pattern=[[-1, 128]],
                                    channel_multiplier=1).then_inc(s_const, 1)
            nc.gpsimd.affine_select(out=identb[:, :], in_=identb[:, :], compare_op=ALU.not_equal,
                                    fill=1.0, base=0, pattern=[[-1, 128]],
                                    channel_multiplier=1).then_inc(s_const, 1)
            nc.gpsimd.affine_select(out=maskb[:, :], in_=maskb[:, :], compare_op=ALU.is_ge,
                                    fill=MASK, base=0, pattern=[[-1, 128]],
                                    channel_multiplier=1).then_inc(s_const, 1)
            for k in range(2):
                pool.wait_ge(s_st, k + 1)
                nc.gpsimd.tensor_tensor(rs[:, 4 * k:4 * k + 4], rs[:, 4 * k:4 * k + 4],
                                        powc[:, 0, 0:4], ALU.pow).then_inc(s_pow, 1)
            pool.wait_ge(s_st, 3)
            nc.gpsimd.tensor_tensor(NR, NF, powc[:, 1, 0:6], ALU.pow).then_inc(s_pow, 1)
            pool.wait_ge(s_pow, 3)
            nc.gpsimd.memset(CA[64:128, :], 1.0 / WS).then_inc(s_const, 1)
            pool.wait_ge(s_const, 10)
            nc.gpsimd.memset(CB[0:64, :], 1.0 / WS).then_inc(s_const, 1)
            pool.wait_ge(s_const, 11)
            nc.gpsimd.memset(V[:, :, :, DH:DH + 1], 1.0).then_inc(s_const, 1)
            for s in range(2):
                pool.wait_ge((s_whi, s_wlo)[s], 6)
                wq = WQ[:, s, :, :].rearrange("p (q e) c -> p q e c", e=2)
                for e in range(2):
                    o = 64 * e
                    for a in range(2):
                        nc.gpsimd.tensor_copy(
                            WSW[:, s, :, o + 32 * a:o + 32 * a + 32],
                            wq[:, :, e, o + 32 * (1 - a):o + 32 * (1 - a) + 32]).then_inc(s_wsw, 1)

            def rotate(g, m):
                n = 4 * g + m
                hf, pr = divmod(m, 2)
                pool.wait_ge(s_afr, 4 * n + 4)
                w, a, b = (STG[:, n % 2, k, :] for k in range(3))
                if n == 0:
                    pool.wait_ge(s_wsw, 8)
                else:
                    pool.wait_ge(s_qlo, 2 * n)
                nc.gpsimd.tensor_tensor(a[0:64, :], a[0:64, :], w[0:64, :], ALU.add)\
                    .then_inc(s_rot, 1)
                pool.wait_ge(s_rot, 2 * n + 1)
                nc.gpsimd.tensor_tensor(b[64:128, :], b[64:128, :], w[64:128, :], ALU.add)\
                    .then_inc(s_rot, 1)
                pool.wait_ge(s_qhi, 2 * (n + 1))
                for e in range(2):
                    dst = QL[:, g % 2, 2 * pr + e, 512 * hf:512 * hf + 512]
                    if e == 0 and g >= 2 and m == 0:
                        pool.wait_ge(s_sc, U * (g - 1))
                    nc.gpsimd.tensor_tensor(dst, STG[:, n % 2, 1 + e, :],
                                            QH[:, g % 2, 2 * pr + e, 512 * hf:512 * hf + 512],
                                            ALU.subtract).then_inc(s_qlo, 1)

            def dequant(q):
                m, c = CHUNKS[q]
                pool.wait_ge(s_bits, q + 1)
                if q == 0:
                    pool.wait_ge(s_sf, 1)
                if q >= 2:
                    pool.wait_ge(s_aux, 16 * G + 2 * (q - 1))
                codes = BITS[:, :].bitcast(F16).rearrange("p (b k) -> p b k", k=QB)
                if m < 2:
                    sc = SG[:, m, 32 * c:32 * c + 32]
                else:
                    sc = SG[:, 2, 64 * (c // 2) + 32 * (c % 2):64 * (c // 2) + 32 * (c % 2) + 32]
                nc.gpsimd.tensor_tensor(DQ[:, q % 2, :].rearrange("p (b k) -> p b k", k=QB), codes,
                                        sc.unsqueeze(2).broadcast_to([128, 32, QB]),
                                        ALU.mult).then_inc(s_deq, 1)

            for m in range(4):
                rotate(0, m)
            pool.wait_ge(s_sm, 1)
            nc.gpsimd.partition_all_reduce(gx[:, 4:7], gx[:, 0:3], 128, RMAX).then_inc(s_gm, 1)
            for n in range(4, 4 * G - 1):
                rotate(n // 4, n % 4)
            dequant(0)
            rotate(G - 1, 3)
            for q in range(1, 12):
                dequant(q)
            def rstd(b, count):
                pool.wait_ge(t_st, count)
                nc.gpsimd.tensor_tensor(rs[:, b:b + 1], rs[:, b:b + 1], powc[:, 0, 0:1],
                                        ALU.pow).then_inc(t_pw, 1)

            for s in range(TAIL):
                if 0 <= s - 3 < NB:
                    rstd(s - 3, t_count("pow1", s - 3))
                if 0 <= s - 4 < NB:
                    b = s - 4
                    pool.wait_ge(t_y, b + 1)
                    nc.gpsimd.tensor_tensor(X[:, b, :], X[:, b, :], YB[:, b % 4, :], ALU.add)\
                        .then_inc(t_x, 1)
                if 0 <= s - 5 < NB:
                    rstd(s - 5, t_count("pow2", s - 5))
            for k in range(2 * NT):
                pool.wait_ge(m_hi, k + 1)
                if k >= 3:
                    pool.wait_ge(m_d, k - 2)
                nc.gpsimd.tensor_tensor(IH[:, k % 3, 1, :], itr[:, k % 2, :], IH[:, k % 3, 0, :],
                                        ALU.subtract).then_inc(m_lo, 1)
            for b in range(NB):
                rstd(b, 2 * NB + b + 1)
                pool.wait_ge(t_y, NB + b + 1)
                nc.gpsimd.tensor_tensor(X[:, b, :], X[:, b, :], YB[:, b % 4, :], ALU.add)\
                    .then_inc(t_x, 1)

        @block.scalar
        def _(act):
            act.dma_start(r_dq, w_dq.rearrange("(k p) m -> p k m", p=128)).then_inc(ld_w, 16)
            act.dma_start(r_dkv, w_dkv.rearrange("(k p) m -> p k m", p=128)).then_inc(ld_w, 16)
            act.dma_start(r_qc, w_qc.rearrange("h p c -> p h c")).then_inc(ld_h, 16)
            act.dma_start(r_qr, w_qr.rearrange("h p c -> p h c")).then_inc(ld_h, 16)

            def square_sum(i, w):
                n = w.shape[1] * w.shape[2]
                nc.scalar.activation(junk[:, 0:n].rearrange("p (a b) -> p a b", a=w.shape[1]), w,
                                     ACT.Square, accum_out=nrm[:, i:i + 1]).then_inc(s_sq, 1)
                act.wait_ge(s_sq, i + 1)

            act.wait_ge(ld_w, 48)
            for i, w in enumerate((r_dq, r_dkv, r_kr)):
                square_sum(i, w)
            for b in range(4):
                act.wait_ge(s_xtp, b + 1)
                hf, k = divmod(b, 2)
                nc.scalar.activation(xT[:, k, 512 * hf:512 * hf + 512], bank(b), ACT.Copy)\
                    .then_inc(s_xt, 1)
            act.wait_ge(ld_h, 64)
            for i, w in enumerate((r_qc, r_qr, r_uk)):
                square_sum(3 + i, w)
            for hf in range(2):
                act.wait_ge(s_pj, 3 + hf)
                nc.scalar.activation(CKV[:, 512 * hf:512 * hf + 512], bank(SETUP_BANKS[2 + hf]),
                                     ACT.Copy).then_inc(s_phi, 1)
            act.wait_ge(s_wf, 1)

            def latent_hi(hf):
                for j, f in ((hf, f_dq), (2 + hf, f_dkv)):
                    nc.scalar.activation((XD, CK)[j // 2][:, 0, 512 * hf:512 * hf + 512],
                                         bank(SETUP_BANKS[j]), ACT.Copy, scale=f)\
                        .then_inc(s_phi, 1)

            latent_hi(0)
            for dst, src in zip(UK_PARTS(0), UK_SRC):
                nc.scalar.activation(dst, src, ACT.Copy, scale=f_uk).then_inc(s_uhi, 1)
            for dst, src in zip(Q_PARTS(0), Q_SRC):
                nc.scalar.activation(dst, src, ACT.Copy, scale=f_q).then_inc(s_whi, 1)
            latent_hi(1)
            for v in range(4):
                act.wait_ge(s_vp, v + 1)
                nc.scalar.activation(V[:, 2 * v:2 * v + 2, :, 0:DH],
                                     bank(VALUE_BANKS[v]).rearrange("p (b h c) -> p b h c", b=2,
                                                                    h=H), ACT.Copy)\
                    .then_inc(s_vs, 1)

            def rope_copy(n):
                buf, hf, e, q, s = KCOPIES[n]
                act.wait_ge(s_plo, 5 + hf)
                r, cols = slice(64 * e, 64 * e + 64), slice(512 * hf, 512 * hf + 512)
                nc.scalar.activation((KH, KL)[s][r, buf, 2 * q + e, cols], KRS[r, s, cols],
                                     ACT.Copy).then_inc(s_krc, 1)

            def khi(g, j):
                pr, hf, _ = QJOBS[j]
                act.wait_ge(s_aux, aux_index(g, j) + 1)
                if g >= 2 and j == 0:
                    act.wait_ge(s_sc, U * (g - 1))
                for e, r in ((1, 0), (0, 64)):
                    nc.scalar.activation(KH[r:r + 64, g % 2, 2 * pr + e, 512 * hf:512 * hf + 512],
                                         PS[r:r + 64, jobbank(g, j), :], ACT.Copy,
                                         scale=1.0 / WS)\
                        .then_inc(s_ahi, 1)

            def whi(j):
                m, c, k = WJOBS[j]
                act.wait_ge(s_aux, 16 * G + j + 1)
                if j == 0:
                    act.wait_ge(s_sc, U * (G - 1))
                if m < 2:
                    nc.scalar.activation((WG, WU)[m][0][:, k, 512 * c:512 * c + 512], bank(7),
                                         ACT.Copy).then_inc(s_ahi, 1)
                else:
                    h, n0 = c // 2, 8 * (c % 2) + 4 * k
                    nc.scalar.activation(WD[0][:, n0:n0 + 4, 128 * h:128 * h + 128],
                                         bank(7).rearrange("p (n c) -> p n c", n=4), ACT.Copy)\
                        .then_inc(s_ahi, 1)

            def exps(n):
                i = n % U
                w = width(i // HG)
                act.wait_ge(s_nb, n + 1)
                last = n - i + after(i)
                if last >= 0:
                    act.wait_ge(s_tp, banks_before(last + 1))
                nc.scalar.activation(slot(pr, n), slot(ps, n), ACT.Exp,
                                     bias=nb[:, n % 8:n % 8 + 1], scale=ESC).then_inc(s_ex, 1)

            def evac(n):
                g, i = divmod(n, U)
                sb_, h = divmod(i, HG)
                u = g * NB + sb_
                if h == 0 and u >= 2:
                    act.wait_ge(s_pv, u - 1)
                for q in range(nbanks(i)):
                    act.wait_ge(s_tp, banks_before(n) + q + 1)
                    k = min(4, sb_ + 1 - 4 * q)
                    nc.scalar.activation(PT[:, u % 2, h, 4 * q:4 * q + k, :],
                                         bank(4 + (banks_before(n) + q) % 2, 128 * k)
                                         .rearrange("p (b c) -> p b c", c=128), ACT.Copy)\
                        .then_inc(s_te, 1)

            khi(0, 0)
            khi(0, 4)
            for n in range(8):
                rope_copy(n)
            for m in SOON[-2] + SOON[-1]:
                exps(m)
            for g in range(G):
                for i in range(U):
                    n = g * U + i
                    evac(n)
                    for m in SOON[i]:
                        if g * U + m < G * U:
                            exps(g * U + m)
                    if i in JOBS[g] and QJOBS[JOBS[g][i][1]][2] == "K":
                        khi(*JOBS[g][i])
                    if g == 0 and 8 + i < len(KCOPIES):
                        rope_copy(8 + i)
                    if g == G - 1 and i in wjob_at:
                        whi(wjob_at.index(i))
            def tail(s):
                if 0 <= s - 1 < NB:
                    b = s - 1
                    act.wait_ge(t_b, b + 1)
                    if b >= 4:
                        act.wait_ge(t_c, b - 3)
                    nc.scalar.activation(AT[:, b % 4, :, :],
                                         bank(2 + b % 2, 256).rearrange("p (k t) -> p k t", k=2),
                                         ACT.Copy).then_inc(t_e, 1)
                if 0 <= s - 7 < NB:
                    b = s - 7
                    act.wait_ge(t_d, b + 1)
                    nc.scalar.activation(X2[:, 0, :, 128 * b:128 * b + 128],
                                         bank(6 + b % 2, 256).rearrange("p (k t) -> p k t", k=2),
                                         ACT.Copy, scale=XS).then_inc(t_hi, 1)
            def square(k):
                n = k % NT
                act.wait_ge(m_g, k + 1)
                if k >= 2:
                    act.wait_ge(m_in, k - 1)
                nc.scalar.activation(sq[:, k % 2, :], bank(k % 2), ACT.Square,
                                     scale=K3[:, n:n + 1]).then_inc(m_sq, 1)

            for s in range(HALF_DONE):
                tail(s)
            square(0)
            for k in range(2 * NT):
                n = k % NT
                act.wait_ge(m_in, k + 1)
                nc.scalar.activation(inn[:, k % 2, :], inn[:, k % 2, :], ACT.Tanh,
                                     scale=KT[:, n:n + 1]).then_inc(m_th, 1)
                if k + 1 < 2 * NT:
                    square(k + 1)
                act.wait_ge(m_it, k + 1)
                if k >= 3:
                    act.wait_ge(m_d, k - 2)
                nc.scalar.activation(IH[:, k % 3, 0, :], itr[:, k % 2, :], ACT.Copy)\
                    .then_inc(m_hi, 1)
                if HALF_DONE + k < TAIL:
                    tail(HALF_DONE + k)

        @block.tensor
        def _(pe):
            def split_mm(out_, lhs, rhs, start=True, stop=True, check=True):
                nc.tensor.matmul(out_, lhs[0], rhs[0], start=start, stop=False,
                                 skip_group_check=not check)
                nc.tensor.matmul(out_, lhs[0], rhs[1], start=False, stop=False,
                                 skip_group_check=not check)
                return nc.tensor.matmul(out_, lhs[1], rhs[0], start=False, stop=stop,
                                        skip_group_check=not check)

            pe.wait_ge(s_const, 9)
            for hf in range(2):
                pe.wait_ge(s_xn, 4 * hf + 4)
                for k in range(2):
                    for b in range(4):
                        mm = nc.tensor.transpose(PS[:, 2 * hf + k, 128 * b:128 * b + 128],
                                                 XN[:, 4 * hf + b, 128 * k:128 * k + 128],
                                                 ident[:, :])
                    mm.then_inc(s_xtp, 1)
            pe.wait_ge(ld_w, 48)
            setups = [(r_dq, 0), (r_dq, 1), (r_dkv, 0), (r_dkv, 1),
                      (KR2, 0), (KR2S, 0), (KR2, 1), (KR2S, 1)]
            for j, (w, hf) in enumerate(setups):
                pe.wait_ge(s_xt, 2 + 2 * hf)
                if j == 4:
                    pe.wait_ge(s_kr2, 8)
                    pe.wait_ge(s_sq, 6)
                    nc.tensor.matmul(bank(7, 6), ones[:, :], NF, start=True, stop=True)\
                        .then_inc(s_nsum, 1)
                if j == 7:
                    pe.wait_ge(s_st, 3)
                for k in range(2):
                    mm = nc.tensor.matmul(bank(SETUP_BANKS[j]), w[:, k, :],
                                          xT[:, k, 512 * hf:512 * hf + 512],
                                          start=(k == 0), stop=(k == 1))
                mm.then_inc(s_pj, 1)
            pe.wait_ge(s_phi, 2)
            for v in range(4):
                pe.wait_ge(s_plo, 4)
                for a in range(2):
                    b = 2 * v + a
                    mm = nc.tensor.matmul(PS[:, VALUE_BANKS[v], 256 * a:256 * a + 256],
                                          CKV[:, 128 * b:128 * b + 128],
                                          r_uv.rearrange("p h c -> p (h c)"),
                                          start=True, stop=True)
                mm.then_inc(s_vp, 1)

            def qjob(g, j):
                pr, hf, kind = QJOBS[j]
                n = aux_index(g, j)
                o = bank(jobbank(g, j))
                if n == 8:
                    pe.wait_ge(s_plo, 6)
                if n >= 9:
                    pe.wait_ge(s_afr, n)
                q, cols = 2 * g + pr, slice(512 * hf, 512 * hf + 512)
                xd = (XD[:, 0, cols], XD[:, 1, cols])
                if kind == "S":
                    mm = split_mm(o, (WSW[:, 0, q, :], WSW[:, 1, q, :]), xd)
                elif kind == "K":
                    mm = split_mm(o, (WUK[:, 0, q, :], WUK[:, 1, q, :]),
                                  (CK[:, 0, cols], CK[:, 1, cols]))
                else:
                    h = 2 * q + (kind == "B")
                    mm = split_mm(o, (WQ[:, 0, h, :], WQ[:, 1, h, :]), xd)
                mm.then_inc(s_aux, 1)

            def wjob(j):
                m, c, k = WJOBS[j]
                q = j // 2
                pe.wait_ge(s_afr, 16 * G + j)
                pe.wait_ge(s_deq, q + 1)
                for a in range(4):
                    if m < 2:
                        src = DQ[:, q % 2, 256 * a + 128 * k:256 * a + 128 * k + 128]
                    else:
                        src = DQ[:, q % 2, 128 * (4 * k + a):128 * (4 * k + a) + 128]
                    mm = nc.tensor.transpose(PS[:, 7, 128 * a:128 * a + 128], src, ident[:, :])
                mm.then_inc(s_aux, 1)

            def scores(n):
                g, i = divmod(n, U)
                sb_, h = divmod(i, HG)
                w = width(sb_)
                last = n - i + after(i)
                if last >= 0:
                    pe.wait_ge(s_ex, last + 1)
                if i in (0, 2):
                    pe.wait_ge(s_qhi, 8 * g + 2 + i)
                    pe.wait_ge(s_qlo, 8 * g + 2 + i)
                    pe.wait_ge(s_afr, 16 * g + 4 + 2 * i)
                if i == SMALL:
                    pe.wait_ge(s_qhi, 8 * (g + 1))
                    pe.wait_ge(s_qlo, 8 * (g + 1))
                    pe.wait_ge(s_afr, 16 * (g + 1))
                if n in (0, SMALL, U):
                    pe.wait_ge(s_krc, {0: 8, SMALL: 16, U: 32}[n])
                qs = [q[:, g % 2, h, 128 * sb_:128 * sb_ + 128] for q in (QH, QL)]
                for c in range((w + 511) // 512):
                    last = 512 * (c + 1) >= w
                    ks = [k[:, g % 2, h, 512 * c:min(w, 512 * c + 512)] for k in (KH, KL)]
                    o = slot(ps, n)[:, 512 * c:min(w, 512 * c + 512)]
                    mm = split_mm(o, qs, ks, stop=not last)
                    if last:
                        mm = nc.tensor.matmul(o[:, o.shape[1] - 128:o.shape[1]], identb[:, :],
                                              maskb[:, :], start=False, stop=True)
                mm.then_inc(s_sc, 1)

            def transp(n):
                g, i = divmod(n, U)
                sb_ = i // HG
                pe.wait_ge(s_ex, n + 1)
                for q in range(nbanks(i)):
                    k = banks_before(n) + q
                    if k >= 2:
                        pe.wait_ge(s_te, k - 1)
                    for a in range(min(4, sb_ + 1 - 4 * q)):
                        b = 4 * q + a
                        mm = nc.tensor.transpose(PS[:, 4 + k % 2, 128 * a:128 * a + 128],
                                                 slot(pr, n)[:, 128 * b:128 * b + 128],
                                                 ident[:, :])
                    mm.then_inc(s_tp, 1)

            def pv(g, sb_):
                u = g * NB + sb_
                pe.wait_ge(s_te, banks_before(g * U + HG * sb_ + HG))
                pe.wait_ge(s_ov, u + 1)
                for b in range(sb_ + 1):
                    for h in range(HG):
                        mm = nc.tensor.matmul(PS[32 * h:32 * h + DH + 1, 6, 0:128],
                                              V[:, b, HG * g + h, :], PT[:, u % 2, h, b, :],
                                              start=(b == 0), stop=(b == sb_),
                                              tile_position=(0, 32 * h))
                mm.then_inc(s_pv, 1)

            pe.wait_ge(s_ulo, 2)
            pe.wait_ge(s_wlo, 6)
            pe.wait_ge(s_plo, 5)
            pe.wait_ge(s_const, 12)
            for j in range(8):
                if j == 1:
                    pe.wait_ge(s_vs, 4)
                if j == 3:
                    pe.wait_ge(s_wsw, 8)
                if j >= 6:
                    pe.wait_ge(s_afr, j - 3)
                qjob(0, j)
            for m in LEAD[-2] + LEAD[-1]:
                scores(m)
            for g in range(G):
                for i in range(U):
                    n = g * U + i
                    transp(n)
                    for m in LEAD[i]:
                        if g * U + m < G * U:
                            scores(g * U + m)
                    if i in JOBS[g]:
                        qjob(*JOBS[g][i])
                    if g == G - 1 and i in wjob_at:
                        wjob(wjob_at.index(i))
                    if i % HG == 0 and i > 0:
                        pv(g, i // HG - 1)
                pv(g, NB - 1)

            pe.wait_ge(ld_wo, 16)
            pe.wait_ge(s_ex, G * U)
            pe.wait_ge(s_te, banks_before(G * U))
            pe.wait_ge(s_afr, 16 * G + 24)
            pe.wait_ge(s_ov, G * NB + 1)
            def tail(s):
                if s < NB:
                    b = s
                    if b >= 2:
                        pe.wait_ge(t_n, b - 1)
                    for g in range(G):
                        mm = nc.tensor.transpose(PS[:, b % 2, 128 * g:128 * g + 128],
                                                 OT[:, g, 128 * b:128 * b + 128], ident[:, :])
                    mm.then_inc(t_a, 1)
                if 0 <= s - 1 < NB:
                    b = s - 1
                    pe.wait_ge(t_n, b + 1)
                    if b >= 2:
                        pe.wait_ge(t_e, b - 1)
                    for k in range(2):
                        mm = nc.tensor.transpose(PS[:, 2 + b % 2, 128 * k:128 * k + 128],
                                                 AN[:, b % 4, 128 * k:128 * k + 128], ident[:, :])
                    mm.then_inc(t_b, 1)
                if 0 <= s - 2 < NB:
                    b = s - 2
                    pe.wait_ge(t_e, b + 1)
                    if b >= 2:
                        pe.wait_ge(t_y, b - 1)
                    for k in range(2):
                        mm = nc.tensor.matmul(bank(4 + b % 2, 256), AT[:, b % 4, k, :], WO[:, k, :],
                                              start=(k == 0), stop=(k == 1))
                    mm.then_inc(t_c, 1)
                if 0 <= s - 7 < NB:
                    b = s - 7
                    pe.wait_ge(t_xn, b + 1)
                    if b >= 2:
                        pe.wait_ge(t_lo, b - 1)
                    for k in range(2):
                        mm = nc.tensor.transpose(PS[:, 6 + b % 2, 128 * k:128 * k + 128],
                                                 XN2[:, b % 4, 128 * k:128 * k + 128], ident[:, :])
                    mm.then_inc(t_d, 1)

            for s in range(HALF_DONE):
                tail(s)

            def down(k):
                c, n = divmod(k, NT)
                pe.wait_ge(m_hi, k + 1)
                pe.wait_ge(m_lo, k + 1)
                for a in range(4):
                    o = PS[:, 4 + 2 * c + a // 2, 256 * (a % 2):256 * (a % 2) + 256]
                    lh = [IH[:, k % 3, s, 128 * a:128 * a + 128] for s in range(2)]
                    mm = split_mm(o, lh, [WD[s][:, n, :] for s in range(2)],
                                  start=(n == 0 and a % 2 == 0), stop=(n == NT - 1), check=False)
                mm.then_inc(m_d, 1)

            pe.wait_ge(t_lo, NB // 2)
            pe.wait_ge(t_y, NB)
            for k in range(2 * NT + 2):
                if k == NT:
                    pe.wait_ge(t_lo, NB)
                if k < 2 * NT:
                    c, n = divmod(k, NT)
                    xs = [[X2[:, s, kc, 512 * c:512 * c + 512] for s in range(2)]
                          for kc in range(2)]
                    for w, b0, done in ((WG, 0, m_g), (WU, 2, m_u)):
                        if k >= 2:
                            pe.wait_ge(m_h if b0 == 0 else m_it, k - 1)
                        for kc in range(2):
                            mm = split_mm(bank(b0 + k % 2),
                                          [w[s][:, kc, 128 * n:128 * n + 128] for s in range(2)],
                                          xs[kc], start=(kc == 0), stop=(kc == 1))
                        mm.then_inc(done, 1)
                if k >= 2:
                    down(k - 2)
                if HALF_DONE + k < TAIL:
                    tail(HALF_DONE + k)

        @block.vector
        def _(dve):
            chain = [0]

            def link(ins):
                chain[0] += 1
                ins.then_inc(s_v, 1)
                dve.wait_ge(s_v, chain[0])

            V_ = nc.vector
            for k in range(2):
                dve.wait_ge(ld_x[k], 16)
                for b in range(4 * k, 4 * k + 4):
                    i = V_.bn_stats(st6[:, b, :], X[:, b, :])
                link(i)
                for b in range(4 * k, 4 * k + 4):
                    i = V_.bn_aggr(mv[:, b, :], st6[:, b, :])
                link(i)
                V_.tensor_scalar(rs[:, 4 * k:4 * k + 4], mv[:, 4 * k:4 * k + 4, 1], EPS, None,
                                 ALU.add).then_inc(s_st, 1)
            for k in range(2):
                dve.wait_ge(s_pow, k + 1)
                for b in range(4 * k, 4 * k + 4):
                    V_.tensor_scalar(XN[:, b, :], X[:, b, :], mv[:, b, 0:1], rs[:, b:b + 1],
                                     ALU.subtract, ALU.mult).then_inc(s_xn, 1)
            dve.wait_ge(ld_w, 48)
            krp = r_kr.rearrange("p k (i a) -> p k a i", a=2)
            for e in range(2):
                for a in range(2):
                    o = 64 * e + 32 * a
                    V_.tensor_copy(KR2[:, :, o:o + 32], krp[:, :, a, :]).then_inc(s_kr2, 1)
                    V_.tensor_copy(KR2S[:, :, o:o + 32], krp[:, :, 1 - a, :]).then_inc(s_kr2, 1)
            dve.wait_ge(s_nsum, 1)
            link(V_.tensor_scalar(NF, bank(7, 6), 1e-20, None, ALU.max))
            link(V_.tensor_tensor(nrm[:, 3:4], nrm[:, 3:4], nrm[:, 4:5], ALU.add))
            V_.tensor_copy(nrm[:, 6:7], nrm[:, 3:4]).then_inc(s_st, 1)
            dve.wait_ge(s_pow, 3)
            n_dq, n_dkv, n_kr, n_q, n_uk = (nrm[:, 8 + i:9 + i] for i in (0, 1, 2, 3, 5))
            V_.tensor_scalar(tmp1, n_dkv, n_uk, None, ALU.mult)
            V_.reciprocal(nrm[:, 24:25], n_q)
            V_.reciprocal(nrm[:, 21:22], n_dq)
            link(V_.reciprocal(nrm[:, 22:23], n_dkv))
            V_.tensor_scalar(f_q, f_q, WS, None, ALU.mult)
            V_.tensor_scalar(f_dq, f_dq, XS, None, ALU.mult)
            V_.tensor_scalar(f_dkv, f_dkv, XS, None, ALU.mult)
            V_.tensor_scalar(tmp2, n_dq, n_q, None, ALU.mult)
            link(V_.tensor_tensor(DEN, tmp1, n_kr, ALU.add))
            V_.tensor_scalar(ESC, tmp2, DEN, DH ** -0.5 / XS ** 2, ALU.mult, ALU.mult)
            link(V_.reciprocal(rD, DEN))
            V_.tensor_scalar(NESC, ESC, -1.0, None, ALU.mult)
            V_.tensor_scalar(f_kr, rD, XS * WS, None, ALU.mult)
            V_.tensor_scalar(f_uk, rD, n_dkv, WS, ALU.mult, ALU.mult).then_inc(s_wf, 1)
            dve.wait_ge(s_wf, 1)

            def rope_key(hf):
                cols = slice(512 * hf, 512 * hf + 512)
                dve.wait_ge(s_pj, 6 + 2 * hf)
                if hf == 0:
                    dve.wait_ge(ld_rope, 64)
                a, b = DQ[:, 0, 0:512], DQ[:, 0, 512:1024]
                V_.scalar_tensor_tensor(out=b, in0=bank(SETUP_BANKS[5 + 2 * hf]), scalar=f_kr,
                                        in1=SS[:, cols], op0=ALU.mult, op1=ALU.mult)
                link(V_.scalar_tensor_tensor(out=a, in0=bank(SETUP_BANKS[4 + 2 * hf]), scalar=f_kr,
                                             in1=CF[:, cols], op0=ALU.mult, op1=ALU.mult))
                link(V_.tensor_tensor(a, a, b, ALU.add))
                hi, lo = (KRS[:, s, cols] for s in range(2))
                link(V_.tensor_copy(hi, a))
                V_.tensor_tensor(lo, a, hi, ALU.subtract).then_inc(s_plo, 1)

            for hf in range(2):
                cols = slice(512 * hf, 512 * hf + 512)
                for j, f in ((hf, f_dq), (2 + hf, f_dkv)):
                    dve.wait_ge(s_phi, 3 + 2 * hf + j // 2)
                    t = (XD, CK)[j // 2]
                    V_.scalar_tensor_tensor(out=t[:, 1, cols], in0=bank(SETUP_BANKS[j]), scalar=f,
                                            in1=t[:, 0, cols], op0=ALU.mult, op1=ALU.subtract)\
                        .then_inc(s_plo, 1)
                if hf == 0:
                    dve.wait_ge(s_uhi, 2)
                    for lo, hi, src in zip(UK_PARTS(1), UK_PARTS(0), UK_SRC):
                        V_.scalar_tensor_tensor(out=lo, in0=src, scalar=f_uk, in1=hi,
                                                op0=ALU.mult, op1=ALU.subtract).then_inc(s_ulo, 1)
                    dve.wait_ge(s_whi, 6)
                    for lo, hi, src in zip(Q_PARTS(1), Q_PARTS(0), Q_SRC):
                        V_.scalar_tensor_tensor(out=lo, in0=src, scalar=f_q, in1=hi,
                                                op0=ALU.mult, op1=ALU.subtract).then_inc(s_wlo, 1)
            rope_key(0)

            def qwork(g, j):
                pr, hf, kind = QJOBS[j]
                n, m = aux_index(g, j), 4 * g + j // 4
                cols = slice(512 * hf, 512 * hf + 512)
                dve.wait_ge(s_aux, n + 1)
                if kind == "K":
                    dve.wait_ge(s_ahi, 2 * (m + 1))
                    for e, r in ((1, 0), (0, 64)):
                        i = V_.scalar_tensor_tensor(
                            out=KL[r:r + 64, g % 2, 2 * pr + e, cols],
                            in0=PS[r:r + 64, jobbank(g, j), :],
                            scalar=1.0 / WS, in1=KH[r:r + 64, g % 2, 2 * pr + e, cols],
                            op0=ALU.mult, op1=ALU.subtract)
                    i.then_inc(s_afr, 1)
                    return
                k = "SAB".index(kind)
                if k == 1 and m >= 2:
                    dve.wait_ge(s_qlo, 2 * (m - 1))
                tab = (SS, CA, CB)[k]
                V_.tensor_tensor(STG[:, m % 2, k, :], bank(jobbank(g, j)), tab[:, cols], ALU.mult)\
                    .then_inc(s_afr, 1)

            def qhi(g, m):
                n = 4 * g + m
                hf, pr = divmod(m, 2)
                if g >= 2 and m == 0:
                    dve.wait_ge(s_sc, U * (g - 1))
                dve.wait_ge(s_rot, 2 * (n + 1))
                for e in range(2):
                    V_.tensor_copy(QH[:, g % 2, 2 * pr + e, 512 * hf:512 * hf + 512],
                                   STG[:, n % 2, 1 + e, :]).then_inc(s_qhi, 1)

            def maxima(n):
                i = n % U
                w = width(i // HG)
                dve.wait_ge(s_sc, n + 1)
                if n >= 8:
                    dve.wait_ge(s_ex, n - 7)
                V_.tensor_reduce(mx[:, n % 4:n % 4 + 1], slot(ps, n), AX.X, ALU.max)\
                    .then_inc(s_mx, 1)
                dve.wait_ge(s_mx, n + 1)
                V_.tensor_scalar(nb[:, n % 8:n % 8 + 1], mx[:, n % 4:n % 4 + 1], NESC, None,
                                 ALU.mult).then_inc(s_nb, 1)

            def take_out(u):
                g, sb_ = divmod(u, NB)
                dve.wait_ge(s_pv, u + 1)
                V_.tensor_copy(OT[:, g, 128 * sb_:128 * sb_ + 128], PS[:, 6, 0:128])\
                    .then_inc(s_ov, 1)

            def scale_maxima():
                dve.wait_ge(ld_s, 48)
                for m, dst in ((0, GM), (1, UM), (2, gx[:, 2:3])):
                    src = SG[:, m, :]
                    if m < 2:
                        src = src.rearrange("p (n b) -> p n b", b=8)
                    low = SM[:, 7, 0:dst.shape[1]]
                    link(V_.tensor_reduce(dst, src, AX.X, ALU.max))
                    link(V_.tensor_reduce(low, src, AX.X, ALU.min))
                    link(V_.scalar_tensor_tensor(out=dst, in0=low, scalar=-1.0, in1=dst,
                                                 op0=ALU.mult, op1=ALU.max))
                link(V_.tensor_scalar(SM[:, 0:2, :], SM[:, 0:2, :], 1e-6, None, ALU.max))
                link(V_.tensor_reduce(gx[:, 0:2], SM[:, 0:2, :], AX.X, ALU.max))
                V_.tensor_scalar(gx[:, 2:3], gx[:, 2:3], 1e-6, None, ALU.max).then_inc(s_sm, 1)

            def scale_factors():
                link(V_.reciprocal(SM[:, 2:4, :], SM[:, 0:2, :]))
                dve.wait_ge(s_gm, 1)
                link(V_.reciprocal(gx[:, 8:11], gx[:, 4:7]))
                for m in range(2):
                    sv = SG[:, m, :].rearrange("p (n b) -> p n b", b=8)
                    link(V_.scalar_tensor_tensor(
                        out=sv, in0=sv, scalar=FS * CODE,
                        in1=SM[:, 2 + m, :].unsqueeze(2).broadcast_to([128, NT, 8]),
                        op0=ALU.mult, op1=ALU.mult))
                link(V_.tensor_scalar(SG[:, 2, :], SG[:, 2, :], gx[:, 10:11], FS * CODE, ALU.mult,
                                      ALU.mult))
                link(V_.tensor_scalar(K3, GM, math.sqrt(G3) / (XS * FS), None, ALU.mult))
                link(V_.tensor_scalar(KT, GM, GC / (XS * FS), None, ALU.mult))
                link(V_.tensor_tensor(KI, GM, UM, ALU.mult))
                link(V_.tensor_scalar(tmp1, gx[:, 8:9], gx[:, 9:10], None, ALU.mult))
                link(V_.tensor_scalar(KI, KI, tmp1, 0.5 * IS / (XS * FS) ** 2, ALU.mult, ALU.mult))
                link(V_.tensor_scalar(tmp2, tmp1, gx[:, 10:11], IS * FS, ALU.mult, ALU.mult))
                V_.tensor_scalar(CEPS, tmp2, tmp2, EPS, ALU.mult, ALU.mult).then_inc(s_sf, 1)

            def spread(q):
                y, t = RAW[:, q % 2, :], BITS[:, :]
                dve.wait_ge(ld_raw[q % 2], 16 * (q // 2 + 1))
                link(V_.scalar_tensor_tensor(out=y, in0=y, scalar=12, in1=y,
                                             op0=ALU.logical_shift_left, op1=ALU.bitwise_or))
                if q >= 1:
                    dve.wait_ge(s_deq, q)
                link(V_.tensor_scalar(t, y, 0x00070007, 9, ALU.bitwise_and,
                                      ALU.logical_shift_left))
                link(V_.tensor_scalar(y, y, 0x00080008, 12, ALU.bitwise_and,
                                      ALU.logical_shift_left))
                V_.tensor_tensor(t, t, y, ALU.bitwise_or).then_inc(s_bits, 1)

            def wlo(j):
                m, c, k = WJOBS[j]
                dve.wait_ge(s_ahi, 8 * G + j + 1)
                if m < 2:
                    cols = slice(512 * c, 512 * c + 512)
                    w = (WG, WU)[m]
                    V_.tensor_tensor(w[1][:, k, cols], bank(7), w[0][:, k, cols], ALU.subtract)\
                        .then_inc(s_afr, 1)
                else:
                    h, n0 = c // 2, 8 * (c % 2) + 4 * k
                    V_.tensor_tensor(WD[1][:, n0:n0 + 4, 128 * h:128 * h + 128],
                                     bank(7).rearrange("p (n c) -> p n c", n=4),
                                     WD[0][:, n0:n0 + 4, 128 * h:128 * h + 128],
                                     ALU.subtract).then_inc(s_afr, 1)

            for j in range(4):
                qwork(0, j)
            qwork(0, 4)
            qwork(0, 5)
            qhi(0, 0)
            qwork(0, 6)
            qwork(0, 7)
            qhi(0, 1)
            for m in SOON[-2] + SOON[-1]:
                maxima(m)
            rope_key(1)
            dve.wait_ge(s_plo, 6)
            V_.memset(bank(6), 0.0).then_inc(s_ov, 1)
            for g in range(G):
                for i in range(U):
                    n = g * U + i
                    gj, ij = divmod(n - 1, U)
                    if n > 0 and ij in JOBS[gj]:
                        qwork(*JOBS[gj][ij])
                    if i in HIS[g]:
                        qhi(*HIS[g][i])
                    if g == G - 1 and i - 1 in wjob_at:
                        wlo(wjob_at.index(i - 1))
                    if (g, i) == (0, 13):
                        scale_maxima()
                    if (g, i) == (1, 20):
                        scale_factors()
                    for m in SOON[i]:
                        if g * U + m < G * U:
                            maxima(g * U + m)
                    if g == G - 1 and i in spread_at:
                        spread(spread_at.index(i))
                    if i % HG == 0 and i > 0:
                        take_out(g * NB + i // HG - 1)
                take_out(g * NB + NB - 1)

            def norm_stats(src, b, eps, done):
                link(V_.bn_stats(st6[:, b, :], src))
                link(V_.bn_aggr(mv[:, b, :], st6[:, b, :]))
                V_.tensor_scalar(rs[:, b:b + 1], mv[:, b, 1:2], eps, None, ALU.add)\
                    .then_inc(done, 1)

            def tail(s):
                if s < NB:
                    b = s
                    dve.wait_ge(t_a, b + 1)
                    t = bank(b % 2).rearrange("p (h c) -> p h c", c=32)
                    link(V_.reciprocal(rc[:, b % 2, :], t[:, :, DH]))
                    if b >= 4:
                        dve.wait_ge(t_b, b - 3)
                    V_.tensor_tensor(AN[:, b % 4, :].rearrange("p (h c) -> p h c", c=DH),
                                     t[:, :, 0:DH],
                                     rc[:, b % 2, :].unsqueeze(2).broadcast_to([128, H, DH]),
                                     ALU.mult).then_inc(t_n, 1)
                if 0 <= s - 3 < NB:
                    b = s - 3
                    dve.wait_ge(t_c, b + 1)
                    norm_stats(bank(4 + b % 2, 256), b, EPS, t_st)
                if 0 <= s - 4 < NB:
                    b = s - 4
                    dve.wait_ge(t_pw, t_count("pow1", b))
                    if b >= 4:
                        dve.wait_ge(t_x, b - 3)
                    V_.tensor_scalar(YB[:, b % 4, :], bank(4 + b % 2, 256), mv[:, b, 0:1],
                                     rs[:, b:b + 1], ALU.subtract, ALU.mult).then_inc(t_y, 1)
                if 0 <= s - 5 < NB:
                    b = s - 5
                    dve.wait_ge(t_x, b + 1)
                    dve.wait_ge(t_y, b + 1)
                    norm_stats(X[:, b, :], b, EPS, t_st)
                if 0 <= s - 6 < NB:
                    b = s - 6
                    dve.wait_ge(t_pw, t_count("pow2", b))
                    if b >= 4:
                        dve.wait_ge(t_d, b - 3)
                    V_.tensor_scalar(XN2[:, b % 4, :], X[:, b, :], mv[:, b, 0:1],
                                     rs[:, b:b + 1], ALU.subtract, ALU.mult).then_inc(t_xn, 1)
                if 0 <= s - 8 < NB:
                    b = s - 8
                    dve.wait_ge(t_hi, b + 1)
                    cols = slice(128 * b, 128 * b + 128)
                    V_.scalar_tensor_tensor(
                        out=X2[:, 1, :, cols],
                        in0=bank(6 + b % 2, 256).rearrange("p (k t) -> p k t", k=2), scalar=XS,
                        in1=X2[:, 0, :, cols], op0=ALU.mult, op1=ALU.subtract).then_inc(t_lo, 1)
            for s in range(HALF_DONE):
                tail(s)
            for k in range(2 * NT):
                n = k % NT
                dve.wait_ge(m_sq, k + 1)
                V_.scalar_tensor_tensor(out=inn[:, k % 2, :], in0=sq[:, k % 2, :], scalar=1.0,
                                        in1=bank(k % 2), op0=ALU.add, op1=ALU.mult)\
                    .then_inc(m_in, 1)
                dve.wait_ge(m_th, k + 1)
                V_.scalar_tensor_tensor(out=hg[:, k % 2, :], in0=inn[:, k % 2, :], scalar=1.0,
                                        in1=bank(k % 2), op0=ALU.add, op1=ALU.mult)\
                    .then_inc(m_h, 1)
                dve.wait_ge(m_h, k + 1)
                dve.wait_ge(m_u, k + 1)
                if k >= 2:
                    dve.wait_ge(m_lo, k - 1)
                V_.scalar_tensor_tensor(out=itr[:, k % 2, :], in0=hg[:, k % 2, :],
                                        scalar=KI[:, n:n + 1], in1=bank(2 + k % 2), op0=ALU.mult,
                                        op1=ALU.mult).then_inc(m_it, 1)
                if HALF_DONE + k < TAIL:
                    tail(HALF_DONE + k)
            for b in range(NB):
                o = PS[:, 4 + b // 2, 256 * (b % 2):256 * (b % 2) + 256]
                dve.wait_ge(m_d, NT * (b // 4 + 1))
                norm_stats(o, b, CEPS, t_st)
                dve.wait_ge(t_pw, 2 * NB + b + 1)
                if b >= 4:
                    dve.wait_ge(t_x, NB + b - 3)
                V_.tensor_scalar(YB[:, b % 4, :], o, mv[:, b, 0:1], rs[:, b:b + 1], ALU.subtract,
                                 ALU.mult).then_inc(t_y, 1)


_INS = ["L0_attn_x", "L0_attn_W_dkv", "L0_attn_W_dq", "L0_attn_W_kr", "L0_attn_W_qc", "L0_attn_W_qr",
        "L0_attn_W_uk", "L0_attn_W_uv", "L0_attn_W_o", "L0_ffn_gate_W_packed", "L0_ffn_gate_scales",
        "L0_ffn_up_W_packed", "L0_ffn_up_scales", "L0_ffn_down_W_packed", "L0_ffn_down_scales"]


def _rope_constants():
    half = DR // 2
    freqs = np.exp(np.arange(half, dtype=np.float32) * np.float32(-math.log(10000.0) / half))
    ang = (np.arange(T, dtype=np.float32)[None, :] * freqs[:, None].astype(np.float32))
    cos = (np.cos(ang.astype(np.float64)) / WS).astype(np.float32)
    sin = (np.sin(ang.astype(np.float64)) / WS).astype(np.float32)
    return np.concatenate([cos] * 4), np.concatenate([-sin, sin] * 2)


def kernel(**inputs):
    import numpy as _np
    import concourse.bacc as _bacc
    from concourse import mybir as _mybir
    from concourse.bass_utils import run_bass_kernel_spmd as _run

    nc = _bacc.Bacc("TRN2", target_bir_lowering=False, num_devices=1)
    arrays, args = {}, []
    cos, sin = _rope_constants()
    for name, a in [(n, inputs[n]) for n in _INS] + [("rope_cos", cos), ("rope_sin", sin)]:
        a = _np.ascontiguousarray(a)
        arrays[f"in_{name}_dram"] = a
        args.append(nc.dram_tensor(f"in_{name}_dram", a.shape, _mybir.dt.from_np(a.dtype),
                                   kind="ExternalInput").ap())
    out = nc.dram_tensor("out_0_dram", (1, T, E), F32, kind="ExternalOutput").ap()
    layer_kernel(nc, *args, out)
    r = _run(nc, [arrays], core_ids=[0])
    return r.results[0]["out_0_dram"]
```

```python
import math
from contextlib import ExitStack

import numpy as np

import concourse.bass as bass
from concourse import mybir

F32 = mybir.dt.float32
F16 = mybir.dt.float16
BF16 = mybir.dt.bfloat16
I32 = mybir.dt.int32
ALU = mybir.AluOpType
ACT = mybir.ActivationFunctionType
AX = mybir.AxisListType
RMAX = bass.bass_isa.ReduceOp.max

T, E = 1024, 256
H, DKV, DC, DR, DH = 16, 128, 64, 64, 16
F = 2048
QB = 32
NB = T // 128
NT = F // 128
HG = 4
G = H // HG
U = NB * HG
EPS = 1e-5
GC = 0.7978845608028654
G3 = 0.044715
XS = 2.0 ** 11
WS = 2.0 ** 14
FS = 2.0 ** 11
CODE = 2.0 ** 14
IS = 2.0 ** -6
MASK = -1e38


def layer_kernel(nc, x, w_dkv, w_dq, w_kr, w_qc, w_qr, w_uk, w_uv, w_o, gate_w, gate_s, up_w, up_s,
                 down_w, down_s, rope_cos, rope_sin, out):
    with ExitStack() as ctx:
        def sb(name, shape, dt=F32):
            return ctx.enter_context(nc.sbuf_tensor(name, shape, dt))

        def sem(name):
            return ctx.enter_context(nc.semaphore(name))

        X = sb("X", [128, NB, E])
        XD = sb("XD", [128, 2, T], F16)
        CK = sb("CK", [128, 2, T], F16)
        WP = sb("WP", [128, 8192], F16)
        CA = sb("CA", [128, T])
        CB = sb("CB", [128, T])
        SS = sb("SS", [128, T])
        V = sb("V", [128, NB, H, DH + 1])
        QH = sb("QH", [128, 2, HG, T], F16)
        QL = sb("QL", [128, 2, HG, T], F16)
        KH = sb("KH", [128, 2, HG, T], F16)
        KL = sb("KL", [128, 2, HG, T], F16)
        PR = sb("PR", [128, 4, 512])
        PT = sb("PT", [128, 2, HG, NB, 128])
        OT = sb("OT", [128, G, T])
        STG = sb("STG", [128, 2, 3, 512])
        WO = sb("WO", [128, 2, E])
        RAW = sb("RAW", [128, 3, 512], I32)
        BITS = sb("BITS", [128, 512], I32)
        DQ = sb("DQ", [128, 2, 1024])
        ident = sb("ident", [128, 128])
        identb = sb("identb", [128, 128], BF16)
        maskb = sb("maskb", [128, 128], BF16)
        ones = sb("ones", [128, 128])
        st6 = sb("st6", [128, NB, 6])
        mv = sb("mv", [128, NB, 2])
        rs = sb("rs", [128, NB])
        powc = sb("powc", [128, 2, 8])
        nrm = sb("nrm", [128, 32])
        mx = sb("mx", [128, 8])
        nb = sb("nb", [128, 8])
        SG = sb("SG", [128, 3, NT * 8])
        SM = sb("SM", [128, 8, NT])
        gx = sb("gx", [128, 16])
        rc = sb("rc", [128, 2, H])
        PS = ctx.enter_context(nc.psum_tensor("PS", [128, 8, 512], F32))

        pt = PT[:, :, :, :, :].rearrange("p a h b c -> p (a h b c)")
        xT = pt[:, 0:2048].rearrange("p (k t) -> p k t", k=2)
        CKV = pt[:, 2048:3072]
        r_qc = pt[:, 3072:4096].rearrange("p (h c) -> p h c", h=H)
        r_qr = pt[:, 4096:5120].rearrange("p (h c) -> p h c", h=H)
        r_uk = pt[:, 5120:6144].rearrange("p (h c) -> p h c", h=H)
        CF = pt[:, 6144:7168]
        r_dq = pt[:, 7168:7424].rearrange("p (k m) -> p k m", k=2)
        r_dkv = pt[:, 7424:7680].rearrange("p (k m) -> p k m", k=2)
        r_kr = pt[:, 7680:7808].rearrange("p (k m) -> p k m", k=2)
        ot = OT[:, :, :].rearrange("p g t -> p (g t)")
        r_uv = ot[:, 3072:3328].rearrange("p (h c) -> p h c", h=H)
        KR2 = ot[:, 3328:3584].rearrange("p (k m) -> p k m", k=2)
        KR2S = ot[:, 3584:3840].rearrange("p (k m) -> p k m", k=2)
        XN = PR[:, :, :].rearrange("p a (b c) -> p (a b) c", c=E)
        pr = PR[:, :, :].rearrange("p a c -> p (a c)")
        junk = STG[:, :, :, :].rearrange("p a b c -> p (a b c)")
        CODES = [OT[:, G - 1, 512 * a:512 * a + 512].bitcast(I32) for a in range(2)] +\
            [RAW[:, a, :] for a in range(3)]
        KRS = DQ[:, 1, :].bitcast(F16).rearrange("p (s t) -> p s t", s=2)
        WQ = WP[:, 0:4096].rearrange("p (s h c) -> p s h c", s=2, h=H)
        WSW = WP[:, 4096:6144].rearrange("p (s q c) -> p s q c", s=2, q=H // 2)
        WUK = WP[:, 6144:8192].rearrange("p (s q c) -> p s q c", s=2, q=H // 2)
        WG = [q[:, 0, :, :].rearrange("p h t -> p (h t)").rearrange("p (k n) -> p k n", k=2)
              for q in (QH, QL)]
        WU = [q[:, 0, :, :].rearrange("p h t -> p (h t)").rearrange("p (k n) -> p k n", k=2)
              for q in (KH, KL)]
        WD = [WP[:, 4096 * s:4096 * (s + 1)].rearrange("p (n h) -> p n h", n=NT) for s in range(2)]
        sq = pt[:, 2048:3072].rearrange("p (a t) -> p a t", a=2)
        inn = pt[:, 3072:4096].rearrange("p (a t) -> p a t", a=2)
        hg = pt[:, 4096:5120].rearrange("p (a t) -> p a t", a=2)
        itr = pt[:, 5120:6144].rearrange("p (a t) -> p a t", a=2)
        IH = pt[:, 6144:7680].bitcast(F16).rearrange("p (a s t) -> p a s t", a=3, s=2)
        X2 = [t[:, :].bitcast(F16).rearrange("p (k t) -> p k t", k=2) for t in (CB, SS)]
        YB = CA[:, :].rearrange("p (a c) -> p a c", a=4)
        AN = junk[:, 0:1024].rearrange("p (a c) -> p a c", a=4)
        XN2 = junk[:, 1024:2048].rearrange("p (a c) -> p a c", a=4)
        AT = junk[:, 2048:3072].rearrange("p (a k t) -> p a k t", a=4, k=2)
        NF, NR = nrm[:, 0:6], nrm[:, 8:14]
        DEN, rD, ESC, NESC, CEPS = (nrm[:, i:i + 1] for i in (16, 17, 18, 19, 20))
        f_dq, f_dkv, f_kr, f_q, f_uk = (nrm[:, i:i + 1] for i in range(21, 26))
        tmp1, tmp2, tmp3 = (nrm[:, i:i + 1] for i in (27, 28, 29))
        GM, UM, GI, UI, K3, KT, KI = (SM[:, i, :] for i in range(7))

        ld_x = [sem("ld_x0"), sem("ld_x1")]
        ld_w, ld_h, ld_qc, ld_qr, ld_rope, ld_wo, ld_s = (sem(s) for s in (
            "ld_w", "ld_h", "ld_qc", "ld_qr", "ld_rope", "ld_wo", "ld_s"))
        ld_raw = [sem(f"ld_raw{a}") for a in range(5)]
        s_const = sem("s_const")
        s_sq = sem("s_sq")
        s_nsum = sem("s_nsum")
        s_v = sem("s_v")
        s_pow = sem("s_pow")
        s_st = sem("s_st")
        s_xn = sem("s_xn")
        s_xtp = sem("s_xtp")
        s_xt = sem("s_xt")
        s_wf = sem("s_wf")
        s_whi = sem("s_whi")
        s_wlo = sem("s_wlo")
        s_uhi = sem("s_uhi")
        s_ulo = sem("s_ulo")
        s_krc = sem("s_krc")
        s_kr2 = sem("s_kr2")
        s_wsw = sem("s_wsw")
        s_pj = sem("s_pj")
        s_phi = sem("s_phi")
        s_plo = sem("s_plo")
        s_vp = sem("s_vp")
        s_vs = sem("s_vs")
        s_sc = sem("s_sc")
        s_nb = sem("s_nb")
        s_mx = sem("s_mx")
        s_ex = sem("s_ex")
        s_tp = sem("s_tp")
        s_te = sem("s_te")
        s_pv = sem("s_pv")
        s_ov = sem("s_ov")
        s_aux = sem("s_aux")
        s_afr = sem("s_afr")
        s_ahi = sem("s_ahi")
        s_rot = sem("s_rot")
        s_qhi = sem("s_qhi")
        s_qlo = sem("s_qlo")
        s_qd = sem("s_qd")
        s_bits = sem("s_bits")
        s_deq = sem("s_deq")
        s_sm = sem("s_sm")
        s_gm = sem("s_gm")
        s_sf = sem("s_sf")
        t_a, t_b, t_c, t_d = (sem(s) for s in ("t_a", "t_b", "t_c", "t_d"))
        t_n = sem("t_n")
        t_e = sem("t_e")
        t_st = sem("t_st")
        t_pw = sem("t_pw")
        t_y = sem("t_y")
        t_x = sem("t_x")
        t_xn = sem("t_xn")
        t_hi = sem("t_hi")
        t_lo = sem("t_lo")
        m_g, m_u, m_d = sem("m_g"), sem("m_u"), sem("m_d")
        m_sq, m_in, m_th, m_h, m_it, m_hi, m_lo = (sem(s) for s in (
            "m_sq", "m_in", "m_th", "m_h", "m_it", "m_hi", "m_lo"))
        s_out = sem("s_out")

        ps = PS[:, :, :].rearrange("p b c -> p (b c)")

        def bank(b, w=512):
            return PS[:, b, 0:w]

        def width(sb_):
            return (sb_ + 1) * 128

        def nbanks(i):
            return i // HG // 4 + 1

        def banks_before(n):
            g, i = divmod(n, U)
            return g * sum(nbanks(k) for k in range(U)) + sum(nbanks(k) for k in range(i))

        SMALL = U // 2

        def after(i):
            if i < HG:
                return -2 + i // 2
            if i < SMALL:
                return i - HG
            return {SMALL: SMALL - 3, SMALL + 1: SMALL - 1}.get(i, i - 2)

        def slot(base, n):
            i = n % U
            w, a = width(i // HG), (i % HG if i < SMALL else 2 * (i % 2))
            return base[:, 512 * a:512 * a + w]

        LEAD = {i: [m for m in range(U + HG) if (after(m % U) + (m // U) * U) == i]
                for i in range(-2, U)}
        SOON = {i: [m for m in range(U + HG)
                    if max(after(m % U) + (m // U) * U, m - 2) == i] for i in range(-2, U)}

        QJOBS = [(pr, hf, kind) for hf in range(2) for pr in range(HG // 2) for kind in "KABS"]
        CHUNKS = [(m, c) for m in range(2) for c in range(4)] + [(2, c) for c in range(4)]
        WJOBS = [(m, c, k) for m, c in CHUNKS for k in range(2)]
        BESIDE = list(range(14, 30))
        JOB_STEPS = [[2, *range(4, 11), *BESIDE], BESIDE, BESIDE, []]
        HI_STEPS = [[8, 12, 21, 26, 29], [3, 21, 27, 29], [3, 22, 26, 30], [4]]
        WJOB_STEPS = [2, 3, *range(6, 24), 26, 27, 28, 30]
        SPREAD_STEPS = [(1, 22), (1, 27), (2, 2), (2, 4), (2, 11)] +\
            [(G - 1, i) for i in (7, 10, 12, 14, 16, 18, 22)]
        SCALE_STEPS = [(0, 13), (1, 10)]
        ROPE_STEP = 1
        PV_STEP, OUT_STEP = 2, 3
        JOB_AT = dict(zip([(g, i) for g in range(G) for i in JOB_STEPS[g]],
                          [divmod(n, 16) for n in range(8, 16 * G)]))
        HI_AT = dict(zip([(g, i) for g in range(G) for i in HI_STEPS[g]],
                         [divmod(n, 4) for n in range(2, 4 * G)]))
        WJOB_AT = {(G - 1, i): j for j, i in enumerate(WJOB_STEPS)}

        def chunk_slot(q):
            return (q, 0) if q < 5 else (2 + (q - 2) % 3, (q - 2) // 3)

        def aux_index(g, j):
            return 16 * g + j

        def by_pool(n):
            return n - min(2, max(0, n - 2))

        def jobbank(g, j):
            return FIRST_BANKS[j] if (g, j) < (0, 8) else 7

        HALF = NB // 2
        HALF_DONE = U
        TAIL_STEPS = {"heads": [11, 15, 19, 23], "back": [12, 16, 20, 24],
                      "project": [13, 17, 21, 25], "stats": [13, 17, 21, 25],
                      "norm": [14, 18, 22, 26], "stats2": [15, 21, 23, 28],
                      "norm2": [16, 22, 24, 30], "columns": [17, 23, 25, 31],
                      "split": [17, 23, 25, 31]}
        assert all(at % HG != PV_STEP for st in ("heads", "back", "project")
                   for at in TAIL_STEPS[st])
        assert all((TAIL_STEPS["norm"][b] - PV_STEP - 1) // HG ==
                   (TAIL_STEPS["heads"][b] - PV_STEP - 1) // HG for b in range(HALF))
        TAIL_AT = {(st, b): at[b] for st, at in TAIL_STEPS.items() for b in range(HALF)}
        for b in range(HALF):
            for st, first, pace in (("heads", 0, 2), ("back", 1, 2), ("project", 2, 2),
                                    ("stats", 2, 2), ("norm", 3, 2), ("stats2", 4, 2),
                                    ("norm2", 5, 2), ("columns", 10, 1), ("split", 11, 1)):
                TAIL_AT[st, HALF + b] = HALF_DONE + first + pace * b
            TAIL_AT["stats3", b] = HALF_DONE + NT + 3 + 2 * b
            TAIL_AT["norm3", b] = HALF_DONE + NT + 4 + 2 * b
        TAIL_DO = {}
        for (st, b), step in TAIL_AT.items():
            TAIL_DO[st, step] = b
        LAST = [(st, c) for b in range(HALF, NB + 1) for st, c in (("stats3", b), ("norm3", b - 1))
                if HALF <= c < NB]
        STATS = [(st, TAIL_DO[st, step]) for step in range(HALF_DONE + 2 * NT)
                 for st in ("stats", "stats2", "stats3") if (st, step) in TAIL_DO] +\
            [x for x in LAST if x[0] == "stats3"]
        assert max(TAIL_AT.values()) < HALF_DONE + 2 * NT
        assert all(TAIL_AT["split", b] < HALF_DONE + NT for b in range(NB))

        def tail_out(st, b, w=256):
            if b < HALF:
                return bank(7 if st == "columns" else 6, w)
            return bank({"heads": 6, "back": 6, "project": 7, "columns": 6 + b % 2}[st], w)

        AUX_LAST = []
        for i in range(HALF_DONE):
            AUX_LAST += [(st, TAIL_DO[st, i]) for st in ("columns",)
                         if (st, i) in TAIL_DO]
            AUX_LAST += [("weights", WJOB_AT[G - 1, i])] if (G - 1, i) in WJOB_AT else []

        def outs_before(i):
            return len([k for k in range(i) if k >= HG and k % HG == PV_STEP])

        SETUP_BANKS = [4, 5, 3, 0, 1, 2, 6, 7]
        VALUE_BANKS = [1, 2, 5, 3]
        FIRST_BANKS = [3, 4, 1, 2, 5, 0, 3, 4]

        def Q_PARTS(s):
            wq = WQ[:, s, :, :].rearrange("p (q e) c -> p q e c", e=2)
            return [wq[:, :, e, 64 * e + a:64 * e + a + 32] for e in range(2) for a in (0, 32)] +\
                [wq[:, :, e, 64 - 64 * e:128 - 64 * e] for e in range(2)]

        qr_v = r_qr.rearrange("p (q e) (i a) -> p q e a i", e=2, a=2)
        qc_v = r_qc.rearrange("p (q e) c -> p q e c", e=2)
        Q_SRC = [qr_v[:, :, e, a, :] for e in range(2) for a in range(2)] +\
            [qc_v[:, :, e, :] for e in range(2)]

        def UK_PARTS(s):
            return [WUK[:, s, :, 64 - 64 * e:128 - 64 * e] for e in range(2)]

        uk_v = r_uk.rearrange("p (q e) c -> p q e c", e=2)
        UK_SRC = [uk_v[:, :, e, :] for e in range(2)]
        KCOPIES = [(buf, hf, e, q, s) for buf in range(2) for hf in range(2) for q in range(2)
                   for e in range(2) for s in range(2)]

        def t_count(st, b):
            return STATS.index((st, b)) + 1

        block = ctx.enter_context(nc.Block())

        @block.sync
        def _(sp):
            xv = x.rearrange("o (b p) e -> p (o b) e", p=128)
            for k in range(2):
                sp.dma_start(X[:, 4 * k:4 * k + 4, :], xv[:, 4 * k:4 * k + 4, :])\
                    .then_inc(ld_x[k], 16)
            sp.dma_start(r_kr, w_kr.rearrange("(k p) m -> p k m", p=128)).then_inc(ld_w, 16)
            sp.dma_start(r_uk, w_uk.rearrange("h p c -> p h c")).then_inc(ld_h, 16)
            sp.dma_start(r_uv, w_uv.rearrange("h p c -> p h c")).then_inc(ld_h, 16)
            sp.dma_start(CF, rope_cos[:, :]).then_inc(ld_rope, 16)
            sp.dma_start(SS[:, :], rope_sin[:, :]).then_inc(ld_rope, 16)
            sp.dma_start(CA[0:64, :], rope_cos[0:64, :]).then_inc(ld_rope, 16)
            sp.dma_start(CB[64:128, :], rope_cos[64:128, :]).then_inc(ld_rope, 16)
            sp.dma_start(WO[:, :, :], w_o.rearrange("(k p) e -> p k e", p=128)).then_inc(ld_wo, 16)
            for i, s in enumerate((gate_s, up_s)):
                sp.dma_start(SG[:, i, :].rearrange("p (n b) -> p n b", b=8),
                             s.rearrange("(n p) b -> p n b", p=128)).then_inc(ld_s, 16)
            sp.dma_start(SG[:, 2, :].rearrange("p (h b) -> p h b", h=2),
                         down_s.rearrange("(h p) b -> p h b", p=128)).then_inc(ld_s, 16)
            gw = gate_w.rearrange("(n p) w -> p n w", p=128)
            uw = up_w.rearrange("(n p) w -> p n w", p=128)
            dw = down_w.rearrange("(h p) w -> p h w", p=128)
            sp.wait_ge(s_vp, 4)
            for q, (m, c) in enumerate(CHUNKS):
                a, before = chunk_slot(q)
                if q >= 5:
                    sp.wait_ge(s_deq, q - 2)
                if m < 2:
                    sp.dma_start(CODES[a].rearrange("p (n w) -> p n w", n=4),
                                 (gw, uw)[m][:, 4 * c:4 * c + 4, :]).then_inc(ld_raw[a], 16)
                else:
                    sp.dma_start(CODES[a], dw[:, c // 2, 512 * (c % 2):512 * (c % 2 + 1)])\
                        .then_inc(ld_raw[a], 16)
            for b in range(NB):
                sp.wait_ge(t_x, NB + b + 1)
                sp.dma_start(out.rearrange("o (b p) e -> p (o b) e", p=128)[:, b, :],
                             X[:, b, :]).then_inc(s_out, 16)
            sp.wait_ge(s_out, 16 * NB)

        @block.gpsimd
        def _(pool):
            nc.gpsimd.memset(ones[:, :], 1.0).then_inc(s_const, 1)
            nc.gpsimd.memset(powc[:, 0, :], -0.5).then_inc(s_const, 1)
            nc.gpsimd.memset(powc[:, 1, :], 0.5).then_inc(s_const, 1)
            nc.gpsimd.memset(ident[:, :], 0.0).then_inc(s_const, 1)
            nc.gpsimd.memset(identb[:, :], 0.0).then_inc(s_const, 1)
            nc.gpsimd.memset(maskb[:, :], 0.0).then_inc(s_const, 1)
            pool.wait_ge(s_const, 6)
            nc.gpsimd.affine_select(out=ident[:, :], in_=ident[:, :], compare_op=ALU.not_equal,
                                    fill=1.0, base=0, pattern=[[-1, 128]],
                                    channel_multiplier=1).then_inc(s_const, 1)
            nc.gpsimd.affine_select(out=identb[:, :], in_=identb[:, :], compare_op=ALU.not_equal,
                                    fill=1.0, base=0, pattern=[[-1, 128]],
                                    channel_multiplier=1).then_inc(s_const, 1)
            nc.gpsimd.affine_select(out=maskb[:, :], in_=maskb[:, :], compare_op=ALU.is_ge,
                                    fill=MASK, base=0, pattern=[[-1, 128]],
                                    channel_multiplier=1).then_inc(s_const, 1)
            for k in range(2):
                pool.wait_ge(s_st, k + 1)
                nc.gpsimd.tensor_tensor(rs[:, 4 * k:4 * k + 4], rs[:, 4 * k:4 * k + 4],
                                        powc[:, 0, 0:4], ALU.pow).then_inc(s_pow, 1)
            pool.wait_ge(s_st, 3)
            nc.gpsimd.tensor_tensor(NR, NF, powc[:, 1, 0:6], ALU.pow).then_inc(s_pow, 1)
            pool.wait_ge(s_pow, 3)
            nc.gpsimd.memset(CA[64:128, :], 1.0 / WS).then_inc(s_const, 1)
            pool.wait_ge(s_const, 10)
            nc.gpsimd.memset(CB[0:64, :], 1.0 / WS).then_inc(s_const, 1)
            pool.wait_ge(s_const, 11)
            nc.gpsimd.memset(V[:, :, :, DH:DH + 1], 1.0).then_inc(s_const, 1)
            for s in range(2):
                wq = WQ[:, s, :, :].rearrange("p (q e) c -> p q e c", e=2)
                for e in range(2):
                    o = 64 * e
                    pool.wait_ge((s_whi, s_wlo)[s], 2 * (e + 1))
                    for a in range(2):
                        nc.gpsimd.tensor_copy(
                            WSW[:, s, :, o + 32 * a:o + 32 * a + 32],
                            wq[:, :, e, o + 32 * (1 - a):o + 32 * (1 - a) + 32]).then_inc(s_wsw, 1)

            def rotate(g, m):
                n = 4 * g + m
                hf, pr = divmod(m, 2)
                pool.wait_ge(s_afr, 4 * n + 4)
                w, a, b = (STG[:, n % 2, k, :] for k in range(3))
                if n == 0:
                    pool.wait_ge(s_wsw, 8)
                else:
                    pool.wait_ge(s_qlo, by_pool(2 * n))
                nc.gpsimd.tensor_tensor(a[0:64, :], a[0:64, :], w[0:64, :], ALU.add)\
                    .then_inc(s_rot, 1)
                pool.wait_ge(s_rot, by_pool(2 * n) + 1)
                nc.gpsimd.tensor_tensor(b[64:128, :], b[64:128, :], w[64:128, :], ALU.add)\
                    .then_inc(s_rot, 1)
                pool.wait_ge(s_qhi, 2 * (n + 1))
                for e in range(2):
                    dst = QL[:, g % 2, 2 * pr + e, 512 * hf:512 * hf + 512]
                    if e == 0 and g >= 2 and m == 0:
                        pool.wait_ge(s_sc, U * (g - 1))
                    nc.gpsimd.tensor_tensor(dst, STG[:, n % 2, 1 + e, :],
                                            QH[:, g % 2, 2 * pr + e, 512 * hf:512 * hf + 512],
                                            ALU.subtract).then_inc(s_qlo, 1)

            def dequant(q):
                m, c = CHUNKS[q]
                pool.wait_ge(s_bits, q + 1)
                if q == 0:
                    pool.wait_ge(s_sf, 1)
                if q == 1:
                    pool.wait_ge(s_krc, len(KCOPIES))
                if q >= 2:
                    pool.wait_ge(s_aux, 16 * G + 2 * (q - 1))
                codes = CODES[chunk_slot(q)[0]].bitcast(F16).rearrange("p (b k) -> p b k", k=QB)
                if m < 2:
                    sc = SG[:, m, 32 * c:32 * c + 32]
                else:
                    sc = SG[:, 2, 64 * (c // 2) + 32 * (c % 2):64 * (c // 2) + 32 * (c % 2) + 32]
                nc.gpsimd.tensor_tensor(DQ[:, q % 2, :].rearrange("p (b k) -> p b k", k=QB), codes,
                                        sc.unsqueeze(2).broadcast_to([128, 32, QB]),
                                        ALU.mult).then_inc(s_deq, 1)

            for m in (0, 2, 3):
                rotate(0, m)
            pool.wait_ge(s_sm, 1)
            nc.gpsimd.partition_all_reduce(gx[:, 4:7], gx[:, 0:3], 128, RMAX).then_inc(s_gm, 1)
            for n in range(4, 4 * G):
                if n == 4 * (G - 1):
                    dequant(0)
                    dequant(1)
                rotate(n // 4, n % 4)
            def rstd(st, b):
                pool.wait_ge(t_st, t_count(st, b))
                nc.gpsimd.tensor_tensor(rs[:, b:b + 1], rs[:, b:b + 1], powc[:, 0, 0:1],
                                        ALU.pow).then_inc(t_pw, 1)

            def residual(b, n):
                pool.wait_ge(t_y, n + 1)
                nc.gpsimd.tensor_tensor(X[:, b, :], X[:, b, :], YB[:, b % 4, :], ALU.add)\
                    .then_inc(t_x, 1)

            def tail(s):
                if ("norm", s) in TAIL_DO:
                    residual(TAIL_DO["norm", s], TAIL_DO["norm", s])
                if ("norm3", s) in TAIL_DO:
                    residual(TAIL_DO["norm3", s], NB + TAIL_DO["norm3", s])
                for st in ("stats", "stats2", "stats3"):
                    if (st, s) in TAIL_DO:
                        rstd(st, TAIL_DO[st, s])

            for s in range(HALF_DONE):
                for q in range(2, len(CHUNKS)):
                    if s == WJOB_STEPS[2 * q - 3]:
                        dequant(q)
                tail(s)
            for k in range(2 * NT):
                pool.wait_ge(m_hi, k + 1)
                if k >= 3:
                    pool.wait_ge(m_d, k - 2)
                nc.gpsimd.tensor_tensor(IH[:, k % 3, 1, :], itr[:, k % 2, :], IH[:, k % 3, 0, :],
                                        ALU.subtract).then_inc(m_lo, 1)
                tail(HALF_DONE + k)
            for st, b in LAST:
                if st == "stats3":
                    rstd(st, b)
                else:
                    residual(b, NB + b)

        @block.scalar
        def _(act):
            act.dma_start(r_dq, w_dq.rearrange("(k p) m -> p k m", p=128)).then_inc(ld_w, 16)
            act.dma_start(r_dkv, w_dkv.rearrange("(k p) m -> p k m", p=128)).then_inc(ld_w, 16)
            act.dma_start(r_qc, w_qc.rearrange("h p c -> p h c")).then_inc(ld_qc, 16)
            act.dma_start(r_qr, w_qr.rearrange("h p c -> p h c")).then_inc(ld_qr, 16)

            def square_sum(i, w):
                n = w.shape[1] * w.shape[2]
                nc.scalar.activation(junk[:, 0:n].rearrange("p (a b) -> p a b", a=w.shape[1]), w,
                                     ACT.Square, accum_out=nrm[:, i:i + 1]).then_inc(s_sq, 1)
                act.wait_ge(s_sq, i + 1)

            act.wait_ge(ld_w, 48)
            for i, w in enumerate((r_dq, r_dkv, r_kr)):
                square_sum(i, w)
            for b in range(4):
                act.wait_ge(s_xtp, b + 1)
                hf, k = divmod(b, 2)
                nc.scalar.activation(xT[:, k, 512 * hf:512 * hf + 512], bank(b), ACT.Copy)\
                    .then_inc(s_xt, 1)
            for i, (w, ld, n) in enumerate(((r_qc, ld_qc, 16), (r_qr, ld_qr, 16),
                                            (r_uk, ld_h, 32))):
                act.wait_ge(ld, n)
                square_sum(3 + i, w)
            for hf in range(2):
                act.wait_ge(s_pj, 3 + hf)
                nc.scalar.activation(CKV[:, 512 * hf:512 * hf + 512], bank(SETUP_BANKS[2 + hf]),
                                     ACT.Copy).then_inc(s_phi, 1)
            act.wait_ge(s_wf, 1)

            def latent_hi(hf):
                for j, f in ((hf, f_dq), (2 + hf, f_dkv)):
                    nc.scalar.activation((XD, CK)[j // 2][:, 0, 512 * hf:512 * hf + 512],
                                         bank(SETUP_BANKS[j]), ACT.Copy, scale=f)\
                        .then_inc(s_phi, 1)

            latent_hi(0)
            for dst, src in zip(UK_PARTS(0), UK_SRC):
                nc.scalar.activation(dst, src, ACT.Copy, scale=f_uk).then_inc(s_uhi, 1)
            for dst, src in zip(Q_PARTS(0), Q_SRC):
                nc.scalar.activation(dst, src, ACT.Copy, scale=f_q).then_inc(s_whi, 1)
            latent_hi(1)
            def rope_copy(n):
                buf, hf, e, q, s = KCOPIES[n]
                act.wait_ge(s_plo, (3, 6)[hf])
                r, cols = slice(64 * e, 64 * e + 64), slice(512 * hf, 512 * hf + 512)
                nc.scalar.activation((KH, KL)[s][r, buf, 2 * q + e, cols], KRS[r, s, cols],
                                     ACT.Copy).then_inc(s_krc, 1)

            def khi(g, j):
                pr, hf, _ = QJOBS[j]
                act.wait_ge(s_aux, aux_index(g, j) + 1)
                if g >= 2 and j == 0:
                    act.wait_ge(s_sc, U * (g - 1))
                for e, r in ((1, 0), (0, 64)):
                    nc.scalar.activation(KH[r:r + 64, g % 2, 2 * pr + e, 512 * hf:512 * hf + 512],
                                         PS[r:r + 64, jobbank(g, j), :], ACT.Copy,
                                         scale=1.0 / WS)\
                        .then_inc(s_ahi, 1)

            def whi(j):
                m, c, k = WJOBS[j]
                act.wait_ge(s_aux, 16 * G + j + 1)
                if j == 0:
                    act.wait_ge(s_sc, U * (G - 1))
                if m < 2:
                    nc.scalar.activation((WG, WU)[m][0][:, k, 512 * c:512 * c + 512], bank(7),
                                         ACT.Copy).then_inc(s_ahi, 1)
                else:
                    h, n0 = c // 2, 8 * (c % 2) + 4 * k
                    nc.scalar.activation(WD[0][:, n0:n0 + 4, 128 * h:128 * h + 128],
                                         bank(7).rearrange("p (n c) -> p n c", n=4), ACT.Copy)\
                        .then_inc(s_ahi, 1)

            def exps(n):
                i = n % U
                w = width(i // HG)
                act.wait_ge(s_nb, n + 1)
                last = n - i + after(i)
                if last >= 0:
                    act.wait_ge(s_tp, banks_before(last + 1))
                nc.scalar.activation(slot(pr, n), slot(ps, n), ACT.Exp,
                                     bias=nb[:, n % 8:n % 8 + 1], scale=ESC).then_inc(s_ex, 1)

            def evac(n):
                g, i = divmod(n, U)
                sb_, h = divmod(i, HG)
                u = g * NB + sb_
                if h == 0 and u >= 2:
                    act.wait_ge(s_pv, u - 1)
                for q in range(nbanks(i)):
                    act.wait_ge(s_tp, banks_before(n) + q + 1)
                    k = min(4, sb_ + 1 - 4 * q)
                    nc.scalar.activation(PT[:, u % 2, h, 4 * q:4 * q + k, :],
                                         bank(4 + (banks_before(n) + q) % 2, 128 * k)
                                         .rearrange("p (b c) -> p b c", c=128), ACT.Copy)\
                        .then_inc(s_te, 1)

            def tail(s):
                if ("back", s) in TAIL_DO:
                    b = TAIL_DO["back", s]
                    act.wait_ge(t_b, b + 1)
                    if b >= 4:
                        act.wait_ge(t_c, b - 3)
                    nc.scalar.activation(AT[:, b % 4, :, :],
                                         tail_out("back", b)
                                         .rearrange("p (k t) -> p k t", k=2),
                                         ACT.Copy).then_inc(t_e, 1)
                if ("columns", s) in TAIL_DO:
                    b = TAIL_DO["columns", s]
                    act.wait_ge(t_d, b + 1)
                    nc.scalar.activation(X2[0][:, :, 128 * b:128 * b + 128],
                                         tail_out("columns", b)
                                         .rearrange("p (k t) -> p k t", k=2),
                                         ACT.Copy, scale=XS).then_inc(t_hi, 1)
            khi(0, 0)
            for n in range(8):
                rope_copy(n)
            khi(0, 4)
            for v in range(4):
                act.wait_ge(s_vp, v + 1)
                nc.scalar.activation(V[:, 2 * v:2 * v + 2, :, 0:DH],
                                     bank(VALUE_BANKS[v]).rearrange("p (b h c) -> p b h c", b=2,
                                                                    h=H), ACT.Copy)\
                    .then_inc(s_vs, 1)
            for m in SOON[-2] + SOON[-1]:
                exps(m)
            for g in range(G):
                for i in range(U):
                    n = g * U + i
                    evac(n)
                    if g == G - 1:
                        tail(i)
                    for m in SOON[i]:
                        if g * U + m < G * U:
                            exps(g * U + m)
                    if (g, i) in JOB_AT and QJOBS[JOB_AT[g, i][1]][2] == "K":
                        khi(*JOB_AT[g, i])
                    if 0 < n - ROPE_STEP <= len(KCOPIES) - 8:
                        rope_copy(7 + n - ROPE_STEP)
                    if (g, i) in WJOB_AT:
                        whi(WJOB_AT[g, i])
            def square(k):
                n = k % NT
                act.wait_ge(m_g, k + 1)
                if k >= 2:
                    act.wait_ge(m_in, k - 1)
                nc.scalar.activation(sq[:, k % 2, :], bank(k % 2), ACT.Square,
                                     scale=K3[:, n:n + 1]).then_inc(m_sq, 1)

            for s in range(U, HALF_DONE):
                tail(s)
            square(0)
            for k in range(2 * NT):
                n = k % NT
                act.wait_ge(m_in, k + 1)
                nc.scalar.activation(inn[:, k % 2, :], inn[:, k % 2, :], ACT.Tanh,
                                     scale=KT[:, n:n + 1]).then_inc(m_th, 1)
                if k + 1 < 2 * NT:
                    square(k + 1)
                act.wait_ge(m_it, k + 1)
                if k >= 3:
                    act.wait_ge(m_d, k - 2)
                nc.scalar.activation(IH[:, k % 3, 0, :], itr[:, k % 2, :], ACT.Copy)\
                    .then_inc(m_hi, 1)
                tail(HALF_DONE + k)

        @block.tensor
        def _(pe):
            def split_mm(out_, lhs, rhs, start=True, stop=True, check=True):
                nc.tensor.matmul(out_, lhs[0], rhs[0], start=start, stop=False,
                                 skip_group_check=not check)
                nc.tensor.matmul(out_, lhs[0], rhs[1], start=False, stop=False,
                                 skip_group_check=not check)
                return nc.tensor.matmul(out_, lhs[1], rhs[0], start=False, stop=stop,
                                        skip_group_check=not check)

            pe.wait_ge(s_const, 9)
            for hf in range(2):
                pe.wait_ge(s_xn, 4 * hf + 4)
                for k in range(2):
                    for b in range(4):
                        mm = nc.tensor.transpose(PS[:, 2 * hf + k, 128 * b:128 * b + 128],
                                                 XN[:, 4 * hf + b, 128 * k:128 * k + 128],
                                                 ident[:, :])
                    mm.then_inc(s_xtp, 1)
            pe.wait_ge(ld_w, 48)
            setups = [(r_dq, 0), (r_dq, 1), (r_dkv, 0), (r_dkv, 1),
                      (KR2, 0), (KR2S, 0), (KR2, 1), (KR2S, 1)]
            for j, (w, hf) in enumerate(setups):
                pe.wait_ge(s_xt, 2 + 2 * hf)
                if j == 4:
                    pe.wait_ge(s_kr2, 8)
                    pe.wait_ge(s_sq, 6)
                    nc.tensor.matmul(bank(7, 6), ones[:, :], NF, start=True, stop=True)\
                        .then_inc(s_nsum, 1)
                if j == 7:
                    pe.wait_ge(s_st, 3)
                for k in range(2):
                    mm = nc.tensor.matmul(bank(SETUP_BANKS[j]), w[:, k, :],
                                          xT[:, k, 512 * hf:512 * hf + 512],
                                          start=(k == 0), stop=(k == 1))
                mm.then_inc(s_pj, 1)
            def qjob(g, j):
                pr, hf, kind = QJOBS[j]
                n = aux_index(g, j)
                o = bank(jobbank(g, j))
                if n == 8:
                    pe.wait_ge(s_plo, 6)
                if n >= 9:
                    pe.wait_ge(s_afr, n)
                q, cols = 2 * g + pr, slice(512 * hf, 512 * hf + 512)
                xd = (XD[:, 0, cols], XD[:, 1, cols])
                if kind == "S":
                    mm = split_mm(o, (WSW[:, 0, q, :], WSW[:, 1, q, :]), xd)
                elif kind == "K":
                    mm = split_mm(o, (WUK[:, 0, q, :], WUK[:, 1, q, :]),
                                  (CK[:, 0, cols], CK[:, 1, cols]))
                else:
                    h = 2 * q + (kind == "B")
                    mm = split_mm(o, (WQ[:, 0, h, :], WQ[:, 1, h, :]), xd)
                mm.then_inc(s_aux, 1)

            def wjob(j):
                m, c, k = WJOBS[j]
                q = j // 2
                aux_read(("weights", j))
                pe.wait_ge(s_deq, q + 1)
                for a in range(4):
                    if m < 2:
                        src = DQ[:, q % 2, 256 * a + 128 * k:256 * a + 128 * k + 128]
                    else:
                        src = DQ[:, q % 2, 128 * (4 * k + a):128 * (4 * k + a) + 128]
                    mm = nc.tensor.transpose(PS[:, 7, 128 * a:128 * a + 128], src, ident[:, :])
                mm.then_inc(s_aux, 1)

            def scores(n):
                g, i = divmod(n, U)
                sb_, h = divmod(i, HG)
                w = width(sb_)
                last = n - i + after(i)
                if last >= 0:
                    pe.wait_ge(s_ex, last + 1)
                if i < HG:
                    pe.wait_ge(s_qhi, 8 * g + 2 * (i // 2) + 2)
                    if g == 0 and i >= 2:
                        pe.wait_ge(s_qd, i - 1)
                    else:
                        pe.wait_ge(s_qlo, by_pool(8 * g + i + 1))
                    pe.wait_ge(s_afr, 16 * g + 4 + 4 * (i // 2))
                if g == 0 and 1 <= i < HG:
                    pe.wait_ge(s_vs, (1, 2, 4)[i - 1])
                if i == SMALL:
                    pe.wait_ge(s_qhi, 8 * (g + 1))
                    pe.wait_ge(s_qlo, by_pool(8 * (g + 1)))
                    pe.wait_ge(s_afr, 16 * (g + 1))
                if n in (0, SMALL, U):
                    pe.wait_ge(s_krc, {0: 8, SMALL: 16, U: 32}[n])
                qs = [q[:, g % 2, h, 128 * sb_:128 * sb_ + 128] for q in (QH, QL)]
                for c in range((w + 511) // 512):
                    last = 512 * (c + 1) >= w
                    ks = [k[:, g % 2, h, 512 * c:min(w, 512 * c + 512)] for k in (KH, KL)]
                    o = slot(ps, n)[:, 512 * c:min(w, 512 * c + 512)]
                    mm = split_mm(o, qs, ks, stop=not last)
                    if last:
                        mm = nc.tensor.matmul(o[:, o.shape[1] - 128:o.shape[1]], identb[:, :],
                                              maskb[:, :], start=False, stop=True)
                mm.then_inc(s_sc, 1)

            def transp(n):
                g, i = divmod(n, U)
                sb_ = i // HG
                pe.wait_ge(s_ex, n + 1)
                for q in range(nbanks(i)):
                    k = banks_before(n) + q
                    if k >= 2:
                        pe.wait_ge(s_te, k - 1)
                    for a in range(min(4, sb_ + 1 - 4 * q)):
                        b = 4 * q + a
                        mm = nc.tensor.transpose(PS[:, 4 + k % 2, 128 * a:128 * a + 128],
                                                 slot(pr, n)[:, 128 * b:128 * b + 128],
                                                 ident[:, :])
                    mm.then_inc(s_tp, 1)

            def pv(g, sb_):
                u = g * NB + sb_
                pe.wait_ge(s_te, banks_before(g * U + HG * sb_ + HG))
                pe.wait_ge(s_ov, u + 1)
                now = U if u == G * NB - 1 else HG * (sb_ + 1) + PV_STEP
                projects = [b for b in range(HALF) if TAIL_AT["project", b] < now]
                if g == G - 1 and projects:
                    pe.wait_ge(t_y, len(projects))
                for b in range(sb_ + 1):
                    for h in range(HG):
                        mm = nc.tensor.matmul(PS[32 * h:32 * h + DH + 1, 6, 0:128],
                                              V[:, b, HG * g + h, :], PT[:, u % 2, h, b, :],
                                              start=(b == 0), stop=(b == sb_),
                                              tile_position=(0, 32 * h))
                mm.then_inc(s_pv, 1)

            def aux_read(job):
                n = AUX_LAST.index(job)
                st, b = AUX_LAST[n - 1] if n else ("weights", -1)
                pe.wait_ge({"weights": s_afr, "columns": t_lo}[st],
                           b + 1 + (16 * G if st == "weights" else 0))

            def tail(s):
                if ("heads", s) in TAIL_DO:
                    b = TAIL_DO["heads", s]
                    if b < HALF:
                        pe.wait_ge(s_ov, (G - 1) * NB + outs_before(s) + 1)
                    else:
                        pe.wait_ge(s_ov, G * NB + 1)
                        pe.wait_ge(t_e, b)
                    for g in range(G):
                        mm = nc.tensor.transpose(tail_out("heads", b, 512)
                                                 [:, 128 * g:128 * g + 128],
                                                 OT[:, g, 128 * b:128 * b + 128], ident[:, :])
                    mm.then_inc(t_a, 1)
                if ("back", s) in TAIL_DO:
                    b = TAIL_DO["back", s]
                    pe.wait_ge(t_n, b + 1)
                    for k in range(2):
                        mm = nc.tensor.transpose(tail_out("back", b)[:, 128 * k:128 * k + 128],
                                                 AN[:, b % 4, 128 * k:128 * k + 128], ident[:, :])
                    mm.then_inc(t_b, 1)
                if ("project", s) in TAIL_DO:
                    b = TAIL_DO["project", s]
                    if b == 0:
                        pe.wait_ge(ld_wo, 16)
                    else:
                        pe.wait_ge(t_y, b)
                    pe.wait_ge(t_e, b + 1)
                    for k in range(2):
                        mm = nc.tensor.matmul(tail_out("project", b), AT[:, b % 4, k, :],
                                              WO[:, k, :], start=(k == 0), stop=(k == 1))
                    mm.then_inc(t_c, 1)
                if ("columns", s) in TAIL_DO:
                    b = TAIL_DO["columns", s]
                    if b < HALF:
                        aux_read(("columns", b))
                    else:
                        pe.wait_ge(t_y, NB)
                        pe.wait_ge(t_lo, b - 1)
                    pe.wait_ge(t_xn, b + 1)
                    for k in range(2):
                        mm = nc.tensor.transpose(tail_out("columns", b)[:, 128 * k:128 * k + 128],
                                                 XN2[:, b % 4, 128 * k:128 * k + 128], ident[:, :])
                    mm.then_inc(t_d, 1)

            pe.wait_ge(s_ulo, 2)
            pe.wait_ge(s_plo, 2)
            pe.wait_ge(s_const, 12)
            for j in range(8):
                if j == 1:
                    pe.wait_ge(s_wlo, 6)
                if j == 3:
                    pe.wait_ge(s_wsw, 8)
                if 2 <= j < 6:
                    pe.wait_ge(s_plo, (3, 3, 4, 5)[j - 2])
                if j >= 6:
                    pe.wait_ge(s_afr, j - 5)
                qjob(0, j)
            pe.wait_ge(s_phi, 2)
            for v in range(4):
                pe.wait_ge(s_afr, (3, 4, 5, 7)[v])
                for a in range(2):
                    b = 2 * v + a
                    mm = nc.tensor.matmul(PS[:, VALUE_BANKS[v], 256 * a:256 * a + 256],
                                          CKV[:, 128 * b:128 * b + 128],
                                          r_uv.rearrange("p h c -> p (h c)"),
                                          start=True, stop=True)
                mm.then_inc(s_vp, 1)
            for m in LEAD[-2] + LEAD[-1]:
                scores(m)
            for g in range(G):
                for i in range(U):
                    n = g * U + i
                    transp(n)
                    for m in LEAD[i]:
                        if g * U + m < G * U:
                            scores(g * U + m)
                    if g == G - 1:
                        tail(i)
                    if (g, i) in JOB_AT:
                        qjob(*JOB_AT[g, i])
                    if (g, i) in WJOB_AT:
                        wjob(WJOB_AT[g, i])
                    if n >= HG and i % HG == PV_STEP:
                        pv(*divmod(n // HG - 1, NB))
            pv(G - 1, NB - 1)

            pe.wait_ge(s_ex, G * U)
            pe.wait_ge(s_te, banks_before(G * U))
            for s in range(U, HALF_DONE):
                tail(s)

            def down(k):
                c, n = divmod(k, NT)
                pe.wait_ge(m_hi, k + 1)
                pe.wait_ge(m_lo, k + 1)
                for a in range(4):
                    o = PS[:, 4 + 2 * c + a // 2, 256 * (a % 2):256 * (a % 2) + 256]
                    lh = [IH[:, k % 3, s, 128 * a:128 * a + 128] for s in range(2)]
                    mm = split_mm(o, lh, [WD[s][:, n, :] for s in range(2)],
                                  start=(n == 0 and a % 2 == 0), stop=(n == NT - 1), check=False)
                mm.then_inc(m_d, 1)

            pe.wait_ge(t_lo, HALF)
            for k in range(2 * NT + 2):
                if k == NT:
                    pe.wait_ge(t_lo, NB)
                if k < 2 * NT:
                    c, n = divmod(k, NT)
                    xs = [[X2[s][:, kc, 512 * c:512 * c + 512] for s in range(2)]
                          for kc in range(2)]
                    for w, b0, done in ((WG, 0, m_g), (WU, 2, m_u)):
                        if k >= 2:
                            pe.wait_ge(m_h if b0 == 0 else m_it, k - 1)
                        for kc in range(2):
                            mm = split_mm(bank(b0 + k % 2),
                                          [w[s][:, kc, 128 * n:128 * n + 128] for s in range(2)],
                                          xs[kc], start=(kc == 0), stop=(kc == 1))
                        mm.then_inc(done, 1)
                if k >= 2:
                    down(k - 2)
                tail(HALF_DONE + k)

        @block.vector
        def _(dve):
            chain = [0]

            def link(ins):
                chain[0] += 1
                ins.then_inc(s_v, 1)
                dve.wait_ge(s_v, chain[0])

            V_ = nc.vector
            for k in range(2):
                dve.wait_ge(ld_x[k], 16)
                for b in range(4 * k, 4 * k + 4):
                    i = V_.bn_stats(st6[:, b, :], X[:, b, :])
                link(i)
                for b in range(4 * k, 4 * k + 4):
                    i = V_.bn_aggr(mv[:, b, :], st6[:, b, :])
                link(i)
                V_.tensor_scalar(rs[:, 4 * k:4 * k + 4], mv[:, 4 * k:4 * k + 4, 1], EPS, None,
                                 ALU.add).then_inc(s_st, 1)
            for k in range(2):
                dve.wait_ge(s_pow, k + 1)
                for b in range(4 * k, 4 * k + 4):
                    V_.tensor_scalar(XN[:, b, :], X[:, b, :], mv[:, b, 0:1], rs[:, b:b + 1],
                                     ALU.subtract, ALU.mult).then_inc(s_xn, 1)
            dve.wait_ge(ld_w, 48)
            krp = r_kr.rearrange("p k (i a) -> p k a i", a=2)
            for e in range(2):
                for a in range(2):
                    o = 64 * e + 32 * a
                    V_.tensor_copy(KR2[:, :, o:o + 32], krp[:, :, a, :]).then_inc(s_kr2, 1)
                    V_.tensor_copy(KR2S[:, :, o:o + 32], krp[:, :, 1 - a, :]).then_inc(s_kr2, 1)
            dve.wait_ge(s_nsum, 1)
            link(V_.tensor_scalar(NF, bank(7, 6), 1e-20, None, ALU.max))
            link(V_.tensor_tensor(nrm[:, 3:4], nrm[:, 3:4], nrm[:, 4:5], ALU.add))
            V_.tensor_copy(nrm[:, 6:7], nrm[:, 3:4]).then_inc(s_st, 1)
            dve.wait_ge(s_pow, 3)
            n_dq, n_dkv, n_kr, n_q, n_uk = (nrm[:, 8 + i:9 + i] for i in (0, 1, 2, 3, 5))
            V_.tensor_scalar(tmp1, n_dkv, n_uk, None, ALU.mult)
            V_.reciprocal(nrm[:, 24:25], n_q)
            V_.reciprocal(nrm[:, 21:22], n_dq)
            link(V_.reciprocal(nrm[:, 22:23], n_dkv))
            V_.tensor_scalar(f_q, f_q, WS, None, ALU.mult)
            V_.tensor_scalar(f_dq, f_dq, XS, None, ALU.mult)
            V_.tensor_scalar(f_dkv, f_dkv, XS, None, ALU.mult)
            V_.tensor_scalar(tmp2, n_dq, n_q, None, ALU.mult)
            link(V_.tensor_tensor(DEN, tmp1, n_kr, ALU.add))
            V_.tensor_scalar(ESC, tmp2, DEN, DH ** -0.5 / XS ** 2, ALU.mult, ALU.mult)
            link(V_.reciprocal(rD, DEN))
            V_.tensor_scalar(NESC, ESC, -1.0, None, ALU.mult)
            V_.tensor_scalar(f_kr, rD, XS * WS, None, ALU.mult)
            V_.tensor_scalar(f_uk, rD, n_dkv, WS, ALU.mult, ALU.mult).then_inc(s_wf, 1)
            dve.wait_ge(s_wf, 1)

            def rope_key(hf):
                cols = slice(512 * hf, 512 * hf + 512)
                dve.wait_ge(s_pj, 6 + 2 * hf)
                if hf == 0:
                    dve.wait_ge(ld_rope, 64)
                a, b = DQ[:, 0, 0:512], DQ[:, 0, 512:1024]
                V_.scalar_tensor_tensor(out=b, in0=bank(SETUP_BANKS[5 + 2 * hf]), scalar=f_kr,
                                        in1=SS[:, cols], op0=ALU.mult, op1=ALU.mult)
                link(V_.scalar_tensor_tensor(out=a, in0=bank(SETUP_BANKS[4 + 2 * hf]), scalar=f_kr,
                                             in1=CF[:, cols], op0=ALU.mult, op1=ALU.mult))
                link(V_.tensor_tensor(a, a, b, ALU.add))
                hi, lo = (KRS[:, s, cols] for s in range(2))
                link(V_.tensor_copy(hi, a))
                V_.tensor_tensor(lo, a, hi, ALU.subtract).then_inc(s_plo, 1)

            def latent_lo(hf):
                cols = slice(512 * hf, 512 * hf + 512)
                for j, f in ((hf, f_dq), (2 + hf, f_dkv)):
                    dve.wait_ge(s_phi, 3 + 2 * hf + j // 2)
                    t = (XD, CK)[j // 2]
                    V_.scalar_tensor_tensor(out=t[:, 1, cols], in0=bank(SETUP_BANKS[j]), scalar=f,
                                            in1=t[:, 0, cols], op0=ALU.mult, op1=ALU.subtract)\
                        .then_inc(s_plo, 1)

            latent_lo(0)
            dve.wait_ge(s_uhi, 2)
            for lo, hi, src in zip(UK_PARTS(1), UK_PARTS(0), UK_SRC):
                V_.scalar_tensor_tensor(out=lo, in0=src, scalar=f_uk, in1=hi,
                                        op0=ALU.mult, op1=ALU.subtract).then_inc(s_ulo, 1)
            for n, (lo, hi, src) in enumerate(zip(Q_PARTS(1), Q_PARTS(0), Q_SRC)):
                dve.wait_ge(s_whi, n + 1)
                V_.scalar_tensor_tensor(out=lo, in0=src, scalar=f_q, in1=hi,
                                        op0=ALU.mult, op1=ALU.subtract).then_inc(s_wlo, 1)
            rope_key(0)

            def qwork(g, j):
                pr, hf, kind = QJOBS[j]
                n, m = aux_index(g, j), 4 * g + j // 4
                cols = slice(512 * hf, 512 * hf + 512)
                dve.wait_ge(s_aux, n + 1)
                if kind == "K":
                    dve.wait_ge(s_ahi, 2 * (m + 1))
                    for e, r in ((1, 0), (0, 64)):
                        i = V_.scalar_tensor_tensor(
                            out=KL[r:r + 64, g % 2, 2 * pr + e, cols],
                            in0=PS[r:r + 64, jobbank(g, j), :],
                            scalar=1.0 / WS, in1=KH[r:r + 64, g % 2, 2 * pr + e, cols],
                            op0=ALU.mult, op1=ALU.subtract)
                    i.then_inc(s_afr, 1)
                    return
                k = "SAB".index(kind)
                if k == 1 and m >= 2:
                    dve.wait_ge(s_qlo, by_pool(2 * (m - 1)))
                tab = (SS, CA, CB)[k]
                V_.tensor_tensor(STG[:, m % 2, k, :], bank(jobbank(g, j)), tab[:, cols], ALU.mult)\
                    .then_inc(s_afr, 1)

            def qhi(g, m):
                n = 4 * g + m
                hf, pr = divmod(m, 2)
                if g >= 2 and m == 0:
                    dve.wait_ge(s_sc, U * (g - 1))
                dve.wait_ge(s_rot, by_pool(2 * (n + 1)))
                for e in range(2):
                    V_.tensor_copy(QH[:, g % 2, 2 * pr + e, 512 * hf:512 * hf + 512],
                                   STG[:, n % 2, 1 + e, :]).then_inc(s_qhi, 1)

            def maxima(n):
                i = n % U
                w = width(i // HG)
                dve.wait_ge(s_sc, n + 1)
                if n >= 8:
                    dve.wait_ge(s_ex, n - 7)
                V_.tensor_reduce(mx[:, n % 4:n % 4 + 1], slot(ps, n), AX.X, ALU.max)\
                    .then_inc(s_mx, 1)
                dve.wait_ge(s_mx, n + 1)
                V_.tensor_scalar(nb[:, n % 8:n % 8 + 1], mx[:, n % 4:n % 4 + 1], NESC, None,
                                 ALU.mult).then_inc(s_nb, 1)

            def take_out(u):
                g, sb_ = divmod(u, NB)
                dve.wait_ge(s_pv, u + 1)
                V_.tensor_copy(OT[:, g, 128 * sb_:128 * sb_ + 128], PS[:, 6, 0:128])\
                    .then_inc(s_ov, 1)

            def scale_maxima():
                dve.wait_ge(ld_s, 48)
                for m, dst in ((0, GM), (1, UM), (2, gx[:, 2:3])):
                    src = SG[:, m, :]
                    if m < 2:
                        src = src.rearrange("p (n b) -> p n b", b=8)
                    low = SM[:, 7, 0:dst.shape[1]]
                    link(V_.tensor_reduce(dst, src, AX.X, ALU.max))
                    link(V_.tensor_reduce(low, src, AX.X, ALU.min))
                    link(V_.scalar_tensor_tensor(out=dst, in0=low, scalar=-1.0, in1=dst,
                                                 op0=ALU.mult, op1=ALU.max))
                link(V_.tensor_scalar(SM[:, 0:2, :], SM[:, 0:2, :], 1e-6, None, ALU.max))
                link(V_.tensor_reduce(gx[:, 0:2], SM[:, 0:2, :], AX.X, ALU.max))
                V_.tensor_scalar(gx[:, 2:3], gx[:, 2:3], 1e-6, None, ALU.max).then_inc(s_sm, 1)

            def scale_factors():
                link(V_.reciprocal(SM[:, 2:4, :], SM[:, 0:2, :]))
                dve.wait_ge(s_gm, 1)
                link(V_.reciprocal(gx[:, 8:11], gx[:, 4:7]))
                for m in range(2):
                    sv = SG[:, m, :].rearrange("p (n b) -> p n b", b=8)
                    link(V_.scalar_tensor_tensor(
                        out=sv, in0=sv, scalar=FS * CODE,
                        in1=SM[:, 2 + m, :].unsqueeze(2).broadcast_to([128, NT, 8]),
                        op0=ALU.mult, op1=ALU.mult))
                link(V_.tensor_scalar(SG[:, 2, :], SG[:, 2, :], gx[:, 10:11], FS * CODE, ALU.mult,
                                      ALU.mult))
                link(V_.tensor_scalar(K3, GM, math.sqrt(G3) / (XS * FS), None, ALU.mult))
                link(V_.tensor_scalar(KT, GM, GC / (XS * FS), None, ALU.mult))
                link(V_.tensor_tensor(KI, GM, UM, ALU.mult))
                link(V_.tensor_scalar(tmp1, gx[:, 8:9], gx[:, 9:10], None, ALU.mult))
                link(V_.tensor_scalar(KI, KI, tmp1, 0.5 * IS / (XS * FS) ** 2, ALU.mult, ALU.mult))
                link(V_.tensor_scalar(tmp2, tmp1, gx[:, 10:11], IS * FS, ALU.mult, ALU.mult))
                V_.tensor_scalar(CEPS, tmp2, tmp2, EPS, ALU.mult, ALU.mult).then_inc(s_sf, 1)

            def spread(q, part):
                a, before = chunk_slot(q)
                y, t = CODES[a], BITS[:, :]
                if part == 0:
                    dve.wait_ge(ld_raw[a], 16 * (before + 1))
                    link(V_.scalar_tensor_tensor(out=y, in0=y, scalar=12, in1=y,
                                                 op0=ALU.logical_shift_left, op1=ALU.bitwise_or))
                    if q >= 1:
                        dve.wait_ge(s_bits, q)
                    link(V_.tensor_scalar(t, y, 0x00070007, 9, ALU.bitwise_and,
                                          ALU.logical_shift_left))
                else:
                    link(V_.tensor_scalar(y, y, 0x00080008, 12, ALU.bitwise_and,
                                          ALU.logical_shift_left))
                    V_.tensor_tensor(y, t, y, ALU.bitwise_or).then_inc(s_bits, 1)

            def wlo(j):
                m, c, k = WJOBS[j]
                dve.wait_ge(s_ahi, 8 * G + j + 1)
                if m < 2:
                    cols = slice(512 * c, 512 * c + 512)
                    w = (WG, WU)[m]
                    V_.tensor_tensor(w[1][:, k, cols], bank(7), w[0][:, k, cols], ALU.subtract)\
                        .then_inc(s_afr, 1)
                else:
                    h, n0 = c // 2, 8 * (c % 2) + 4 * k
                    V_.tensor_tensor(WD[1][:, n0:n0 + 4, 128 * h:128 * h + 128],
                                     bank(7).rearrange("p (n c) -> p n c", n=4),
                                     WD[0][:, n0:n0 + 4, 128 * h:128 * h + 128],
                                     ALU.subtract).then_inc(s_afr, 1)

            def norm_stats(src, b, eps, done):
                link(V_.bn_stats(st6[:, b, :], src))
                link(V_.bn_aggr(mv[:, b, :], st6[:, b, :]))
                V_.tensor_scalar(rs[:, b:b + 1], mv[:, b, 1:2], eps, None, ALU.add)\
                    .then_inc(done, 1)

            def mlp_out(b):
                return PS[:, 4 + b // 2, 256 * (b % 2):256 * (b % 2) + 256]

            def last_stats(b):
                dve.wait_ge(m_d, NT * (b // HALF + 1))
                norm_stats(mlp_out(b), b, CEPS, t_st)

            def last_norm(b):
                dve.wait_ge(t_pw, t_count("stats3", b))
                dve.wait_ge(t_x, NB + b - 3)
                V_.tensor_scalar(YB[:, b % 4, :], mlp_out(b), mv[:, b, 0:1], rs[:, b:b + 1],
                                 ALU.subtract, ALU.mult).then_inc(t_y, 1)

            def tail(s):
                if ("norm", s) in TAIL_DO:
                    b = TAIL_DO["norm", s]
                    dve.wait_ge(t_pw, t_count("stats", b))
                    if b >= 4:
                        dve.wait_ge(t_x, b - 3)
                    V_.tensor_scalar(YB[:, b % 4, :], tail_out("project", b),
                                     mv[:, b, 0:1], rs[:, b:b + 1], ALU.subtract, ALU.mult)\
                        .then_inc(t_y, 1)
                if ("norm2", s) in TAIL_DO:
                    b = TAIL_DO["norm2", s]
                    dve.wait_ge(t_pw, t_count("stats2", b))
                    if b >= 4:
                        dve.wait_ge(t_d, b - 3)
                    V_.tensor_scalar(XN2[:, b % 4, :], X[:, b, :], mv[:, b, 0:1],
                                     rs[:, b:b + 1], ALU.subtract, ALU.mult).then_inc(t_xn, 1)
                if ("norm3", s) in TAIL_DO:
                    last_norm(TAIL_DO["norm3", s])
                if ("split", s) in TAIL_DO:
                    b = TAIL_DO["split", s]
                    dve.wait_ge(t_hi, b + 1)
                    cols = slice(128 * b, 128 * b + 128)
                    V_.scalar_tensor_tensor(
                        out=X2[1][:, :, cols],
                        in0=tail_out("columns", b)
                        .rearrange("p (k t) -> p k t", k=2), scalar=XS,
                        in1=X2[0][:, :, cols], op0=ALU.mult, op1=ALU.subtract).then_inc(t_lo, 1)
                if ("heads", s) in TAIL_DO:
                    b = TAIL_DO["heads", s]
                    dve.wait_ge(t_a, b + 1)
                    t = tail_out("heads", b, 512).rearrange("p (h c) -> p h c", c=32)
                    link(V_.reciprocal(rc[:, b % 2, :], t[:, :, DH]))
                    if b >= 4:
                        dve.wait_ge(t_b, b - 3)
                    V_.tensor_tensor(AN[:, b % 4, :].rearrange("p (h c) -> p h c", c=DH),
                                     t[:, :, 0:DH],
                                     rc[:, b % 2, :].unsqueeze(2).broadcast_to([128, H, DH]),
                                     ALU.mult).then_inc(t_n, 1)
                if ("stats", s) in TAIL_DO:
                    b = TAIL_DO["stats", s]
                    dve.wait_ge(t_c, b + 1)
                    norm_stats(tail_out("project", b), b, EPS, t_st)
                if ("stats2", s) in TAIL_DO:
                    b = TAIL_DO["stats2", s]
                    dve.wait_ge(t_x, b + 1)
                    norm_stats(X[:, b, :], b, EPS, t_st)
                if ("stats3", s) in TAIL_DO:
                    last_stats(TAIL_DO["stats3", s])

            for j in range(4):
                qwork(0, j)
            latent_lo(1)
            qwork(0, 4)
            qwork(0, 5)
            qhi(0, 0)
            qwork(0, 6)
            qwork(0, 7)
            w, a, b = (STG[:, 1, k, :] for k in range(3))
            dve.wait_ge(s_afr, 8)
            V_.tensor_tensor(a[0:64, :], a[0:64, :], w[0:64, :], ALU.add)
            link(V_.tensor_tensor(b[64:128, :], b[64:128, :], w[64:128, :], ALU.add))
            for e in range(2):
                V_.tensor_copy(QH[:, 0, 2 + e, 0:512], (a, b)[e]).then_inc(s_qhi, 1)
            dve.wait_ge(s_qhi, 4)
            for e in range(2):
                V_.tensor_tensor(QL[:, 0, 2 + e, 0:512], (a, b)[e], QH[:, 0, 2 + e, 0:512],
                                 ALU.subtract).then_inc(s_qd, 1)
            for m in SOON[-2] + SOON[-1]:
                maxima(m)
            for g in range(G):
                for i in range(U):
                    n = g * U + i
                    if g == G - 1 and i >= HG and i % HG == OUT_STEP:
                        take_out(n // HG - 1)
                    before = divmod(n - 1, U)
                    if before in JOB_AT:
                        qwork(*JOB_AT[before])
                    if (g, i) in HI_AT:
                        qhi(*HI_AT[g, i])
                    if before in WJOB_AT:
                        wlo(WJOB_AT[before])
                    if (g, i) == SCALE_STEPS[0]:
                        scale_maxima()
                    if (g, i) == SCALE_STEPS[1]:
                        scale_factors()
                    for m in SOON[i]:
                        if g * U + m < G * U:
                            maxima(g * U + m)
                    if g == G - 1:
                        tail(i)
                    for part in range(2):
                        if (g, i - part) in SPREAD_STEPS:
                            spread(SPREAD_STEPS.index((g, i - part)), part)
                    if n == ROPE_STEP:
                        rope_key(1)
                        dve.wait_ge(s_plo, 6)
                        V_.memset(bank(6), 0.0).then_inc(s_ov, 1)
                    if n >= HG and (g < G - 1 or i < HG) and i % HG == OUT_STEP:
                        take_out(n // HG - 1)
            take_out(G * NB - 1)

            for s in range(U, HALF_DONE):
                tail(s)
            for k in range(2 * NT):
                n = k % NT
                dve.wait_ge(m_sq, k + 1)
                V_.scalar_tensor_tensor(out=inn[:, k % 2, :], in0=sq[:, k % 2, :], scalar=1.0,
                                        in1=bank(k % 2), op0=ALU.add, op1=ALU.mult)\
                    .then_inc(m_in, 1)
                dve.wait_ge(m_th, k + 1)
                V_.scalar_tensor_tensor(out=hg[:, k % 2, :], in0=inn[:, k % 2, :], scalar=1.0,
                                        in1=bank(k % 2), op0=ALU.add, op1=ALU.mult)\
                    .then_inc(m_h, 1)
                dve.wait_ge(m_h, k + 1)
                dve.wait_ge(m_u, k + 1)
                if k >= 2:
                    dve.wait_ge(m_lo, k - 1)
                V_.scalar_tensor_tensor(out=itr[:, k % 2, :], in0=hg[:, k % 2, :],
                                        scalar=KI[:, n:n + 1], in1=bank(2 + k % 2), op0=ALU.mult,
                                        op1=ALU.mult).then_inc(m_it, 1)
                tail(HALF_DONE + k)
            for st, b in LAST:
                (last_stats if st == "stats3" else last_norm)(b)


_INS = ["L0_attn_x", "L0_attn_W_dkv", "L0_attn_W_dq", "L0_attn_W_kr", "L0_attn_W_qc", "L0_attn_W_qr",
        "L0_attn_W_uk", "L0_attn_W_uv", "L0_attn_W_o", "L0_ffn_gate_W_packed", "L0_ffn_gate_scales",
        "L0_ffn_up_W_packed", "L0_ffn_up_scales", "L0_ffn_down_W_packed", "L0_ffn_down_scales"]


def _rope_constants():
    half = DR // 2
    freqs = np.exp(np.arange(half, dtype=np.float32) * np.float32(-math.log(10000.0) / half))
    ang = (np.arange(T, dtype=np.float32)[None, :] * freqs[:, None].astype(np.float32))
    cos = (np.cos(ang.astype(np.float64)) / WS).astype(np.float32)
    sin = (np.sin(ang.astype(np.float64)) / WS).astype(np.float32)
    return np.concatenate([cos] * 4), np.concatenate([-sin, sin] * 2)


def kernel(**inputs):
    import numpy as _np
    import concourse.bacc as _bacc
    from concourse import mybir as _mybir
    from concourse.bass_utils import run_bass_kernel_spmd as _run

    nc = _bacc.Bacc("TRN2", target_bir_lowering=False, num_devices=1)
    arrays, args = {}, []
    cos, sin = _rope_constants()
    for name, a in [(n, inputs[n]) for n in _INS] + [("rope_cos", cos), ("rope_sin", sin)]:
        a = _np.ascontiguousarray(a)
        arrays[f"in_{name}_dram"] = a
        args.append(nc.dram_tensor(f"in_{name}_dram", a.shape, _mybir.dt.from_np(a.dtype),
                                   kind="ExternalInput").ap())
    out = nc.dram_tensor("out_0_dram", (1, T, E), F32, kind="ExternalOutput").ap()
    layer_kernel(nc, *args, out)
    r = _run(nc, [arrays], core_ids=[0])
    return r.results[0]["out_0_dram"]
```
